# Optimizing a Trainium2 kernel written in Bass

```python
import numpy as np
import jax
import jax.numpy as jnp

def _softmax(x, axis=-1):
    return jax.nn.softmax(x, axis=axis)

def _gelu(x):
    return jax.nn.gelu(x, approximate=True)

def _silu(x):
    return jax.nn.silu(x)

def _sigmoid(x):
    return jax.nn.sigmoid(x)

def _layernorm(x, axis=-1, eps=1e-05):
    m = jnp.mean(x, axis=axis, keepdims=True)
    v = jnp.var(x, axis=axis, keepdims=True)
    return (x - m) / jnp.sqrt(v + eps)

def _scatter_add(tgt, idx, src, axis=0):
    return tgt.at[idx].add(src)

def _segment_sum(src, seg, n):
    return jax.ops.segment_sum(src, seg, n)
kernel_name = 'mk_adaln_attn_ffn_d1_seqx_r8_9083c5'

def setup_inputs(seed: int=0):
    np.random.seed(seed)
    _w = jnp.asarray

    def _rec_inputs():
        import jax
        import jax.numpy as jnp
        _rk = jax.random.key(seed)
        x = -0.0002919 + 1 * jax.random.normal(jax.random.fold_in(_rk, 1), (64, 32, 128), jnp.float32)
        _lenS = 32 - jax.random.randint(jax.random.fold_in(_rk, 7), (64,), 0, max(1, 32 // 4) + 1, jnp.int32)
        _lenS2 = 32 - jax.random.randint(jax.random.fold_in(_rk, 8), (64,), 0, max(1, 32 // 4) + 1, jnp.int32)
        cond_1024 = 0.0061147 + 1.02565 * jax.random.normal(jax.random.fold_in(_rk, 11), (64, 128), jnp.float32)
        _validS = jnp.arange(32)[None, :] < _lenS[:, None]
        _validS2 = jnp.arange(32)[None, :] < _lenS2[:, None]
        _causal = jnp.tril(jnp.ones((32, 32), dtype=bool))
        mask_Bx1x1xS_ff0 = jnp.where(jnp.ones((64, 1, 1, 32), dtype=bool), 0.0, -1000000000.0).astype(jnp.float32)
        return (x, cond_1024, mask_Bx1x1xS_ff0)
    x, cond_1024, mask_Bx1x1xS_ff0 = _rec_inputs()

    def _L0_cond_setup():
        import jax, jax.numpy as jnp
        import numpy as np
        EMBED = 128
        HEADS = 16
        HDIM = EMBED // HEADS
        MASK_OUT = -10000.0

        def _split_heads(t):
            B, T, _ = t.shape
            return t.reshape(B, T, HEADS, HDIM).transpose(0, 2, 1, 3)
        key = jax.random.key(seed)
        ks = jax.random.split(key, 12)
        B, S = (4, 1023)
        scale = 0.02
        return {'word_hidden_states': jax.random.normal(ks[0], (B, S, EMBED), jnp.float32), 'image_hidden_states': jax.random.normal(ks[1], (B, EMBED), jnp.float32), 'attention_mask': jnp.zeros((B, 1, 1, S), jnp.float32), 'c_attn_w': jax.random.normal(ks[2], (EMBED, 3 * EMBED), jnp.float32) * scale, 'c_attn_b': jnp.zeros((3 * EMBED,), jnp.float32), 'c_proj_w': jax.random.normal(ks[3], (EMBED, EMBED), jnp.float32) * scale, 'c_proj_b': jnp.zeros((EMBED,), jnp.float32), 'uk_w': jax.random.normal(ks[4], (EMBED, EMBED), jnp.float32) * scale, 'uk_b': jnp.zeros((EMBED,), jnp.float32), 'uv_w': jax.random.normal(ks[5], (EMBED, EMBED), jnp.float32) * scale, 'uv_b': jnp.zeros((EMBED,), jnp.float32)}
    _L0_cond_all = _L0_cond_setup()
    _L0_cond_in = {k: v for k, v in _L0_cond_all.items() if k in ('c_attn_w', 'c_attn_b', 'c_proj_w', 'c_proj_b', 'uk_w', 'uk_b', 'uv_w', 'uv_b')}
    del _L0_cond_all

    def _L0_attn_setup():
        import jax, jax.numpy as jnp
        import numpy as np
        CHUNK = 32
        B, L, D, H = (4, 256, 128, 4)
        DK, DV = (D // H, D // H)
        GH = D * 2

        def l2norm(x):
            return x / jnp.linalg.norm(x, axis=-1, keepdims=True)

        def short_conv(x, w):
            kk = w.shape[-1]
            xt = jnp.transpose(x, (0, 2, 1))
            xt = jnp.pad(xt, ((0, 0), (0, 0), (kk - 1, 0)))
            y = jax.lax.conv_general_dilated(xt, w[:, None, :], (1,), 'VALID', dimension_numbers=('NCH', 'OIH', 'NCH'), feature_group_count=w.shape[0])
            return jax.nn.silu(jnp.transpose(y, (0, 2, 1)))

        def fir_conv(x, filt):
            b, l, h, d = x.shape
            kk = filt.shape[-1]
            xt = jnp.transpose(x, (0, 2, 3, 1)).reshape(b, h * d, l)
            xt = jnp.pad(xt, ((0, 0), (0, 0), (kk - 1, 0)))
            y = jax.lax.conv_general_dilated(xt, filt.reshape(h * d, 1, kk), (1,), 'VALID', dimension_numbers=('NCH', 'OIH', 'NCH'), feature_group_count=h * d)
            return jnp.transpose(y.reshape(b, h, d, l), (0, 3, 1, 2))

        def delta_rule_chunkwise(q, k, v, beta, chunk_size=CHUNK):
            b, h, Ltot, dk = q.shape
            dv = v.shape[-1]
            pad = -Ltot % chunk_size
            if pad:
                p4 = ((0, 0), (0, 0), (0, pad), (0, 0))
                q, k, v = (jnp.pad(q, p4), jnp.pad(k, p4), jnp.pad(v, p4))
                beta = jnp.pad(beta, ((0, 0), (0, 0), (0, pad)))
            Lp = Ltot + pad
            n = Lp // chunk_size
            q, k = (l2norm(q), l2norm(k))
            v = v * beta[..., None]
            k_beta = k * beta[..., None]
            resh = lambda t: t.reshape(b, h, n, chunk_size, t.shape[-1])
            q, k, v, k_beta = map(resh, (q, k, v, k_beta))
            tri_strict = jnp.tril(jnp.ones((chunk_size, chunk_size), bool), -1)
            attn = -(k_beta @ jnp.swapaxes(k, -1, -2)) * tri_strict

            def body(i, A):
                row = A[..., i, :]
                upd = jnp.einsum('bhnj,bhnjk->bhnk', row, A)
                new_row = jnp.where(jnp.arange(chunk_size) < i, row + upd, row)
                return A.at[..., i, :].set(new_row)
            attn = jax.lax.fori_loop(1, chunk_size, body, attn)
            attn = attn + jnp.eye(chunk_size, dtype=attn.dtype)
            u = attn @ v
            w = attn @ k_beta
            keep = jnp.tril(jnp.ones((chunk_size, chunk_size), bool))

            def step(S, xs):
                q_i, k_i, u_i, w_i = xs
                attn_local = q_i @ jnp.swapaxes(k_i, -1, -2) * keep
                u_new = u_i - w_i @ S
                o_i = q_i @ S + attn_local @ u_new
                S = S + jnp.swapaxes(k_i, -1, -2) @ u_new
                return (S, o_i)
            xs = tuple((jnp.moveaxis(t, 2, 0) for t in (q, k, u, w)))
            S0 = jnp.zeros((b, h, dk, dv), q.dtype)
            S, o = jax.lax.scan(step, S0, xs)
            o = jnp.moveaxis(o, 0, 2).reshape(b, h, Lp, dv)
            return (o[:, :, :Ltot], S)
        key = jax.random.key(seed)
        ks = jax.random.split(key, 16)
        s = 0.02
        return {'hidden_states': jax.random.normal(ks[0], (B, L, D), jnp.float32), 'q_proj_w': jax.random.normal(ks[1], (H * DK, D), jnp.float32) * s, 'k_proj_w': jax.random.normal(ks[2], (H * DK, D), jnp.float32) * s, 'v_proj_w': jax.random.normal(ks[3], (H * DV, D), jnp.float32) * s, 'b_proj_w': jax.random.normal(ks[4], (H, D), jnp.float32) * s, 'q_conv_w': jax.random.normal(ks[5], (H * DK, 4), jnp.float32) * s, 'k_conv_w': jax.random.normal(ks[6], (H * DK, 4), jnp.float32) * s, 'v_conv_w': jax.random.normal(ks[7], (H * DV, 4), jnp.float32) * s, 'fir_short_w': jax.random.normal(ks[8], (H, DV, 7), jnp.float32) * s, 'fir_long_w': jax.random.normal(ks[9], (H, DV, 31), jnp.float32) * s, 'alpha': jnp.full((H, 1), 0.2, jnp.float32), 'gmix_w1': jax.random.normal(ks[10], (GH, D), jnp.float32) * s, 'gmix_b1': jnp.zeros((GH,), jnp.float32), 'gmix_w2': jax.random.normal(ks[11], (H * 4, GH), jnp.float32) * s, 'gmix_b2': jnp.zeros((H * 4,), jnp.float32).at[H * 2:H * 3].set(0.03), 'o_norm_w': jnp.ones((DV,), jnp.float32), 'o_proj_w': jax.random.normal(ks[12], (D, H * DV), jnp.float32) * s}
    _L0_attn_all = _L0_attn_setup()
    _L0_attn_in = {k: v for k, v in _L0_attn_all.items() if k in ('q_proj_w', 'k_proj_w', 'v_proj_w', 'b_proj_w', 'q_conv_w', 'k_conv_w', 'v_conv_w', 'fir_short_w', 'fir_long_w', 'alpha', 'gmix_w1', 'gmix_b1', 'gmix_w2', 'gmix_b2', 'o_norm_w', 'o_proj_w')}
    del _L0_attn_all

    def _L0_cond2_setup():
        import jax, jax.numpy as jnp
        import numpy as np
        NHID = 128
        NHEAD = 16
        HEAD_DIM = 64
        B, L = (8, 512)
        key = jax.random.key(seed)
        ks = jax.random.split(key, 12)
        s_in = 1.0 / np.sqrt(NHID)
        s_o = 1.0 / np.sqrt(NHEAD * HEAD_DIM)
        return {'x': jax.random.normal(ks[0], (B, L, NHID), dtype=jnp.float32), 'ax': jax.random.normal(ks[1], (B, NHID), dtype=jnp.float32), 'WQ_w': jax.random.normal(ks[2], (NHID, NHEAD * HEAD_DIM), dtype=jnp.float32) * s_in, 'WQ_b': jnp.zeros((NHEAD * HEAD_DIM,), dtype=jnp.float32), 'WK_w': jax.random.normal(ks[3], (NHID, NHEAD * HEAD_DIM), dtype=jnp.float32) * s_in, 'WK_b': jnp.zeros((NHEAD * HEAD_DIM,), dtype=jnp.float32), 'WV_w': jax.random.normal(ks[4], (NHID, NHEAD * HEAD_DIM), dtype=jnp.float32) * s_in, 'WV_b': jnp.zeros((NHEAD * HEAD_DIM,), dtype=jnp.float32), 'WO_w': jax.random.normal(ks[5], (NHEAD * HEAD_DIM, NHID), dtype=jnp.float32) * s_o, 'WO_b': jnp.zeros((NHID,), dtype=jnp.float32)}
    _L0_cond2_all = _L0_cond2_setup()
    _L0_cond2_in = {k: v for k, v in _L0_cond2_all.items() if k in ('WQ_w', 'WQ_b', 'WK_w', 'WK_b', 'WV_w', 'WV_b', 'WO_w', 'WO_b')}
    del _L0_cond2_all

    def _L0_ffn_setup():
        import jax, jax.numpy as jnp
        import numpy as np
        B, T, C = (8, 256, 128)
        E, K = (8, 2)
        H = 4 * C
        CAP_FACTOR = 1.2
        EPS = 1e-09
        key = jax.random.key(seed)
        ks = jax.random.split(key, 6)
        x = jax.random.normal(ks[0], (B, T, C), dtype=jnp.float32)
        router_w = jax.random.normal(ks[1], (E, C), dtype=jnp.float32) * 0.02
        router_b = jnp.zeros((E,), dtype=jnp.float32)
        fc1_w = jax.random.normal(ks[2], (E, H, C), dtype=jnp.float32) * (1.0 / np.sqrt(C))
        fc1_b = jnp.zeros((E, H), dtype=jnp.float32)
        fc2_w = jax.random.normal(ks[3], (E, C, H), dtype=jnp.float32) * (1.0 / np.sqrt(H))
        fc2_b = jnp.zeros((E, C), dtype=jnp.float32)
        layer_scale = jnp.full((E, C), 0.1, dtype=jnp.float32)
        return {'x': x, 'router_w': router_w, 'router_b': router_b, 'fc1_w': fc1_w, 'fc1_b': fc1_b, 'fc2_w': fc2_w, 'fc2_b': fc2_b, 'layer_scale': layer_scale}
    _L0_ffn_all = _L0_ffn_setup()
    _L0_ffn_in = {k: v for k, v in _L0_ffn_all.items() if k in ('router_w', 'router_b', 'fc1_w', 'fc1_b', 'fc2_w', 'fc2_b', 'layer_scale')}
    del _L0_ffn_all
    return {'x': x, 'cond_1024': cond_1024, 'mask_Bx1x1xS_ff0': mask_Bx1x1xS_ff0, 'L0_cond_c_attn_w': _L0_cond_in['c_attn_w'], 'L0_cond_c_attn_b': _L0_cond_in['c_attn_b'], 'L0_cond_c_proj_w': _L0_cond_in['c_proj_w'], 'L0_cond_c_proj_b': _L0_cond_in['c_proj_b'], 'L0_cond_uk_w': _L0_cond_in['uk_w'], 'L0_cond_uk_b': _L0_cond_in['uk_b'], 'L0_cond_uv_w': _L0_cond_in['uv_w'], 'L0_cond_uv_b': _L0_cond_in['uv_b'], 'L0_attn_q_proj_w': _L0_attn_in['q_proj_w'], 'L0_attn_k_proj_w': _L0_attn_in['k_proj_w'], 'L0_attn_v_proj_w': _L0_attn_in['v_proj_w'], 'L0_attn_b_proj_w': _L0_attn_in['b_proj_w'], 'L0_attn_q_conv_w': _L0_attn_in['q_conv_w'], 'L0_attn_k_conv_w': _L0_attn_in['k_conv_w'], 'L0_attn_v_conv_w': _L0_attn_in['v_conv_w'], 'L0_attn_fir_short_w': _L0_attn_in['fir_short_w'], 'L0_attn_fir_long_w': _L0_attn_in['fir_long_w'], 'L0_attn_alpha': _L0_attn_in['alpha'], 'L0_attn_gmix_w1': _L0_attn_in['gmix_w1'], 'L0_attn_gmix_b1': _L0_attn_in['gmix_b1'], 'L0_attn_gmix_w2': _L0_attn_in['gmix_w2'], 'L0_attn_gmix_b2': _L0_attn_in['gmix_b2'], 'L0_attn_o_norm_w': _L0_attn_in['o_norm_w'], 'L0_attn_o_proj_w': _L0_attn_in['o_proj_w'], 'L0_cond2_WQ_w': _L0_cond2_in['WQ_w'], 'L0_cond2_WQ_b': _L0_cond2_in['WQ_b'], 'L0_cond2_WK_w': _L0_cond2_in['WK_w'], 'L0_cond2_WK_b': _L0_cond2_in['WK_b'], 'L0_cond2_WV_w': _L0_cond2_in['WV_w'], 'L0_cond2_WV_b': _L0_cond2_in['WV_b'], 'L0_cond2_WO_w': _L0_cond2_in['WO_w'], 'L0_cond2_WO_b': _L0_cond2_in['WO_b'], 'L0_ffn_router_w': _L0_ffn_in['router_w'], 'L0_ffn_router_b': _L0_ffn_in['router_b'], 'L0_ffn_fc1_w': _L0_ffn_in['fc1_w'], 'L0_ffn_fc1_b': _L0_ffn_in['fc1_b'], 'L0_ffn_fc2_w': _L0_ffn_in['fc2_w'], 'L0_ffn_fc2_b': _L0_ffn_in['fc2_b'], 'L0_ffn_layer_scale': _L0_ffn_in['layer_scale']}

def reference(x, cond_1024, mask_Bx1x1xS_ff0, L0_cond_c_attn_w, L0_cond_c_attn_b, L0_cond_c_proj_w, L0_cond_c_proj_b, L0_cond_uk_w, L0_cond_uk_b, L0_cond_uv_w, L0_cond_uv_b, L0_attn_q_proj_w, L0_attn_k_proj_w, L0_attn_v_proj_w, L0_attn_b_proj_w, L0_attn_q_conv_w, L0_attn_k_conv_w, L0_attn_v_conv_w, L0_attn_fir_short_w, L0_attn_fir_long_w, L0_attn_alpha, L0_attn_gmix_w1, L0_attn_gmix_b1, L0_attn_gmix_w2, L0_attn_gmix_b2, L0_attn_o_norm_w, L0_attn_o_proj_w, L0_cond2_WQ_w, L0_cond2_WQ_b, L0_cond2_WK_w, L0_cond2_WK_b, L0_cond2_WV_w, L0_cond2_WV_b, L0_cond2_WO_w, L0_cond2_WO_b, L0_ffn_router_w, L0_ffn_router_b, L0_ffn_fc1_w, L0_ffn_fc1_b, L0_ffn_fc2_w, L0_ffn_fc2_b, L0_ffn_layer_scale):
    import jax
    import jax.numpy as jnp

    def _L0_cond_ref(word_hidden_states, image_hidden_states, attention_mask, c_attn_w, c_attn_b, c_proj_w, c_proj_b, uk_w, uk_b, uv_w, uv_b):
        import jax, jax.numpy as jnp
        import numpy as np
        EMBED = 128
        HEADS = 16
        HDIM = EMBED // HEADS
        MASK_OUT = -10000.0

        def _split_heads(t):
            B, T, _ = t.shape
            return t.reshape(B, T, HEADS, HDIM).transpose(0, 2, 1, 3)
        B, S, _ = word_hidden_states.shape
        qkv = word_hidden_states @ c_attn_w + c_attn_b
        q_word, k_word, v_word = jnp.split(qkv, 3, axis=-1)
        img = image_hidden_states[:, None, :]
        k_img = img @ uk_w.T + uk_b
        v_img = img @ uv_w.T + uv_b
        k = jnp.concatenate([k_img, k_word], axis=1)
        v = jnp.concatenate([v_img, v_word], axis=1)
        q = _split_heads(q_word)
        k = _split_heads(k)
        v = _split_heads(v)
        scores = jnp.einsum('bhqd,bhkd->bhqk', q, k) / jnp.sqrt(jnp.float32(HDIM))
        qi = jnp.arange(S)[:, None]
        kj = jnp.arange(S + 1)[None, :]
        causal = kj <= qi + 1
        scores = jnp.where(causal[None, None], scores, jnp.float32(MASK_OUT))
        zero_col = jnp.zeros(attention_mask.shape[:-1] + (1,), attention_mask.dtype)
        mask = jnp.concatenate([zero_col, attention_mask], axis=-1)
        scores = scores + mask
        attn = jax.nn.softmax(scores, axis=-1)
        out = jnp.einsum('bhqk,bhkd->bhqd', attn, v)
        out = out.transpose(0, 2, 1, 3).reshape(B, S, EMBED)
        out = out @ c_proj_w + c_proj_b
        return out

    def _L0_attn_ref(hidden_states, q_proj_w, k_proj_w, v_proj_w, b_proj_w, q_conv_w, k_conv_w, v_conv_w, fir_short_w, fir_long_w, alpha, gmix_w1, gmix_b1, gmix_w2, gmix_b2, o_norm_w, o_proj_w):
        import jax, jax.numpy as jnp
        import numpy as np
        CHUNK = 32
        B, L, D, H = (4, 256, 128, 4)
        DK, DV = (D // H, D // H)
        GH = D * 2

        def l2norm(x):
            return x / jnp.linalg.norm(x, axis=-1, keepdims=True)

        def short_conv(x, w):
            kk = w.shape[-1]
            xt = jnp.transpose(x, (0, 2, 1))
            xt = jnp.pad(xt, ((0, 0), (0, 0), (kk - 1, 0)))
            y = jax.lax.conv_general_dilated(xt, w[:, None, :], (1,), 'VALID', dimension_numbers=('NCH', 'OIH', 'NCH'), feature_group_count=w.shape[0])
            return jax.nn.silu(jnp.transpose(y, (0, 2, 1)))

        def fir_conv(x, filt):
            b, l, h, d = x.shape
            kk = filt.shape[-1]
            xt = jnp.transpose(x, (0, 2, 3, 1)).reshape(b, h * d, l)
            xt = jnp.pad(xt, ((0, 0), (0, 0), (kk - 1, 0)))
            y = jax.lax.conv_general_dilated(xt, filt.reshape(h * d, 1, kk), (1,), 'VALID', dimension_numbers=('NCH', 'OIH', 'NCH'), feature_group_count=h * d)
            return jnp.transpose(y.reshape(b, h, d, l), (0, 3, 1, 2))

        def delta_rule_chunkwise(q, k, v, beta, chunk_size=CHUNK):
            b, h, Ltot, dk = q.shape
            dv = v.shape[-1]
            pad = -Ltot % chunk_size
            if pad:
                p4 = ((0, 0), (0, 0), (0, pad), (0, 0))
                q, k, v = (jnp.pad(q, p4), jnp.pad(k, p4), jnp.pad(v, p4))
                beta = jnp.pad(beta, ((0, 0), (0, 0), (0, pad)))
            Lp = Ltot + pad
            n = Lp // chunk_size
            q, k = (l2norm(q), l2norm(k))
            v = v * beta[..., None]
            k_beta = k * beta[..., None]
            resh = lambda t: t.reshape(b, h, n, chunk_size, t.shape[-1])
            q, k, v, k_beta = map(resh, (q, k, v, k_beta))
            tri_strict = jnp.tril(jnp.ones((chunk_size, chunk_size), bool), -1)
            attn = -(k_beta @ jnp.swapaxes(k, -1, -2)) * tri_strict

            def body(i, A):
                row = A[..., i, :]
                upd = jnp.einsum('bhnj,bhnjk->bhnk', row, A)
                new_row = jnp.where(jnp.arange(chunk_size) < i, row + upd, row)
                return A.at[..., i, :].set(new_row)
            attn = jax.lax.fori_loop(1, chunk_size, body, attn)
            attn = attn + jnp.eye(chunk_size, dtype=attn.dtype)
            u = attn @ v
            w = attn @ k_beta
            keep = jnp.tril(jnp.ones((chunk_size, chunk_size), bool))

            def step(S, xs):
                q_i, k_i, u_i, w_i = xs
                attn_local = q_i @ jnp.swapaxes(k_i, -1, -2) * keep
                u_new = u_i - w_i @ S
                o_i = q_i @ S + attn_local @ u_new
                S = S + jnp.swapaxes(k_i, -1, -2) @ u_new
                return (S, o_i)
            xs = tuple((jnp.moveaxis(t, 2, 0) for t in (q, k, u, w)))
            S0 = jnp.zeros((b, h, dk, dv), q.dtype)
            S, o = jax.lax.scan(step, S0, xs)
            o = jnp.moveaxis(o, 0, 2).reshape(b, h, Lp, dv)
            return (o[:, :, :Ltot], S)
        b, l, d = hidden_states.shape
        h = b_proj_w.shape[0]
        dk = q_proj_w.shape[0] // h
        dv = v_proj_w.shape[0] // h
        q = short_conv(hidden_states @ q_proj_w.T, q_conv_w).reshape(b, l, h, dk)
        k = short_conv(hidden_states @ k_proj_w.T, k_conv_w).reshape(b, l, h, dk)
        v = short_conv(hidden_states @ v_proj_w.T, v_conv_w).reshape(b, l, h, dv)
        beta = jax.nn.sigmoid(hidden_states @ b_proj_w.T)
        delta_out, _S = delta_rule_chunkwise(jnp.transpose(q, (0, 2, 1, 3)), jnp.transpose(k, (0, 2, 1, 3)), jnp.transpose(v, (0, 2, 1, 3)), jnp.transpose(beta, (0, 2, 1)))
        delta_out = jnp.transpose(delta_out, (0, 2, 1, 3))
        fir_s = fir_conv(v, fir_short_w)
        fir_l = fir_conv(v, fir_long_w)
        branches = jnp.stack([fir_s, fir_l, delta_out, v], axis=-2)
        mu = branches.mean(-1)
        std = jnp.std(branches, axis=-1, ddof=1)
        mx = branches.max(-1)
        stat_scalar = jnp.stack([mu, std, mx], -1).mean(-1)
        gate = jax.nn.gelu(hidden_states @ gmix_w1.T + gmix_b1, approximate=False) @ gmix_w2.T + gmix_b2
        gate = jnp.transpose(gate.reshape(b, l, 4, h), (0, 1, 3, 2))
        logits = gate + alpha[None, None, :, :] * stat_scalar
        wts = jax.nn.softmax(logits, axis=-1)
        o = jnp.einsum('blhc,blhcd->blhd', wts, branches)
        o = o * jax.lax.rsqrt(jnp.mean(o * o, axis=-1, keepdims=True) + 1e-05) * o_norm_w
        return o.reshape(b, l, h * dv) @ o_proj_w.T

    def _L0_cond2_ref(x, ax, WQ_w, WQ_b, WK_w, WK_b, WV_w, WV_b, WO_w, WO_b):
        import jax, jax.numpy as jnp
        import numpy as np
        NHID = 128
        NHEAD = 16
        HEAD_DIM = 64
        B, L = (8, 512)
        Bx, Lx, H = x.shape
        nh, d = (NHEAD, HEAD_DIM)
        q = (x @ WQ_w + WQ_b).reshape(Bx, Lx, nh, d)
        k = (x @ WK_w + WK_b).reshape(Bx, Lx, nh, d)
        ak = (ax @ WK_w + WK_b).reshape(Bx, 1, nh, d)
        av = (ax @ WV_w + WV_b).reshape(Bx, 1, nh, d)
        pad_k = jnp.pad(k, ((0, 0), (1, 1), (0, 0), (0, 0)))
        k_shift = jnp.stack([pad_k[:, t:Lx + t] for t in range(3)], axis=3)
        akb = jnp.broadcast_to(ak, (Bx, Lx, nh, d))[:, :, :, None, :]
        avb = jnp.broadcast_to(av, (Bx, Lx, nh, d))[:, :, :, None, :]
        K = jnp.concatenate([akb, k_shift], axis=3)
        V = jnp.concatenate([avb, k_shift], axis=3)
        scores = jnp.einsum('blhd,blhjd->blhj', q, K) / jnp.sqrt(jnp.float32(d))
        alphas = jax.nn.softmax(scores, axis=-1)
        att = jnp.einsum('blhj,blhjd->blhd', alphas, V).reshape(Bx, Lx, nh * d)
        return att @ WO_w + WO_b

    def _L0_ffn_ref(x, router_w, router_b, fc1_w, fc1_b, fc2_w, fc2_b, layer_scale):
        import jax, jax.numpy as jnp
        import numpy as np
        B, T, C = (8, 256, 128)
        E, K = (8, 2)
        H = 4 * C
        CAP_FACTOR = 1.2
        EPS = 1e-09
        Bb, Tt, Cc = x.shape
        N = Bb * Tt
        KN = K * N
        capacity = int(CAP_FACTOR * (N // E + 1))
        xf = x.reshape(N, Cc)
        logits = xf @ router_w.T + router_b
        probs = jax.nn.softmax(logits, axis=-1)
        top_vals, top_inds = jax.lax.top_k(probs, K)
        top_vals = top_vals / (jnp.sum(top_vals, axis=-1, keepdims=True) + EPS)
        e_flat = top_inds.T.reshape(-1)
        w_flat = top_vals.T.reshape(-1)
        valid = w_flat > EPS
        onehot = (e_flat[:, None] == jnp.arange(E)[None, :]) & valid[:, None]
        pos = jnp.cumsum(onehot.astype(jnp.int32), axis=0) - 1
        pos_own = jnp.take_along_axis(pos, e_flat[:, None], axis=1)[:, 0]
        keep = valid & (pos_own < capacity)
        scores = jnp.where(keep[None, :] & (e_flat[None, :] == jnp.arange(E)[:, None]), jnp.arange(KN)[None, :], KN)
        sel = jnp.sort(scores, axis=1)[:, :capacity]
        slot_valid = sel < KN
        sel_c = jnp.where(slot_valid, sel, 0)
        tok = sel_c % N
        wgt = jnp.where(slot_valid, w_flat[sel_c], 0.0)
        toks = xf[tok]
        h = jax.nn.gelu(jnp.einsum('etc,ehc->eth', toks, fc1_w) + fc1_b[:, None, :], approximate=False)
        y = jnp.einsum('eth,ech->etc', h, fc2_w) + fc2_b[:, None, :]
        y = toks + y * layer_scale[:, None, :]
        out = jnp.zeros((N, Cc), dtype=x.dtype)
        out = out.at[tok.reshape(-1)].add((wgt[..., None] * y).reshape(-1, Cc))
        return out.reshape(Bb, Tt, Cc)
    x = x + _L0_attn_ref(_L0_cond_ref(x, cond_1024, mask_Bx1x1xS_ff0, L0_cond_c_attn_w, L0_cond_c_attn_b, L0_cond_c_proj_w, L0_cond_c_proj_b, L0_cond_uk_w, L0_cond_uk_b, L0_cond_uv_w, L0_cond_uv_b), L0_attn_q_proj_w, L0_attn_k_proj_w, L0_attn_v_proj_w, L0_attn_b_proj_w, L0_attn_q_conv_w, L0_attn_k_conv_w, L0_attn_v_conv_w, L0_attn_fir_short_w, L0_attn_fir_long_w, L0_attn_alpha, L0_attn_gmix_w1, L0_attn_gmix_b1, L0_attn_gmix_w2, L0_attn_gmix_b2, L0_attn_o_norm_w, L0_attn_o_proj_w)
    x = x + _L0_ffn_ref(_L0_cond2_ref(x, cond_1024, L0_cond2_WQ_w, L0_cond2_WQ_b, L0_cond2_WK_w, L0_cond2_WK_b, L0_cond2_WV_w, L0_cond2_WV_b, L0_cond2_WO_w, L0_cond2_WO_b), L0_ffn_router_w, L0_ffn_router_b, L0_ffn_fc1_w, L0_ffn_fc1_b, L0_ffn_fc2_w, L0_ffn_fc2_b, L0_ffn_layer_scale)
    return x

_drawn_inputs = setup_inputs


def setup_inputs(seed=0):
    import zlib

    import numpy as np

    out = dict(_drawn_inputs(seed))
    spreads = {'L0_cond_c_attn_b': (0.0, 0.298),
     'L0_cond_c_proj_b': (0.0, 0.1),
     'L0_cond_uk_b': (0.0, 0.8),
     'L0_cond_uv_b': (0.0, 0.8),
     'L0_attn_alpha': (0.20000000298023224, 0.6),
     'L0_attn_gmix_b1': (0.0, 0.8),
     'L0_attn_o_norm_w': (1.0, 0.6),
     'L0_cond2_WQ_b': (0.0, 0.1),
     'L0_cond2_WK_b': (0.0, 0.1),
     'L0_cond2_WV_b': (0.0, 0.1),
     'L0_cond2_WO_b': (0.0, 0.1),
     'L0_ffn_router_b': (0.0, 0.1),
     'L0_ffn_fc1_b': (0.0, 0.8),
     'L0_ffn_fc2_b': (0.0, 0.8),
     'L0_ffn_layer_scale': (0.10000000149011612, 0.6)}
    factors = {'L0_cond_c_attn_w': 3.311,
     'L0_cond_uk_w': 8.0,
     'L0_cond_uv_w': 5.287,
     'L0_attn_q_proj_w': 3.188,
     'L0_attn_b_proj_w': 34.549,
     'L0_attn_fir_short_w': 4.627,
     'L0_attn_fir_long_w': 4.62,
     'L0_attn_gmix_w1': 8.0,
     'L0_attn_gmix_w2': 8.0,
     'L0_attn_gmix_b2': 21.893,
     'L0_ffn_fc1_w': 2.971,
     'L0_ffn_fc2_w': 2.764}
    for name, (base, spread) in spreads.items():
        noise = np.random.default_rng([zlib.crc32(name.encode()), seed]).standard_normal(out[name].shape)
        drawn = base * np.exp(spread * noise) if base else spread * noise
        out[name] = jnp.asarray(drawn.astype(out[name].dtype))
    for name, factor in factors.items():
        out[name] = (out[name] * factor).astype(out[name].dtype)
    return out
```

```python
import numpy as np
import concourse.bass as bass
from concourse import mybir
from contextlib import ExitStack

NB, L, D = 64, 32, 128
N = NB * L
P = 128
T = N // P
J = P // L
CH = 4
NC = N // CH
H1, D1 = 16, 8
G1 = 4
K1 = L + 1
H2, D2 = 4, 32
H3, D3 = 16, 64
C3 = H3 * D3 // P
K3 = L + 2
E, HID = 8, 512
HC = HID // P
CAP = int(1.2 * (N // E + 1))
SLOTS = E * CAP
XROWS = SLOTS + 2 * N
PADW = L + 3
NEG = -1e30
EPS = 1e-9

CONSTS = [("ident", P), ("bones", P), ("ones", P), ("before", P), ("hm4", G1), ("hmv", P), ("hm16", H1),
          ("jm4", J), ("c01", K1), ("nonc", K1), ("maskn", 64), ("maska", 64), ("band", K3), ("jm2", 2),
          ("rank", E), ("ebase", E), ("dummy", 2 * T), ("seg", E * 2 * T)]
WEIGHTS = [("wqkv", 3 * D), ("cproj", D), ("ukT", D), ("uvT", D), ("condT", NB),
           ("bq1", 1), ("bk1", 1), ("ukb", 1), ("uvb", 1), ("cpb", 1), ("bv1r", D),
           ("qpT", D), ("kpT", D), ("vpT", D),
           ("bpT", D), ("gw1T", 2 * D), ("gw2T", 2 * H1), ("opT", D), ("wq3", C3 * P), ("wk3", C3 * P),
           ("wv3", C3 * P), ("wo3", C3 * P), ("rwT", E),
           ("cwq", 4), ("cwk", 4), ("cwv", 4),
           ("firs", 7), ("firl", 31), ("gb1", 2), ("onw", 1), ("bq3", C3), ("bk3", C3), ("bv3", C3), ("bo3", 1),
           ("fb1", E * HC), ("fb2", E), ("lsc", E),
           ("gb2r", H1), ("alphar", 4), ("rbr", E), ("bk3r", C3 * P)]


def offsets(fields):
    at, out = 0, {}
    for name, width in fields:
        out[name] = (at, width)
        at += width
    return out, at


def program(nc, xT, w, cst, mask, fc1, fc2, xscr, yscr, nscr, vscr, uscr, zscr, out):
    fp32, i32 = mybir.dt.float32, mybir.dt.int32
    ALU, ACT, AX = mybir.AluOpType, mybir.ActivationFunctionType, mybir.AxisListType
    wo, WW = offsets(WEIGHTS)
    co, CW = offsets(CONSTS)
    ctx = ExitStack()
    with ctx:
        def sb(name, cols, parts=P, dt=fp32):
            return ctx.enter_context(nc.sbuf_tensor(name, [parts, cols], dt))

        def sem(name):
            return ctx.enter_context(nc.semaphore(name))

        W = sb("W", WW)
        Cn = sb("Cn", CW)
        XT = sb("XT", N)
        hP = sb("hP", NB * PADW)
        Z2 = sb("Z2", T * P, 64)
        kimg = sb("kimg", NB)
        vimg = sb("vimg", NB)
        ak3 = sb("ak3", C3 * NB)
        av3 = sb("av3", C3 * NB)
        SM = sb("SM", 3200)
        AR = sb("AR", 33344)
        PS = ctx.enter_context(nc.psum_tensor("PS", [P, 8, 512], fp32))

        def wt(name, a=0, b=None):
            o, n = wo[name]
            return W[:, o + a:o + (n if b is None else b)]

        def cs(name, a=0, b=None):
            o, n = co[name]
            return Cn[:, o + a:o + (n if b is None else b)]

        def ar(at, n, parts=P):
            return AR[0:parts, at:at + n]

        small_at = [0]

        def small(n):
            a = small_at[0]
            small_at[0] += n
            return SM[:, a:a + n]

        ident = cs("ident")

        Qd = ar(0, 8192).rearrange("p (g n) -> p g n", g=G1)
        K0 = ar(8192, 2112).rearrange("p (g t k) -> p g t k", g=G1, t=T)
        Kx = ar(10304, 1056).rearrange("p (r g h k) -> p r g h k", r=2, g=G1, h=4)
        S1 = ar(11360, 1056).rearrange("p (r h k) -> p r h k", r=2, h=H1)
        S2 = ar(12416, 1056).rearrange("p (r h k) -> p r h k", r=2, h=H1)
        P1 = ar(13472, 1056).rearrange("p (r h k) -> p r h k", r=2, h=H1)
        Pn1 = ar(14528, 1024).rearrange("p (r n) -> p r n", r=2)
        PT1 = ar(15552, 1024).rearrange("p (r g n) -> p r g n", r=2, g=G1)
        Vt1 = ar(16576, 1024).rearrange("p (r j c) -> p r j c", r=2, j=J)
        Vx1 = ar(17600, 1024).rearrange("p (r j c) -> p r j c", r=2, j=J)
        Z1 = AR[0:64, 18624:20672].rearrange("p (t c) -> p t c", t=T)
        vie = ar(20672, 1024).rearrange("p (b h) -> p b h", h=H1)
        Mk = ar(21696, 528).rearrange("p (t k) -> p t k", t=T)
        aT1 = ar(22224, 256).rearrange("p (r n) -> p r n", r=2)
        Pie1 = ar(22480, 128).rearrange("p (r j h) -> p r j h", r=2, j=J)
        PiT1 = ar(22608, 256).rearrange("p (r n) -> p r n", r=2)
        Xr = ar(23040, 1024).rearrange("p (r j o n) -> p r j o n", r=2, j=J, o=4)
        Z2s = AR[0:64, 24576:26624].rearrange("p (h c) -> p h c", h=H3)
        mx1 = small(2 * H1).rearrange("p (r h) -> p r h", r=2)
        sm1 = small(2 * H1).rearrange("p (r h) -> p r h", r=2)
        rs1 = small(2 * H1).rearrange("p (r h) -> p r h", r=2)

        s_w, s_wb, s_c, s_am = sem("weights_in"), sem("more_weights_in"), sem("consts_in"), sem("mask_in")
        s_x = [sem(f"x{c}_in") for c in range(CH)]
        s_img, s_imgsb = sem("img_ps"), sem("img_sb")
        s_qp, s_kp, s_qsw, s_ksw = sem("q_ps"), sem("k_ps"), sem("q_swz"), sem("k_swz")
        s_zero, s_k00 = sem("zeroed"), sem("k_img_slot")
        s_vie, s_z1p, s_z1 = sem("vie"), sem("z1_ps"), sem("z1_sb")
        s_ak, s_ak3, s_z2p, s_z2s, s_z2d, s_z2 = sem("ak_ps"), sem("ak_sb"), sem("z2_ps"), sem("z2_sb"), sem("z2_dram"), sem("z2_in")
        s_mk = sem("mask_sum")
        a_kx, a_s, a_s1, a_mx, a_s3, a_p, a_pn = (sem(f"a_{n}") for n in ("kx", "s", "s1", "mx", "s3", "p", "pn"))
        a_pie, a_t, a_pt, a_v, a_vt, a_vx, a_pv, a_at, a_h, a_hs = (
            sem(f"a_{n}") for n in ("pie", "t", "pt", "v", "vt", "vx", "pv", "at", "h", "hs"))
        a_xr = sem("a_xr")
        ch_v, ch_p = sem("dve_chain"), sem("pool_chain")
        b_pad, b_pp, b_pre = sem("b_pad"), sem("b_pp"), sem("b_pre")
        b_cv, b_silu, b_sq, b_n2, b_sqrt, b_bp, b_beta = (sem(f"b_{n}") for n in ("cv", "silu", "sq", "n2", "sqrt", "bp", "beta"))
        b_nrm, b_vb, b_gn, b_gns, b_ga, b_gas = (sem(f"b_{n}") for n in ("nrm", "vb", "gn", "gns", "ga", "gas"))
        b_nd, b_vd, b_pn, b_u0, b_ui, b_solved, b_uo, b_ud, b_utm = (sem(f"b_{n}") for n in (
            "n_dram", "v_dram", "n_pair", "v_pair", "u_init", "solved", "u_out", "u_dram", "u_tm"))
        b_fs, b_fl, b_tr, b_br, b_g1, b_g1s, b_g2, b_gate, b_o, b_od = (sem(f"b_{n}") for n in (
            "fs", "fl", "tr", "br", "g1", "g1s", "g2", "gate", "o", "o_in_br"))
        b_sum, b_dev, b_dsq, b_std, b_stds, b_ee, b_exp, b_wts, b_mix, b_osq, b_ors, b_on = (sem(f"b_{n}") for n in (
            "sum", "dev", "dsq", "var", "std", "logit", "exp", "wts", "mix", "osq", "ors", "on"))
        b_ot, b_ots, b_op, b_x1 = (sem(f"b_{n}") for n in ("ot", "ots", "op", "x1"))
        (c_q, c_qs, c_k, c_ks, c_t, c_ts, c_s, c_s1, c_mx, c_s3, c_p, c_pn, c_ptc, c_pie, c_ptd, c_pit, c_pits, c_pv, c_at,
         c_y, c_ys, c_r, c_yt, c_ytm, c_zero, c_ki) = (sem(f"c_{n}") for n in (
             "q", "qs", "k", "ks", "t", "ts", "s", "s1", "mx", "s3", "p", "pn", "ptc", "pie", "ptd", "pit", "pits", "pv",
             "at", "y", "ys", "r", "yt", "ytm", "zero", "ki"))
        (d_lg, d_ex, d_exps, d_oh, d_cum, d_slot, d_sc, d_xt, d_xts, d_f1, d_f1s, d_f2, d_ye, d_yt, d_yts,
         d_x1t, d_x1s, d_out, d_fin, d_xz, d_fw, d_zt, d_yz) = (sem(f"d_{n}") for n in (
             "lg", "ex", "exps", "oh", "cum", "slot", "sc", "xt", "xts", "f1", "f1s", "f2", "ye", "yt", "yts", "x1t", "x1s", "out", "fin", "xz", "fw", "zt", "yz"))
        d_xg, d_yd = [sem(f"d_xg{r}") for r in range(2)], [sem(f"d_yd{r}") for r in range(2)]
        d_ga = [sem(f"d_ga{c}") for c in range(CH)]
        block = ctx.enter_context(nc.Block())

        pre = [ar(2240 * i, 2240).rearrange("p (b l) -> p b l", b=NB) for i in range(3)]
        qkv = [ar(6720 + N * i, N) for i in range(3)]
        qkv3 = [x.rearrange("p (b l) -> p b l", b=NB) for x in qkv]
        qtmp = ar(27200, N).rearrange("p (b l) -> p b l", b=NB)
        sqr = [ar(0, N), ar(2240, N)]
        beta, kb, vb = ar(12864, N), ar(14912, N), ar(16960, N)
        rn = [ar(19008, N), ar(21056, N)]
        GN = ar(23104, 4096).rearrange("p (h t n) -> p h t n", h=H2, t=T)
        GA = ar(27200, 4096).rearrange("p (h t n) -> p h t n", h=H2, t=T)
        fl = ar(4480, N).rearrange("p (b l) -> p b l", b=NB)
        fs = ar(31296, N).rearrange("p (b l) -> p b l", b=NB)
        PN = ar(12864, 2 * 1024).rearrange("p (s i k) -> p s i k", s=2, i=L)
        V0 = ar(14912, 2 * 1024).rearrange("p (s c i) -> p s c i", s=2, c=D2)
        U = ar(16960, 2 * 1024).rearrange("p (s i c) -> p s i c", s=2, i=L)
        UT = ar(0, N).rearrange("p (t h c) -> p t h c", t=T, h=H2)
        tmpU = ar(2240, 2 * 31 * L).rearrange("p (s i c) -> p s i c", s=2, i=31)
        g1T = ar(19008, 4096).rearrange("p (m n) -> p m n", m=2)
        BR = ar(12864, 8192).rearrange("p (t r h c) -> p t r h c", t=T, r=4, h=H2)
        DV = ar(23104, 8192).rearrange("p (t r h c) -> p t r h c", t=T, r=4, h=H2)
        O = ar(0, N).rearrange("p (t h c) -> p t h c", t=T, h=H2)
        OS = ar(6720, N).rearrange("p (t h c) -> p t h c", t=T, h=H2)
        OT = ar(2048, N)
        gate = small(T * H1).rearrange("p (t r h) -> p t r h", t=T, r=4)
        mu = small(T * 16).rearrange("p (t r h) -> p t r h", t=T, r=4)
        sd = small(T * 16).rearrange("p (t r h) -> p t r h", t=T, r=4)
        bmx = small(T * 16).rearrange("p (t r h) -> p t r h", t=T, r=4)
        lmx = small(T * 4).rearrange("p (t h) -> p t h", t=T)
        oms = small(T * 4).rearrange("p (t h) -> p t h", t=T)

        qs = ar(0, 2048).rearrange("p (r c n) -> p r c n", r=2, c=C3)
        kx3 = ar(2048, 2 * 2176).rearrange("p (r c j h k) -> p r c j h k", r=2, c=C3, j=J, h=2)
        kt3 = ar(6400, 2048).rearrange("p (r n) -> p r n", r=2)
        Sc = ar(8448, 1088).rearrange("p (r h k) -> p r h k", r=2, h=H3)
        Sd = ar(9536, 1088).rearrange("p (r h k) -> p r h k", r=2, h=H3)
        P3 = ar(10624, 1088).rearrange("p (r h k) -> p r h k", r=2, h=H3)
        Pn3 = ar(11712, 1024).rearrange("p (r n) -> p r n", r=2)
        PTc = ar(12736, 1024).rearrange("p (r n) -> p r n", r=2)
        PTd = ar(13760, 2048).rearrange("p (r h i q) -> p r h i q", r=2, h=H3, i=2)
        aT3 = ar(15808, 2048).rearrange("p (r c n) -> p r c n", r=2, c=C3)
        Pie3 = ar(17856, 128).rearrange("p (r j h) -> p r j h", r=2, j=J)
        PiT3 = ar(17984, 256).rearrange("p (r n) -> p r n", r=2)
        FW = ar(18304, 8192).rearrange("p (e s n) -> p e s n", e=E, s=2)
        Y = ar(26496, N).rearrange("p (t c) -> p t c", t=T)
        YT = ar(28544, N)
        Zt = ar(30592, 512)
        mx3 = small(2 * H3).rearrange("p (r h) -> p r h", r=2)
        sm3 = small(2 * H3).rearrange("p (r h) -> p r h", r=2)
        rs3 = small(2 * H3).rearrange("p (r h) -> p r h", r=2)

        LG = small(T * E).rearrange("p (t e) -> p t e", t=T)
        lm = small(T)
        OH = small(2 * T * E).rearrange("p (s t e) -> p s t e", s=2, t=T)
        tq = small(T * E).rearrange("p (t e) -> p t e", t=T)
        tv = small(2 * T).rearrange("p (s t) -> p s t", s=2)
        tk = small(2 * T).rearrange("p (s t) -> p s t", s=2)
        vl = small(2 * T).rearrange("p (s t) -> p s t", s=2)
        tot = small(2 * T * E)
        run_ = small(2 * T * E)
        pos = small(2 * T * E).rearrange("p (s t e) -> p s t e", s=2, t=T)
        pown = small(2 * T)
        keep = small(2 * T)
        slot = small(2 * T)
        sidx = small(2 * T)
        gidx = small(2 * T)
        sI = SM[:, small_at[0]:small_at[0] + 2 * T].bitcast(i32)
        small(2 * T)
        gI = SM[:, small_at[0]:small_at[0] + 2 * T].bitcast(i32)
        small(2 * T)
        XG = ar(0, 2 * 3 * P).rearrange("p (r s c) -> p r s c", r=2, s=3)
        XGT = ar(768, 2 * CAP).rearrange("p (r n) -> p r n", r=2)
        GH = ar(768 + 2 * CAP, 2 * HC * CAP).rearrange("p (r m n) -> p r m n", r=2, m=HC)
        YE = ar(768 + 10 * CAP, 2 * CAP).rearrange("p (r n) -> p r n", r=2)
        YO = ar(768 + 12 * CAP, 768).rearrange("p (r s c) -> p r s c", r=2, s=3)
        X1 = ar(5400, N).rearrange("p (t c) -> p t c", t=T)
        YG = ar(7448, 2 * N).rearrange("p (s t c) -> p s t c", s=2, t=T)
        RO = ar(11600, N).rearrange("p (t c) -> p t c", t=T)
        RPARTS = [(0, P), (P, 2 * P), (2 * P, CAP)]

        def bank(i, cols=512, at=0):
            return PS[:, i, at:at + cols]

        @block.sync
        def _(sp):
            sp.dma_start(W[:, 0:wo["qpT"][0]], w[:, 0:wo["qpT"][0]]).then_inc(s_w, 16)
            for c in range(CH):
                sp.dma_start(XT[:, c * NC:(c + 1) * NC], xT[:, c * NC:(c + 1) * NC]).then_inc(s_x[c], 16)
            sp.dma_start(Cn[:, :], cst).then_inc(s_c, 16)
            sp.dma_start(W[:, wo["qpT"][0]:WW], w[:, wo["qpT"][0]:WW]).then_inc(s_wb, 16)
            sp.wait_ge(s_z2s, 2)
            sp.dma_start(zscr.rearrange("b h c -> b (h c)"), AR[0:64, 24576:26624]).then_inc(s_z2d, 16)
            sp.wait_ge(s_z2d, 16)
            sp.dma_start(Z2[:, :].rearrange("p (t c) -> p t c", t=T),
                         zscr.rearrange("(t j) h c -> (j h) t c", j=J)).then_inc(s_z2, 16)
            sp.wait_ge(b_vb, 1)
            for h in range(H2):
                sp.dma_start(vscr.rearrange("b h c i -> h c b i")[h], vb[32 * h:32 * h + 32, :].rearrange("c (b i) -> c b i", b=NB)).then_inc(b_vd, 16)
            for h in range(H2):
                sp.wait_ge(b_gns, H2 + h + 1)
                for j in range(J):
                    sp.dma_start(nscr.rearrange("(t j) h i k -> j h i t k", j=J)[j, h],
                                 GN[32 * j:32 * j + 32, h, :, 32 * (j % 2):32 * (j % 2) + 32]).then_inc(b_nd, 16)
            sp.wait_ge(b_vd, 16 * H2)
            sp.wait_ge(b_gn, 1)
            sp.dma_start(V0[:, :, :, :].rearrange("p s c i -> p s (c i)"),
                         vscr.rearrange("(s b) h c i -> (b h) s (c i)", s=2)).then_inc(b_u0, 16)
            sp.wait_ge(b_nd, 16 * H2 * J)
            sp.dma_start(PN[:, :, :, :].rearrange("p s i k -> p s (i k)"),
                         nscr.rearrange("(s b) h i k -> (b h) s (i k)", s=2)).then_inc(b_pn, 16)
            sp.wait_ge(b_solved, 1)
            sp.dma_start(uscr.rearrange("(s b) h i c -> (b h) s (i c)", s=2), U[:, :, :, :].rearrange("p s i c -> p s (i c)")).then_inc(b_ud, 16)
            sp.wait_ge(b_ud, 16)
            for j in range(J):
                for h in range(H2):
                    sp.dma_start(UT[32 * j:32 * j + 32, :, h, :], uscr.rearrange("(t j) h i c -> j h i t c", j=J)[j, h]).then_inc(b_utm, 16)
            sp.wait_ge(b_x1, CH)
            sp.dma_start(FW[:, :, 0, :], fc1).then_inc(d_fw, 16)
            sp.dma_start(FW[:, :, 1, :], fc2).then_inc(d_fw, 16)
            sp.wait_ge(d_zt, 1)
            zrow = Zt[:, :].rearrange("p (a c) -> p a c", c=P)
            for a in range(0, 2432, 512):
                n = min(512, 2432 - a) // P
                sp.dma_start(xscr[a:a + n * P, :].rearrange("(a p) c -> p a c", p=P), zrow[:, 0:n, :]).then_inc(d_xz, 16)
            sp.dma_start(xscr[2432:SLOTS, :], Zt[0:SLOTS - 2432, 0:P]).then_inc(d_xz, 16)
            sp.dma_start(yscr[SLOTS:SLOTS + 1, :], Zt[0:1, 0:P]).then_inc(d_yz, 16)
            for e in range(E):
                sp.wait_ge(d_sc, 16 * 2 * T)
                if e >= 2:
                    sp.wait_ge(d_xt, e - 1)
                for s, (a, b) in enumerate(RPARTS):
                    sp.dma_start(XG[0:b - a, e % 2, s, :], xscr[e * CAP + a:e * CAP + b, :]).then_inc(d_xg[e % 2], 16)
            for t in range(T):
                sp.wait_ge(d_fin, t + 1)
                sp.dma_start(out[t * P:(t + 1) * P, :], RO[:, t, :]).then_inc(d_out, 16)
            sp.wait_ge(d_out, 16 * T)

        @block.gpsimd
        def _(pool):
            mv = mask.rearrange("(t j) k -> j t k", j=J)
            pool.memset(Mk[:, :, :], 0.0).then_inc(s_mk, 1)
            pool.wait_ge(s_mk, 1)
            for j in range(J):
                pool.dma_start(Mk[32 * j:32 * j + 32, :, 1:K1], mv[j:j + 1].broadcast_to([32, T, L])).then_inc(s_am, 16)
            pool.memset(ar(0, 8192), 0.0).then_inc(s_zero, 1)
            pool.memset(hP[:, :], 0.0).then_inc(b_pad, 1)
            pool.wait_ge(s_am, 16 * J)
            pool.wait_ge(s_c, 16)
            pool.tensor_tensor(Mk[:, :, :], Mk[:, :, :], cs("nonc").rearrange("p (o k) -> p o k", o=1).broadcast_to([P, T, K1]), ALU.add).then_inc(s_mk, 1)
            pool.wait_ge(s_imgsb, 2)
            pool.tensor_tensor(vie, vimg[:, :].rearrange("p (b o) -> p b o", o=1).broadcast_to([P, NB, H1]),
                               cs("hm16").rearrange("p (o h) -> p o h", o=1).broadcast_to([P, NB, H1]), ALU.mult).then_inc(s_vie, 1)
            pool.wait_ge(s_k00, 16)
            pool.wait_ge(s_ksw, 16)
            hm4 = cs("hm4").rearrange("p (o h u) -> p o h u", o=1, u=1).broadcast_to([P, G1, 4, K1])

            def expand(t):
                if t >= 2:
                    pool.wait_ge(a_s, t - 1)
                pool.tensor_tensor(Kx[:, t % 2], K0[:, :, t, :].rearrange("p g (o k) -> p g o k", o=1).broadcast_to([P, G1, 4, K1]),
                                   hm4, ALU.mult).then_inc(a_kx, 1)

            def repeat(t):
                if t == 0:
                    for c in range(CH):
                        pool.wait_ge(s_x[c], 16)
                if t >= 2:
                    pool.wait_ge(a_v, t - 1)
                pool.tensor_copy(Xr[:, t % 2], XT[:, t * P:(t + 1) * P].rearrange("p (j o n) -> p j o n", j=J, o=1).broadcast_to([P, J, 4, L])).then_inc(a_xr, 1)

            def shift(t):
                pool.wait_ge(a_mx, t + 1)
                pool.tensor_tensor(S2[:, t % 2], S2[:, t % 2], mx1[:, t % 2].rearrange("p (h o) -> p h o", o=1).broadcast_to([P, H1, K1]),
                                   ALU.subtract).then_inc(a_s3, 1)

            def values(t):
                pool.wait_ge(a_vt, t + 1)
                if t >= 2:
                    pool.wait_ge(a_pv, t - 1)
                pool.tensor_tensor(Vx1[:, t % 2], Vt1[:, t % 2], cs("hmv").rearrange("p (o c) -> p o c", o=1).broadcast_to([P, J, P]),
                                   ALU.mult).then_inc(a_vx, 1)

            for t in range(T + 2):
                if t < T:
                    expand(t)
                    repeat(t)
                if 1 <= t <= T:
                    shift(t - 1)
                if t >= 2:
                    values(t - 2)

            pool.wait_ge(s_wb, 16)
            pool.wait_ge(b_pre, 3 * CH)
            y = qkv3[0]
            pool.tensor_scalar(y, pre[0][:, :, 0:L], wt("cwq", 0, 1), None, ALU.mult).then_inc(ch_p, 1)
            for i in range(1, 4):
                pool.tensor_scalar(qtmp, pre[0][:, :, i:i + L], wt("cwq", i, i + 1), None, ALU.mult).then_inc(ch_p, 1)
                pool.wait_ge(ch_p, 2 * i)
                ins = pool.tensor_tensor(y, y, qtmp, ALU.add)
                if i < 3:
                    ins.then_inc(ch_p, 1)
                    pool.wait_ge(ch_p, 2 * i + 1)
            ins.then_inc(b_cv, 1)
            for t in range(T):
                pool.wait_ge(b_sum, t + 1)
                if t == T // 2:
                    pool.wait_ge(b_o, T)
                pool.tensor_tensor(DV[:, t], BR[:, t], mu[:, t].rearrange("p r (h o) -> p r h o", o=1).broadcast_to([P, 4, H2, D2]),
                                   ALU.subtract).then_inc(b_dev, 1)
            pool.wait_ge(b_x1, CH)
            pool.memset(ar(2048, 2 * 2176), 0.0).then_inc(c_zero, 1)
            pool.memset(Zt, 0.0).then_inc(d_zt, 1)

            def shift3(t):
                pool.wait_ge(c_mx, t + 1)
                if t >= 2:
                    pool.wait_ge(c_p, t - 1)
                pool.tensor_tensor(Sd[:, t % 2], Sc[:, t % 2], mx3[:, t % 2].rearrange("p (h o) -> p h o", o=1).broadcast_to([P, H3, K3]),
                                   ALU.subtract).then_inc(c_s3, 1)

            def diag3(t):
                pool.wait_ge(c_ptc, t + 1)
                if t >= 2:
                    pool.wait_ge(c_pv, t - 1)
                pool.tensor_tensor(PTd[:, t % 2], PTc[:, t % 2].rearrange("p (h o q) -> p h o q", h=H3, o=1).broadcast_to([P, H3, 2, L]),
                                   cs("jm2").rearrange("p (o i u) -> p o i u", o=1, u=1).broadcast_to([P, H3, 2, L]), ALU.mult).then_inc(c_ptd, 1)

            for t in range(T + 1):
                if t >= 1:
                    diag3(t - 1)
                if t < T:
                    shift3(t)
            pool.wait_ge(d_slot, 1)
            pool.wait_ge(d_xz, 16 * 6)
            pool.wait_ge(c_ytm, T)
            for s in range(2):
                for t in range(T):
                    pool.indirect_dma_start(out=xscr, out_offset=bass.IndirectOffsetOnAxis(ap=sI[:, s * T + t:s * T + t + 1], axis=0),
                                            in_=Y[:, t, :], in_offset=None).then_inc(d_sc, 16)
            for e in range(E):
                pool.wait_ge(d_yts, e + 1)
                for s, (a, b) in enumerate(RPARTS):
                    pool.dma_start(yscr[e * CAP + a:e * CAP + b, :], YO[0:b - a, e % 2, s, :]).then_inc(d_yd[e % 2], 16)
            for r in range(2):
                pool.wait_ge(d_yd[r], 16 * 3 * E // 2)
            pool.wait_ge(d_yz, 16)
            for t in range(T):
                for s in range(2):
                    pool.indirect_dma_start(out=YG[:, s, t, :], out_offset=None, in_=yscr,
                                            in_offset=bass.IndirectOffsetOnAxis(ap=gI[:, s * T + t:s * T + t + 1], axis=0)).then_inc(d_ga[t // 4], 16)

        @block.tensor
        def _(pe):
            mm = pe.matmul
            pe.wait_ge(s_w, 16)
            mm(bank(0, NB), wt("ukT"), wt("condT"), start=True, stop=True)
            mm(bank(0, NB, NB), wt("uvT"), wt("condT"), start=True, stop=True).then_inc(s_img, 1)
            pe.wait_ge(s_imgsb, 2)
            for c in range(CH):
                pe.wait_ge(s_x[c], 16)
                ins = mm(bank(c), wt("wqkv", 0, D), XT[:, c * NC:(c + 1) * NC], start=True, stop=True)
            ins.then_inc(s_qp, 1)
            for c in range(CH):
                ins = mm(bank(4 + c), wt("wqkv", D, 2 * D), XT[:, c * NC:(c + 1) * NC], start=True, stop=True)
            ins.then_inc(s_kp, 1)
            pe.wait_ge(s_qsw, 16)
            pe.wait_ge(s_wb, 16)
            for i, name in enumerate(("wk3", "wv3")):
                for c in range(C3):
                    ins = mm(bank(i, NB, NB * c), wt(name, c * P, (c + 1) * P), wt("condT"), start=True, stop=True)
            ins.then_inc(s_ak, 1)
            pe.wait_ge(s_vie, 1)
            for t in range(T):
                ins = mm(PS[0:64, 2 + t // 8 if t < 8 else 3, (t % 4) * P:(t % 4 + 1) * P] if False else PS[0:64, 2 + (t // 4) % 2, (t % 4) * P:(t % 4 + 1) * P],
                         vie[:, J * t:J * t + J, :], wt("cproj"), start=True, stop=True)
                if t % 4 == 3:
                    ins.then_inc(s_z1p, 1)
                    if t == 7 or t == 11:
                        pe.wait_ge(s_z1, t // 4)
            pe.wait_ge(s_ak3, 2)
            pe.wait_ge(s_ksw, 16)
            for r in range(2):
                if r:
                    pe.wait_ge(s_z2s, 1)
                for i in range(8):
                    h = 8 * r + i
                    o = 64 * (h % 2)
                    ins = mm(PS[0:64, 4 + (h % 2), (i // 2) * P:(i // 2 + 1) * P], av3[o:o + 64, (h // 2) * NB:(h // 2 + 1) * NB],
                             wt("wo3", (h // 2) * P, (h // 2 + 1) * P)[o:o + 64], start=True, stop=True)
                ins.then_inc(s_z2p, 1)
            pe.wait_ge(s_z2s, 2)
            pe.wait_ge(s_z1, 4)

            def scores(t):
                pe.wait_ge(a_kx, t + 1)
                if t >= 2:
                    pe.wait_ge(a_s1, 2 * (t - 1))
                for g in range(G1):
                    ins = mm(PS[:, 2 * (t % 2) + g // 2, (g % 2) * 132:(g % 2 + 1) * 132], Qd[:, g, t * P:(t + 1) * P],
                             Kx[:, t % 2, g].rearrange("p h k -> p (h k)"), start=True, stop=True)
                ins.then_inc(a_s, 1)

            def v_rows(t):
                pe.wait_ge(a_xr, t + 1)
                if t >= 1:
                    pe.wait_ge(a_vt, t)
                for j in range(J):
                    ins = mm(PS[:, 6, j * P:(j + 1) * P], Xr[:, t % 2, j].rearrange("p o n -> p (o n)"),
                             wt("wqkv", 2 * D, 3 * D), start=True, stop=True)
                ins.then_inc(a_v, 1)

            def turn(t):
                pe.wait_ge(a_pn, t + 1)
                pe.wait_ge(a_pie, t + 1)
                if t >= 1:
                    pe.wait_ge(a_pt, 2 * t)
                    pe.wait_ge(a_hs, t)
                for g in range(G1):
                    pe.transpose(PS[:, 4, g * P:(g + 1) * P], Pn1[:, t % 2, g * P:(g + 1) * P], ident)
                pe.transpose(PS[0:64, 5, 0:P], Pie1[:, t % 2].rearrange("p j h -> p (j h)"), ident).then_inc(a_t, 1)

            def weigh(t):
                pe.wait_ge(a_pt, 2 * t + 2)
                pe.wait_ge(a_vx, t + 1)
                if t >= 1:
                    pe.wait_ge(a_at, t)
                for j in range(J):
                    for g in range(G1):
                        ins = mm(PS[32 * g:32 * g + 32, 7, 32 * j:32 * j + 32], Vx1[:, t % 2, j, 32 * g:32 * g + 32],
                                 PT1[:, t % 2, g, 32 * j:32 * j + 32], start=True, stop=True)
                ins.then_inc(a_pv, 1)

            def project(t):
                pe.wait_ge(a_at, t + 1)
                mm(PS[:, 5, P:2 * P], Z1[:, t, :], PiT1[0:64, t % 2], start=True, stop=False)
                mm(PS[:, 5, P:2 * P], wt("cproj"), aT1[:, t % 2], start=False, stop=True).then_inc(a_h, 1)

            for t in range(T + 2):
                if t < T:
                    scores(t)
                    v_rows(t)
                if t >= 2:
                    weigh(t - 2)
                    project(t - 2)
                if 1 <= t <= T:
                    turn(t - 1)

            n = 0
            hv = hP[:, :].rearrange("p (b l) -> p b l", b=NB)
            pe.wait_ge(a_hs, T)
            for i, name in ((2, "vpT"), (1, "kpT"), (0, "qpT")):
                for c in range(CH):
                    if n >= 4:
                        pe.wait_ge(b_pre, n - 3)
                    mm(bank(n % 4), wt(name), hv[:, 16 * c:16 * c + 16, 3:PADW], start=True, stop=True).then_inc(b_pp, 1)
                    n += 1
            for c in range(CH):
                mm(bank(4 + c), wt("bpT"), hv[:, 16 * c:16 * c + 16, 3:PADW], start=True, stop=True).then_inc(b_bp, 1)
            pe.wait_ge(b_pre, 3 * CH)
            for i in range(2):
                for c in range(CH):
                    pe.wait_ge(b_sq, i + 1)
                    if i:
                        pe.wait_ge(b_sqrt, c + 1)
                    mm(bank(c), cs("bones"), sqr[1 - i][:, c * NC:(c + 1) * NC], start=True, stop=True).then_inc(b_n2, 1)

            def gram(lhs, rhs, b0, done, free, out_sem):
                for r in range(2):
                    if r:
                        pe.wait_ge(free[0], free[1])
                    for h in range(H2):
                        for t8 in range(8):
                            t = 8 * r + t8
                            for f in range(2):
                                c0 = t * P + 64 * f
                                ins = mm(PS[64 * f:64 * f + 64, b0 + h, 64 * t8:64 * t8 + 64], lhs[32 * h:32 * h + 32, c0:c0 + 64],
                                         rhs[32 * h:32 * h + 32, c0:c0 + 64], start=True, stop=True)
                    ins.then_inc(out_sem, 1)

            pe.wait_ge(b_beta, CH)
            pe.wait_ge(b_sqrt, 2 * CH)
            pe.wait_ge(b_nrm, 3)
            gram(kb, qkv[1], 0, None, (b_gns, 4), b_gn)
            gram(qkv[1], qkv[0], 4, None, (b_gas, 4), b_ga)
            pe.wait_ge(b_gns, 8)
            for m in range(2):
                for c in range(CH):
                    n = m * CH + c
                    if n >= 4:
                        pe.wait_ge(b_g1s, n - 3)
                    mm(bank(n % 4), wt("gw1T", m * P, (m + 1) * P), hv[:, 16 * c:16 * c + 16, 3:PADW], start=True, stop=True).then_inc(b_g1, 1)
            pe.wait_ge(b_g1s, 8)
            pe.wait_ge(b_gas, 8)
            for t in range(T):
                for m in range(2):
                    ins = mm(bank(4, H1, H1 * t), g1T[:, m, t * P:(t + 1) * P], wt("gw2T", m * H1, (m + 1) * H1), start=(m == 0), stop=(m == 1))
            ins.then_inc(b_g2, 1)
            pe.wait_ge(b_fs, 1)
            pe.wait_ge(b_fl, 1)
            for t in range(T):
                if t >= 2:
                    pe.wait_ge(b_br, t - 1)
                for r, x in enumerate((fs, fl, qkv3[2])):
                    ins = pe.transpose(bank(t % 2, P, r * P), x[:, J * t:J * t + J, :].rearrange("p b l -> p (b l)"), ident)
                ins.then_inc(b_tr, 1)
            pe.wait_ge(b_utm, 16 * J * H2)
            pe.wait_ge(b_gate, 1)
            for t in range(T):
                q4 = t % 2
                if t >= 2:
                    pe.wait_ge(b_od, 2 * (t - 1))
                for f in range(2):
                    for h in range(H2):
                        ins = mm(PS[64 * f:64 * f + 64, 4 + 2 * q4 + f, 32 * h:32 * h + 32], GA[64 * f:64 * f + 64, h, t, :],
                                 UT[64 * f:64 * f + 64, t, h, :], start=True, stop=True)
                ins.then_inc(b_o, 1)
            for c in range(CH):
                pe.wait_ge(b_on, c + 1)
                for i in range(4):
                    t = 4 * c + i
                    ins = pe.transpose(bank(c, P, i * P), O[:, t].rearrange("p h c -> p (h c)"), ident)
                ins.then_inc(b_ot, 1)
            for c in range(CH):
                pe.wait_ge(b_ots, c + 1)
                mm(bank(4 + c), wt("opT"), OT[:, c * NC:(c + 1) * NC], start=True, stop=True).then_inc(b_op, 1)

            pe.wait_ge(b_x1, CH)
            pe.wait_ge(s_z2, 16)

            def proj3(t):
                x = XT[:, t * P:(t + 1) * P]
                if t >= 1:
                    pe.wait_ge(c_ks, 4 * t)
                for c in range(C3):
                    ins = mm(PS[:, c // 4, (c % 4) * P:(c % 4 + 1) * P], wt("wq3", c * P, (c + 1) * P), x, start=True, stop=True)
                ins.then_inc(c_q, 1)
                pe.wait_ge(c_qs, 2 * t + 2)
                for c in range(C3):
                    ins = mm(PS[:, c // 4, (c % 4) * P:(c % 4 + 1) * P], wt("wk3", c * P, (c + 1) * P), x, start=True, stop=True)
                ins.then_inc(c_k, 1)

            def keys3(t):
                if t >= 1:
                    pe.wait_ge(c_at, 2 * t)
                x = XT[:, t * P:(t + 1) * P]
                for i in range(2):
                    ins = mm(bank(2 + i), x, wt("wk3", i * 512, (i + 1) * 512), start=True, stop=True)
                ins.then_inc(c_t, 1)

            def scores3(t):
                pe.wait_ge(c_ks, 4 * t + 4)
                pe.wait_ge(c_ki, 2 * t + 2)
                if t >= 1:
                    pe.wait_ge(c_s1, 2 * t)
                for j in range(J):
                    for c in range(C3):
                        ins = mm(PS[32 * j:32 * j + 32, 4 + c // 4, (c % 4) * 68:(c % 4 + 1) * 68], qs[:, t % 2, c, 32 * j:32 * j + 32],
                                 kx3[:, t % 2, c, j].rearrange("p h k -> p (h k)"), start=True, stop=True)
                ins.then_inc(c_s, 1)

            def image3(t):
                pe.wait_ge(c_pie, t + 1)
                if t >= 1:
                    pe.wait_ge(c_pits, t)
                pe.transpose(PS[0:64, 7, 0:P], Pie3[:, t % 2].rearrange("p j h -> p (j h)"), ident).then_inc(c_pit, 1)

            def weigh3(t):
                pe.wait_ge(c_ptd, t + 1)
                pe.wait_ge(c_ts, 2 * t + 2)
                for f in range(2):
                    for h in range(H3):
                        o = 64 * (h % 2)
                        ins = mm(PS[o:o + 64, 2 + f, (h // 2) * 64:(h // 2 + 1) * 64], kt3[64 * f:64 * f + 64, t % 2, 64 * h:64 * h + 64],
                                 PTd[64 * f:64 * f + 64, t % 2, h].rearrange("p i q -> p (i q)"), start=True, stop=True)
                ins.then_inc(c_pv, 1)

            def output3(t):
                pe.wait_ge(c_at, 2 * t + 2)
                pe.wait_ge(c_pits, t + 1)
                if t >= 1:
                    pe.wait_ge(c_ytm, t)
                mm(bank(6, P), Z2[:, t * P:(t + 1) * P], PiT3[0:64, t % 2], start=True, stop=False)
                for c in range(C3):
                    ins = mm(bank(6, P), wt("wo3", c * P, (c + 1) * P), aT3[:, t % 2, c, :], start=False, stop=(c == C3 - 1))
                ins.then_inc(c_y, 1)

            def turn3(t):
                pe.wait_ge(c_ys, t + 1)
                pe.transpose(bank(6, P, P), YT[:, t * P:(t + 1) * P], ident).then_inc(c_yt, 1)

            for t in range(T + 1):
                if t < T:
                    proj3(t)
                if t >= 1:
                    image3(t - 1)
                    weigh3(t - 1)
                if t < T:
                    scores3(t)
                if t >= 1:
                    output3(t - 1)
                if t < T:
                    keys3(t)
                if t >= 1:
                    turn3(t - 1)

            pe.wait_ge(c_ytm, T)
            for t in range(T):
                ins = mm(bank(0, E, E * t), YT[:, t * P:(t + 1) * P], wt("rwT"), start=True, stop=True)
            ins.then_inc(d_lg, 1)
            pe.wait_ge(d_oh, 1)
            ohf = OH[:, :, :, :].rearrange("p s t e -> p (s t e)")
            mm(bank(1, 2 * T * E), cs("before"), ohf, start=True, stop=True)
            mm(bank(2, 2 * T * E), cs("ones"), ohf, start=True, stop=True).then_inc(d_cum, 1)
            for c in range(CH):
                for i in range(4):
                    t = 4 * c + i
                    ins = pe.transpose(bank(4 + c, P, i * P), XT[:, t * P:(t + 1) * P], ident)
                ins.then_inc(d_x1t, 1)
            pe.wait_ge(d_x1s, CH)
            pe.wait_ge(d_slot, 1)
            pe.wait_ge(d_fw, 32)
            for e in range(E):
                pe.wait_ge(d_xg[e % 2], 16 * 3 * (e // 2 + 1))
                if e:
                    pe.wait_ge(d_xts, e)
                for s, (a, b) in enumerate(RPARTS):
                    ins = pe.transpose(bank(0, b - a, a), XG[0:b - a, e % 2, s, :], cs("ident")[0:b - a, 0:b - a])
                ins.then_inc(d_xt, 1)
                pe.wait_ge(d_xts, e + 1)
                for m in range(HC):
                    if e:
                        pe.wait_ge(d_f1s, HC * (e - 1) + m + 1)
                    mm(bank(1 + m, CAP), FW[:, e, 0, m * P:(m + 1) * P], XGT[:, e % 2], start=True, stop=True).then_inc(d_f1, 1)
                if e:
                    pe.wait_ge(d_ye, e)
                for m in range(HC):
                    pe.wait_ge(d_f1s, HC * e + m + 1)
                    ins = mm(bank(5, CAP), FW[:, e, 1, m * P:(m + 1) * P], GH[:, e % 2, m], start=(m == 0), stop=(m == HC - 1))
                ins.then_inc(d_f2, 1)
                pe.wait_ge(d_ye, e + 1)
                if e:
                    pe.wait_ge(d_yts, e)
                for s, (a, b) in enumerate(RPARTS):
                    ins = pe.transpose(PS[0:b - a, 6, s * P:(s + 1) * P], YE[:, e % 2, a:b], ident)
                ins.then_inc(d_yt, 1)

        @block.scalar
        def _(act):
            A = act.activation
            act.wait_ge(s_w, 16)
            act.wait_ge(s_img, 1)
            A(kimg[:, :], bank(0, NB), ACT.Identity, bias=wt("ukb")).then_inc(s_imgsb, 1)
            A(vimg[:, :], bank(0, NB, NB), ACT.Identity, bias=wt("uvb")).then_inc(s_imgsb, 1)
            act.wait_ge(s_kp, 1)
            kps = PS[:, 4:8, :].rearrange("p c (t j n) -> p c t j n", j=J, n=L)
            for g in range(G1):
                for j in range(J):
                    A(K0[32 * j:32 * j + 32, g, :, 1:K1].rearrange("p (c t) n -> p c t n", c=4), kps[32 * g:32 * g + 32, :, :, j, :], ACT.Identity,
                      bias=wt("bk1")[32 * g:32 * g + 32]).then_inc(s_ksw, 1)
            act.wait_ge(s_wb, 16)
            act.wait_ge(s_ak, 1)
            for c in range(C3):
                A(ak3[:, c * NB:(c + 1) * NB], bank(0, NB, NB * c), ACT.Identity, bias=wt("bk3", c, c + 1))
            for c in range(C3):
                ins = A(av3[:, c * NB:(c + 1) * NB], bank(1, NB, NB * c), ACT.Identity, bias=wt("bv3", c, c + 1))
            ins.then_inc(s_ak3, 2)
            for i in range(4):
                act.wait_ge(s_z1p, i + 1)
                A(Z1[:, 4 * i:4 * i + 4, :].rearrange("p t c -> p (t c)"), PS[0:64, 2 + i % 2, :], ACT.Copy).then_inc(s_z1, 1)
            for r in range(2):
                act.wait_ge(s_z2p, r + 1)
                for o in range(2):
                    ins = A(Z2s[:, 8 * r + o:8 * r + 8:2, :], PS[0:64, 4 + o, :].rearrange("p (h c) -> p h c", c=P), ACT.Copy)
                ins.then_inc(s_z2s, 1)

            def softexp(t):
                act.wait_ge(a_s3, t + 1)
                if t >= 2:
                    act.wait_ge(a_pie, t - 1)
                A(P1[:, t % 2].rearrange("p h k -> p (h k)"), S2[:, t % 2].rearrange("p h k -> p (h k)"), ACT.Exp).then_inc(a_p, 1)

            def turned(t):
                act.wait_ge(a_t, t + 1)
                if t >= 2:
                    act.wait_ge(a_pv, t - 1)
                A(PT1[:, t % 2].rearrange("p g n -> p (g n)"), bank(4), ACT.Copy).then_inc(a_pt, 1)
                if t >= 2:
                    act.wait_ge(a_h, t - 1)
                A(PiT1[0:64, t % 2], PS[0:64, 5, 0:P], ACT.Copy).then_inc(a_pt, 1)

            def weighed(t):
                act.wait_ge(a_pv, t + 1)
                A(aT1[:, t % 2], bank(7, P), ACT.Copy).then_inc(a_at, 1)

            def projected(t):
                act.wait_ge(a_h, t + 1)
                if t == 0:
                    act.wait_ge(b_pad, 1)
                A(hP[:, :].rearrange("p (b l) -> p b l", b=NB)[:, J * t:J * t + J, 3:PADW], bank(5, P, P).rearrange("p (b l) -> p b l", b=J), ACT.Identity,
                  bias=wt("cpb")).then_inc(a_hs, 1)

            for t in range(T + 2):
                if t < T:
                    softexp(t)
                if t >= 2:
                    weighed(t - 2)
                    projected(t - 2)
                if 1 <= t <= T:
                    turned(t - 1)

            n = 0
            act.wait_ge(b_pad, 2)
            for i in (2, 1, 0):
                for c in range(CH):
                    act.wait_ge(b_pp, n + 1)
                    A(pre[i][:, 16 * c:16 * c + 16, 3:PADW], bank(n % 4).rearrange("p (b l) -> p b l", l=L), ACT.Copy).then_inc(b_pre, 1)
                    n += 1
            for c in range(CH):
                act.wait_ge(b_bp, c + 1)
                A(beta[:, c * NC:(c + 1) * NC], bank(4 + c), ACT.Sigmoid).then_inc(b_beta, 1)
            act.wait_ge(b_nrm, 1)
            A(qkv[2], qkv[2], ACT.Silu).then_inc(b_silu, 1)
            act.wait_ge(b_cv, 1)
            act.wait_ge(b_fl, 1) if False else None
            A(qkv[0], qkv[0], ACT.Silu).then_inc(b_silu, 1)
            act.wait_ge(b_nrm, 2)
            A(qkv[1], qkv[1], ACT.Silu).then_inc(b_silu, 1)
            act.wait_ge(b_silu, 3)
            A(sqr[1], qkv[1], ACT.Square).then_inc(b_sq, 1)
            A(sqr[0], qkv[0], ACT.Square).then_inc(b_sq, 1)
            for i in range(2):
                for c in range(CH):
                    act.wait_ge(b_n2, i * CH + c + 1)
                    A(rn[1 - i][:, c * NC:(c + 1) * NC], bank(c), ACT.Sqrt).then_inc(b_sqrt, 1)
            for n in range(8):
                m, c = n // 4, n % 4
                act.wait_ge(b_g1, n + 1)
                A(g1T[:, m, c * NC:(c + 1) * NC], bank(n % 4), ACT.Gelu, bias=wt("gb1", m, m + 1)).then_inc(b_g1s, 1)
            act.wait_ge(b_u0, 16)
            act.wait_ge(b_vd, 16 * H2)
            A(U[:, :, :, :], V0[:, :, :, :].rearrange("p s c i -> p s i c"), ACT.Copy).then_inc(b_ui, 1)
            act.wait_ge(b_ud, 16)
            for t in range(T):
                act.wait_ge(b_tr, t + 1)
                A(BR[:, t, 0:2].rearrange("p r h c -> p (r h c)"), bank(t % 2, 2 * P), ACT.Copy)
                A(BR[:, t, 3].rearrange("p h c -> p (h c)"), bank(t % 2, P, 2 * P), ACT.Copy).then_inc(b_br, 1)
            for t in range(T):
                act.wait_ge(b_o, t + 1)
                for f in range(2):
                    A(BR[64 * f:64 * f + 64, t, 2].rearrange("p h c -> p (h c)"), PS[64 * f:64 * f + 64, 4 + 2 * (t % 2) + f, 0:P], ACT.Copy).then_inc(b_od, 1)
            for t in range(T):
                act.wait_ge(b_dev, t + 1)
                A(DV[:, t], DV[:, t], ACT.Square).then_inc(b_dsq, 1)
            act.wait_ge(b_std, 1)
            A(sd, sd, ACT.Sqrt, scale=1.0 / (D2 - 1)).then_inc(b_stds, 1)
            act.wait_ge(b_ee, 1)
            A(gate, gate, ACT.Exp).then_inc(b_exp, 1)
            act.wait_ge(b_mix, 1)
            A(OS, O, ACT.Square).then_inc(b_osq, 1)
            act.wait_ge(b_ors, 1)
            A(oms, oms, ACT.Sqrt).then_inc(b_ors, 1)
            for c in range(CH):
                act.wait_ge(b_ot, c + 1)
                A(OT[:, c * NC:(c + 1) * NC], bank(c), ACT.Copy, scale=wt("onw")).then_inc(b_ots, 1)

            def queries3(t):
                act.wait_ge(c_q, t + 1)
                if t >= 2:
                    act.wait_ge(c_s, t - 1)
                for c in range(C3):
                    ins = A(qs[:, t % 2, c, :], PS[:, c // 4, (c % 4) * P:(c % 4 + 1) * P], ACT.Identity, bias=wt("bq3", c, c + 1))
                    if c % 4 == 3:
                        ins.then_inc(c_qs, 1)

            def softexp3(t):
                act.wait_ge(c_s3, t + 1)
                if t >= 2:
                    act.wait_ge(c_pn, t - 1)
                    act.wait_ge(c_pie, t - 1)
                A(P3[:, t % 2].rearrange("p h k -> p (h k)"), Sd[:, t % 2].rearrange("p h k -> p (h k)"), ACT.Exp).then_inc(c_p, 1)

            def image3s(t):
                act.wait_ge(c_pit, t + 1)
                if t >= 2:
                    act.wait_ge(c_y, t - 1)
                A(PiT3[0:64, t % 2], PS[0:64, 7, 0:P], ACT.Copy).then_inc(c_pits, 1)

            def weighed3(t):
                act.wait_ge(c_pv, t + 1)
                for f in range(2):
                    A(aT3[:, t % 2, :, 64 * f:64 * f + 64], bank(2 + f).rearrange("p (c n) -> p c n", c=C3), ACT.Copy).then_inc(c_at, 1)

            def out3(t):
                act.wait_ge(c_y, t + 1)
                A(YT[:, t * P:(t + 1) * P], bank(6, P), ACT.Identity, bias=wt("bo3")).then_inc(c_ys, 1)
                act.wait_ge(c_yt, t + 1)
                A(Y[:, t, :], bank(6, P, P), ACT.Copy).then_inc(c_ytm, 1)

            act.wait_ge(b_x1, CH)
            for t in range(T + 1):
                if t < T:
                    queries3(t)
                if t >= 1:
                    image3s(t - 1)
                    weighed3(t - 1)
                if t < T:
                    softexp3(t)
                if t >= 1:
                    out3(t - 1)

            act.wait_ge(d_ex, 1)
            A(LG, LG, ACT.Exp).then_inc(d_exps, 1)
            for e in range(E):
                for m in range(HC):
                    act.wait_ge(d_f1, HC * e + m + 1)
                    A(GH[:, e % 2, m], bank(1 + m, CAP), ACT.Gelu, bias=wt("fb1", e * HC + m, e * HC + m + 1)).then_inc(d_f1s, 1)

        @block.vector
        def _(dve):
            chain = [0]

            def link(ins):
                chain[0] += 1
                ins.then_inc(ch_v, 1)
                dve.wait_ge(ch_v, chain[0])

            dve.wait_ge(s_w, 16)
            dve.wait_ge(s_zero, 1)
            dve.wait_ge(s_qp, 1)
            qps = PS[:, 0:4, :].rearrange("p c (t j n) -> p c t j n", j=J, n=L)
            for g in range(G1):
                for j in range(J):
                    dve.tensor_scalar(Qd[32 * j:32 * j + 32, g].rearrange("p (c t j n) -> p c t j n", c=4, j=J, n=L)[:, :, :, j, :],
                                      qps[32 * g:32 * g + 32, :, :, j, :], wt("bq1")[32 * g:32 * g + 32], None, ALU.add).then_inc(s_qsw, 1)
            dve.wait_ge(s_imgsb, 2)
            for g in range(G1):
                for j in range(J):
                    dve.tensor_copy(K0[32 * j:32 * j + 32, g, :, 0],
                                    kimg[32 * g:32 * g + 32, :].rearrange("p (t j) -> p j t", j=J)[:, j, :]).then_inc(s_k00, 1)
            dve.wait_ge(s_c, 16)
            dve.wait_ge(s_mk, 2)

            def mask1(t):
                dve.wait_ge(a_s, t + 1)
                for i in range(2):
                    dve.scalar_tensor_tensor(out=S1[:, t % 2, 8 * i:8 * i + 8, :], in0=PS[:, 2 * (t % 2) + i, 0:264].rearrange("p (h k) -> p h k", h=8),
                                             scalar=float(1.0 / np.sqrt(np.float32(D1))),
                                             in1=cs("c01").rearrange("p (o k) -> p o k", o=1).broadcast_to([P, 8, K1]),
                                             op0=ALU.mult, op1=ALU.mult).then_inc(a_s1, 1)
                dve.wait_ge(a_s1, 2 * t + 2)
                if t >= 2:
                    dve.wait_ge(a_p, t - 1)
                link(dve.tensor_tensor(S2[:, t % 2], S1[:, t % 2], Mk[:, t:t + 1, :].broadcast_to([P, H1, K1]), ALU.add))
                dve.tensor_reduce(mx1[:, t % 2], S2[:, t % 2], AX.X, ALU.max).then_inc(a_mx, 1)

            def values1(t):
                dve.wait_ge(a_v, t + 1)
                if t >= 2:
                    dve.wait_ge(a_vx, t - 1)
                dve.tensor_tensor(Vt1[:, t % 2], PS[:, 6, :].rearrange("p (j c) -> p j c", j=J),
                                  wt("bv1r").rearrange("p (o c) -> p o c", o=1).broadcast_to([P, J, P]), ALU.add).then_inc(a_vt, 1)

            def norm1(t):
                dve.wait_ge(a_p, t + 1)
                link(dve.tensor_reduce(sm1[:, t % 2], P1[:, t % 2], AX.X, ALU.add))
                link(dve.reciprocal(rs1[:, t % 2], sm1[:, t % 2]))
                if t >= 2:
                    dve.wait_ge(a_t, t - 1)
                dve.tensor_tensor(Pn1[:, t % 2].rearrange("p (h k) -> p h k", h=H1), P1[:, t % 2, :, 1:K1],
                                  rs1[:, t % 2].rearrange("p (h o) -> p h o", o=1).broadcast_to([P, H1, L]), ALU.mult).then_inc(a_pn, 1)
                link(dve.tensor_tensor(sm1[:, t % 2], P1[:, t % 2, :, 0], rs1[:, t % 2], ALU.mult))
                dve.tensor_tensor(Pie1[:, t % 2], sm1[:, t % 2].rearrange("p (o h) -> p o h", o=1).broadcast_to([P, J, H1]),
                                  cs("jm4").rearrange("p (j o) -> p j o", o=1).broadcast_to([P, J, H1]), ALU.mult).then_inc(a_pie, 1)

            for t in range(T + 1):
                if t < T:
                    mask1(t)
                    values1(t)
                if t >= 1:
                    norm1(t - 1)

            dve.wait_ge(s_wb, 16)
            dve.wait_ge(a_hs, T)
            dve.memset(ar(0, 6720), 0.0).then_inc(b_pad, 1)
            for i, name in ((2, "cwv"), (1, "cwk")):
                dve.wait_ge(b_pre, CH * (3 - i))
                y = qkv3[i]
                link(dve.tensor_scalar(y, pre[i][:, :, 0:L], wt(name, 0, 1), None, ALU.mult))
                for k in range(1, 4):
                    ins = dve.scalar_tensor_tensor(out=y, in0=pre[i][:, :, k:k + L], scalar=wt(name, k, k + 1), in1=y, op0=ALU.mult, op1=ALU.add)
                    if k < 3:
                        link(ins)
                ins.then_inc(b_nrm, 1)
            dve.wait_ge(b_silu, 3)
            dve.wait_ge(b_beta, CH)
            dve.tensor_tensor(vb, qkv[2], beta, ALU.mult).then_inc(b_vb, 1)
            dve.wait_ge(b_sqrt, CH)
            link(dve.reciprocal(rn[1], rn[1]))
            link(dve.tensor_tensor(qkv[1], qkv[1], rn[1], ALU.mult))
            dve.tensor_tensor(kb, qkv[1], beta, ALU.mult)
            dve.wait_ge(b_sqrt, 2 * CH)
            link(dve.reciprocal(rn[0], rn[0]))
            dve.tensor_tensor(qkv[0], qkv[0], rn[0], ALU.mult).then_inc(b_nrm, 1)
            dve.wait_ge(s_z2d, 16)
            mn = cs("maskn").rearrange("p (o n) -> p o n", o=1).broadcast_to([P, 8, 64])
            ma = cs("maska").rearrange("p (o n) -> p o n", o=1).broadcast_to([P, 8, 64])
            for r in range(2):
                for G, b0, ready, done, m in ((GN, 0, b_gn, b_gns, mn), (GA, 4, b_ga, b_gas, ma)):
                    dve.wait_ge(ready, r + 1)
                    for h in range(H2):
                        dve.tensor_tensor(G[:, h, 8 * r:8 * r + 8, :], PS[:, b0 + h, :].rearrange("p (t n) -> p t n", n=64), m, ALU.mult).then_inc(done, 1)
            v = qkv3[2]
            link(dve.tensor_scalar(fs, v, wt("firs", 6, 7), None, ALU.mult))
            for lag in range(1, 7):
                ins = dve.scalar_tensor_tensor(out=fs[:, :, lag:L], in0=v[:, :, 0:L - lag], scalar=wt("firs", 6 - lag, 7 - lag),
                                               in1=fs[:, :, lag:L], op0=ALU.mult, op1=ALU.add)
                if lag < 6:
                    link(ins)
            ins.then_inc(b_fs, 1)
            link(dve.tensor_scalar(fl, v, wt("firl", 30, 31), None, ALU.mult))
            for lag in range(1, 31):
                ins = dve.scalar_tensor_tensor(out=fl[:, :, lag:L], in0=v[:, :, 0:L - lag], scalar=wt("firl", 30 - lag, 31 - lag),
                                               in1=fl[:, :, lag:L], op0=ALU.mult, op1=ALU.add)
                if lag < 30:
                    link(ins)
            ins.then_inc(b_fl, 1)
            dve.wait_ge(b_g2, 1)
            dve.tensor_tensor(gate.rearrange("p t r h -> p t (r h)"), bank(4, T * H1).rearrange("p (t n) -> p t n", t=T),
                              wt("gb2r").rearrange("p (o n) -> p o n", o=1).broadcast_to([P, T, H1]), ALU.add).then_inc(b_gate, 1)
            dve.wait_ge(b_ui, 1)
            dve.wait_ge(b_pn, 16)
            for j in range(L - 1):
                m = L - 1 - j
                link(dve.tensor_tensor(tmpU[:, :, 0:m, :], PN[:, :, j + 1:L, j:j + 1].broadcast_to([P, 2, m, D2]),
                                       U[:, :, j:j + 1, :].broadcast_to([P, 2, m, D2]), ALU.mult))
                ins = dve.tensor_tensor(U[:, :, j + 1:L, :], U[:, :, j + 1:L, :], tmpU[:, :, 0:m, :], ALU.add)
                if j < L - 2:
                    link(ins)
            ins.then_inc(b_solved, 1)
            for t in range(T):
                dve.wait_ge(b_br, t + 1)
                dve.wait_ge(b_od, 2 * t + 2)
                dve.tensor_reduce(bmx[:, t], BR[:, t], AX.X, ALU.max)
                link(dve.tensor_reduce(mu[:, t], BR[:, t], AX.X, ALU.add))
                dve.tensor_scalar(mu[:, t], mu[:, t], 1.0 / D2, None, ALU.mult).then_inc(b_sum, 1)
            for t in range(T):
                dve.wait_ge(b_dsq, t + 1)
                ins = dve.tensor_reduce(sd[:, t], DV[:, t], AX.X, ALU.add)
            ins.then_inc(b_std, 1)
            dve.wait_ge(b_sum, T)
            link(dve.tensor_tensor(mu, mu, bmx, ALU.add))
            dve.wait_ge(b_stds, 1)
            link(dve.tensor_tensor(mu, mu, sd, ALU.add))
            link(dve.tensor_scalar(mu, mu, 1.0 / 3.0, None, ALU.mult))
            al = wt("alphar").rearrange("p (o u h) -> p o u h", o=1, u=1).broadcast_to([P, T, 4, H2])
            link(dve.tensor_tensor(mu, mu, al, ALU.mult))
            link(dve.tensor_tensor(gate, gate, mu, ALU.add))
            link(dve.tensor_reduce(lmx, gate.rearrange("p t r h -> p t h r"), AX.X, ALU.max))
            bc = lambda x: x.rearrange("p t (o h) -> p t o h", o=1).broadcast_to([P, T, 4, H2])
            dve.tensor_tensor(gate, gate, bc(lmx), ALU.subtract).then_inc(b_ee, 1)
            dve.wait_ge(b_exp, 1)
            link(dve.tensor_reduce(lmx, gate.rearrange("p t r h -> p t h r"), AX.X, ALU.add))
            link(dve.reciprocal(lmx, lmx))
            link(dve.tensor_tensor(gate, gate, bc(lmx), ALU.mult))
            for t in range(T):
                link(dve.tensor_tensor(BR[:, t], BR[:, t], gate[:, t].rearrange("p r (h o) -> p r h o", o=1).broadcast_to([P, 4, H2, D2]), ALU.mult))
            link(dve.tensor_tensor(O, BR[:, :, 0], BR[:, :, 1], ALU.add))
            link(dve.tensor_tensor(O, O, BR[:, :, 2], ALU.add))
            dve.tensor_tensor(O, O, BR[:, :, 3], ALU.add).then_inc(b_mix, 1)
            dve.wait_ge(b_osq, 1)
            link(dve.tensor_reduce(oms, OS, AX.X, ALU.add))
            dve.tensor_scalar(oms, oms, 1.0 / D2, 1e-5, ALU.mult, ALU.add).then_inc(b_ors, 1)
            dve.wait_ge(b_ors, 2)
            link(dve.reciprocal(oms, oms))
            for c in range(CH):
                dve.tensor_tensor(O[:, 4 * c:4 * c + 4], O[:, 4 * c:4 * c + 4],
                                  oms[:, 4 * c:4 * c + 4].rearrange("p t (h o) -> p t h o", o=1).broadcast_to([P, 4, H2, D2]), ALU.mult).then_inc(b_on, 1)
            for c in range(CH):
                dve.wait_ge(b_op, c + 1)
                dve.tensor_tensor(XT[:, c * NC:(c + 1) * NC], XT[:, c * NC:(c + 1) * NC], bank(4 + c), ALU.add).then_inc(b_x1, 1)

            def keys3(t):
                dve.wait_ge(c_k, t + 1)
                if t >= 2:
                    dve.wait_ge(c_s, t - 1)
                if t == 0:
                    dve.wait_ge(c_zero, 1)
                for f in range(2):
                    o = slice(64 * f, 64 * f + 64)
                    dve.tensor_copy(kx3[o, t % 2, :, :, f, 0], ak3[o, :].rearrange("p (c b) -> p c b", c=C3)[:, :, J * t:J * t + J]).then_inc(c_ki, 1)
                    for i in range(2):
                        dve.tensor_tensor(kx3[o, t % 2, 4 * i:4 * i + 4, :, f, 1:L + 1], PS[o, i, :].rearrange("p (c j n) -> p c j n", c=4, j=J),
                                          wt("bk3", 4 * i, 4 * i + 4)[o].rearrange("p (c u v) -> p c u v", u=1, v=1).broadcast_to([64, 4, J, L]),
                                          ALU.add).then_inc(c_ks, 1)

            def rows3(t):
                dve.wait_ge(c_t, t + 1)
                if t >= 2:
                    dve.wait_ge(c_pv, t - 1)
                for i in range(2):
                    dve.tensor_tensor(kt3[:, t % 2, 512 * i:512 * i + 512], bank(2 + i), wt("bk3r", 512 * i, 512 * i + 512), ALU.add).then_inc(c_ts, 1)

            def mask3(t):
                dve.wait_ge(c_s, t + 1)
                if t >= 2:
                    dve.wait_ge(c_s3, t - 1)
                for i in range(2):
                    dve.scalar_tensor_tensor(out=Sc[:, t % 2, 8 * i:8 * i + 8, :], in0=PS[:, 4 + i, 0:272].rearrange("p (h k) -> p h k", h=8), scalar=1.0 / 8.0,
                                             in1=cs("band").rearrange("p (o k) -> p o k", o=1).broadcast_to([P, 8, K3]), op0=ALU.mult, op1=ALU.add).then_inc(c_s1, 1)
                dve.wait_ge(c_s1, 2 * t + 2)
                dve.tensor_reduce(mx3[:, t % 2], Sc[:, t % 2], AX.X, ALU.max).then_inc(c_mx, 1)

            def norm3(t):
                dve.wait_ge(c_p, t + 1)
                link(dve.tensor_reduce(sm3[:, t % 2], P3[:, t % 2], AX.X, ALU.add))
                link(dve.reciprocal(rs3[:, t % 2], sm3[:, t % 2]))
                dve.tensor_tensor(Pn3[:, t % 2].rearrange("p (h k) -> p h k", h=H3), P3[:, t % 2, :, 1:L + 1],
                                  rs3[:, t % 2].rearrange("p (h o) -> p h o", o=1).broadcast_to([P, H3, L]), ALU.mult).then_inc(c_pn, 1)
                link(dve.tensor_tensor(sm3[:, t % 2], P3[:, t % 2, :, 0], rs3[:, t % 2], ALU.mult))
                if t >= 2:
                    dve.wait_ge(c_pit, t - 1)
                dve.tensor_tensor(Pie3[:, t % 2], sm3[:, t % 2].rearrange("p (o h) -> p o h", o=1).broadcast_to([P, J, H3]),
                                  cs("jm4").rearrange("p (j o) -> p j o", o=1).broadcast_to([P, J, H3]), ALU.mult).then_inc(c_pie, 1)
                dve.wait_ge(c_pn, t + 1)
                if t >= 2:
                    dve.wait_ge(c_ptd, t - 1)
                dve.transpose(PTc[:, t % 2], Pn3[:, t % 2]).then_inc(c_ptc, 1)

            for t in range(T + 1):
                if t < T:
                    keys3(t)
                    mask3(t)
                    rows3(t)
                    norm3(t)

            dve.wait_ge(d_lg, 1)
            eb = lambda x: x.rearrange("p (t o) -> p t o", o=1).broadcast_to([P, T, E])
            rk = cs("rank").rearrange("p (o e) -> p o e", o=1).broadcast_to([P, T, E])
            link(dve.tensor_tensor(LG, bank(0, T * E).rearrange("p (t e) -> p t e", t=T), wt("rbr").rearrange("p (o e) -> p o e", o=1).broadcast_to([P, T, E]), ALU.add))
            link(dve.tensor_reduce(lm, LG, AX.X, ALU.max))
            dve.tensor_tensor(LG, LG, eb(lm), ALU.subtract).then_inc(d_ex, 1)
            dve.wait_ge(d_exps, 1)
            link(dve.tensor_reduce(lm, LG, AX.X, ALU.add))
            link(dve.reciprocal(lm, lm))
            link(dve.tensor_tensor(LG, LG, eb(lm), ALU.mult))
            for s in range(2):
                link(dve.tensor_reduce(tv[:, s], LG, AX.X, ALU.max))
                link(dve.tensor_tensor(tq, LG, eb(tv[:, s]), ALU.is_equal))
                link(dve.tensor_tensor(tq, tq, rk, ALU.mult))
                link(dve.tensor_reduce(tk[:, s], tq, AX.X, ALU.max))
                link(dve.tensor_tensor(OH[:, s], rk, eb(tk[:, s]), ALU.is_equal))
                if s == 0:
                    link(dve.scalar_tensor_tensor(out=LG, in0=OH[:, 0], scalar=-4.0, in1=LG, op0=ALU.mult, op1=ALU.add))
            link(dve.tensor_tensor(lm, tv[:, 0], tv[:, 1], ALU.add))
            link(dve.tensor_scalar(lm, lm, EPS, None, ALU.add))
            link(dve.reciprocal(lm, lm))
            link(dve.tensor_tensor(tv, tv, lm.rearrange("p (o t) -> p o t", o=1).broadcast_to([P, 2, T]), ALU.mult))
            link(dve.tensor_scalar(vl, tv, EPS, None, ALU.is_gt))
            dve.tensor_tensor(OH, OH, vl.rearrange("p s (t o) -> p s t o", o=1).broadcast_to([P, 2, T, E]), ALU.mult).then_inc(d_oh, 1)
            dve.wait_ge(d_cum, 1)
            totv = tot.rearrange("p (e s t) -> p e s t", e=E, s=2)
            ohe = OH[:, :, :, :].rearrange("p s t e -> p e s t")
            link(dve.tensor_copy(totv, bank(2, 2 * T * E).rearrange("p (s t e) -> p e s t", s=2, t=T)))
            link(dve.tensor_tensor_scan(out=run_, data0=cs("seg"), data1=tot, initial=0.0, op0=ALU.mult, op1=ALU.add))
            link(dve.tensor_tensor(run_, run_, tot, ALU.subtract))
            link(dve.tensor_tensor(pos, run_.rearrange("p (e s t) -> p s t e", e=E, s=2), bank(1, 2 * T * E).rearrange("p (s t e) -> p s t e", s=2, t=T), ALU.add))
            st = lambda x: x.rearrange("p (s t) -> p s t", s=2)
            link(dve.tensor_tensor(pos, pos, OH, ALU.mult))
            link(dve.tensor_reduce(st(pown), pos, AX.X, ALU.add))
            eb4 = cs("ebase").rearrange("p (o u e) -> p o u e", o=1, u=1).broadcast_to([P, 2, T, E])
            link(dve.tensor_tensor(pos, OH, eb4, ALU.mult))
            link(dve.tensor_reduce(st(slot), pos, AX.X, ALU.add))
            link(dve.tensor_scalar(keep, pown, float(CAP), None, ALU.is_lt))
            link(dve.tensor_tensor(st(keep), st(keep), vl, ALU.mult))
            link(dve.tensor_tensor(slot, slot, pown, ALU.add))
            link(dve.tensor_tensor(tv, tv, st(keep), ALU.mult))
            link(dve.tensor_tensor(slot, slot, keep, ALU.mult))
            link(dve.tensor_scalar(pown, keep, -1.0, 1.0, ALU.mult, ALU.add))
            link(dve.tensor_tensor(sidx, pown, cs("dummy"), ALU.mult))
            link(dve.tensor_tensor(sidx, sidx, slot, ALU.add))
            link(dve.scalar_tensor_tensor(out=gidx, in0=pown, scalar=float(SLOTS), in1=slot, op0=ALU.mult, op1=ALU.add))
            link(dve.tensor_copy(sI, sidx))
            dve.tensor_copy(gI, gidx).then_inc(d_slot, 1)
            for c in range(CH):
                dve.wait_ge(d_x1t, c + 1)
                dve.tensor_copy(X1[:, 4 * c:4 * c + 4, :].rearrange("p t c -> p (t c)"), bank(4 + c)).then_inc(d_x1s, 1)
            for e in range(E):
                dve.wait_ge(d_xt, e + 1)
                dve.tensor_copy(XGT[:, e % 2], bank(0, CAP)).then_inc(d_xts, 1)
                dve.wait_ge(d_f2, e + 1)
                dve.wait_ge(d_xts, e + 1)
                if e >= 2:
                    dve.wait_ge(d_yt, e - 1)
                link(dve.tensor_scalar(YE[:, e % 2], bank(5, CAP), wt("fb2", e, e + 1), wt("lsc", e, e + 1), ALU.add, ALU.mult))
                dve.tensor_tensor(YE[:, e % 2], YE[:, e % 2], XGT[:, e % 2], ALU.add).then_inc(d_ye, 1)
                dve.wait_ge(d_yt, e + 1)
                if e >= 2:
                    dve.wait_ge(d_yd[e % 2], 16 * 3 * (e // 2))
                for s, (a, b) in enumerate(RPARTS):
                    ins = dve.tensor_copy(YO[0:b - a, e % 2, s, :], PS[0:b - a, 6, s * P:(s + 1) * P])
                ins.then_inc(d_yts, 1)
            for t in range(T):
                dve.wait_ge(d_ga[t // 4], 16 * 8)
                link(dve.tensor_scalar(RO[:, t, :], YG[:, 0, t, :], tv[:, 0, t:t + 1], None, ALU.mult))
                link(dve.scalar_tensor_tensor(out=RO[:, t, :], in0=YG[:, 1, t, :], scalar=tv[:, 1, t:t + 1], in1=RO[:, t, :], op0=ALU.mult, op1=ALU.add))
                dve.tensor_tensor(RO[:, t, :], RO[:, t, :], X1[:, t, :], ALU.add).then_inc(d_fin, 1)


def constants():
    p = np.arange(P)
    j, q = p // L, p % L
    f = np.float32
    c = {}
    c["ident"] = np.eye(P)
    c["bones"] = (p[:, None] // D2 == p[None] // D2)
    c["ones"] = np.ones((P, P))
    c["before"] = (p[:, None] < p[None])
    c["hm4"] = (p[:, None] % 32) // D1 == np.arange(4)[None]
    c["hmv"] = (p[:, None] // L == (p[None] % 32) // D1)
    c["hm16"] = p[:, None] // D1 == np.arange(H1)[None]
    c["jm4"] = j[:, None] == np.arange(J)[None]
    c["c01"] = np.arange(K1)[None] <= q[:, None] + 1
    c["nonc"] = -10000.0 * (1 - c["c01"])
    k64 = np.arange(64)
    same = (j[:, None] % 2) == (k64[None] // L)
    c["maskn"] = -1.0 * (same & (k64[None] % L < q[:, None]))
    c["maska"] = 1.0 * (same & (q[:, None] <= k64[None] % L))
    band = np.full((P, K3), NEG)
    band[:, 0] = 0
    band[:, 1:L + 1][np.abs(np.arange(L)[None] - q[:, None]) <= 1] = 0
    band[(q == 0) | (q == L - 1), L + 1] = 0
    c["band"] = band
    c["jm2"] = (j[:, None] % 2) == np.arange(2)[None]
    c["rank"] = np.broadcast_to(E - np.arange(E), (P, E))
    c["ebase"] = np.broadcast_to(CAP * np.arange(E), (P, E))
    c["dummy"] = SLOTS + P * np.arange(2 * T)[None] + p[:, None]
    c["seg"] = np.broadcast_to(np.arange(E * 2 * T) % (2 * T) != 0, (P, E * 2 * T))
    return np.concatenate([c[n].astype(f) for n, _ in CONSTS], axis=1)


def kernel(**inputs):
    import concourse.bacc as bacc
    from concourse.bass_utils import run_bass_kernel_spmd

    i = {k: np.asarray(v) for k, v in inputs.items()}
    col = lambda a: a.reshape(-1, P).T
    row = lambda a: np.broadcast_to(a.reshape(1, -1), (P, a.size))
    A, G, S, F = "L0_cond_", "L0_attn_", "L0_cond2_", "L0_ffn_"
    w = {
        "wqkv": i[A + "c_attn_w"], "cproj": i[A + "c_proj_w"], "ukT": i[A + "uk_w"].T, "uvT": i[A + "uv_w"].T,
        "condT": i["cond_1024"].T, "qpT": i[G + "q_proj_w"].T, "kpT": i[G + "k_proj_w"].T, "vpT": i[G + "v_proj_w"].T,
        "bpT": np.repeat(i[G + "b_proj_w"].T, D2, axis=1), "gw1T": i[G + "gmix_w1"].T,
        "gw2T": i[G + "gmix_w2"].T.reshape(2, P, H1).transpose(1, 0, 2).reshape(P, -1), "opT": i[G + "o_proj_w"].T,
        "wq3": i[S + "WQ_w"], "wk3": i[S + "WK_w"], "wv3": i[S + "WV_w"],
        "wo3": i[S + "WO_w"].reshape(C3, P, D).transpose(1, 0, 2).reshape(P, -1), "rwT": i[F + "router_w"].T,
        "bq1": col(i[A + "c_attn_b"][0:D]), "bk1": col(i[A + "c_attn_b"][D:2 * D]), "ukb": col(i[A + "uk_b"]), "uvb": col(i[A + "uv_b"]),
        "cpb": col(i[A + "c_proj_b"]), "cwq": i[G + "q_conv_w"], "cwk": i[G + "k_conv_w"], "cwv": i[G + "v_conv_w"],
        "firs": i[G + "fir_short_w"].reshape(P, -1), "firl": i[G + "fir_long_w"].reshape(P, -1), "gb1": col(i[G + "gmix_b1"]),
        "onw": np.tile(i[G + "o_norm_w"], H2).reshape(P, 1), "bq3": col(i[S + "WQ_b"]), "bk3": col(i[S + "WK_b"]), "bv3": col(i[S + "WV_b"]),
        "bo3": col(i[S + "WO_b"]), "fb1": col(i[F + "fc1_b"]), "fb2": i[F + "fc2_b"].T, "lsc": i[F + "layer_scale"].T,
        "bv1r": row(i[A + "c_attn_b"][2 * D:]), "gb2r": row(i[G + "gmix_b2"]), "alphar": row(i[G + "alpha"]), "rbr": row(i[F + "router_b"]),
        "bk3r": row(i[S + "WK_b"]),
    }
    for n, width in WEIGHTS:
        assert w[n].shape == (P, width), (n, w[n].shape)
    arrays = {
        "xT": np.ascontiguousarray(i["x"].reshape(N, D).T),
        "w": np.ascontiguousarray(np.concatenate([w[n] for n, _ in WEIGHTS], axis=1)),
        "cst": constants(),
        "mask": np.ascontiguousarray(i["mask_Bx1x1xS_ff0"].reshape(NB, L)),
        "fc1": np.ascontiguousarray(i[F + "fc1_w"].transpose(2, 0, 1)),
        "fc2": np.ascontiguousarray(i[F + "fc2_w"].transpose(2, 0, 1).reshape(HC, P, E, D).transpose(1, 2, 0, 3).reshape(P, E, HID)),
    }
    nc = bacc.Bacc("TRN2", target_bir_lowering=False, num_devices=1)
    f = mybir.dt.float32
    aps = [nc.dram_tensor(k, a.shape, f, kind="ExternalInput").ap() for k, a in arrays.items()]
    scratch = {"xscr": (XROWS, D), "yscr": (SLOTS + 1, D), "nscr": (NB, H2, L, L), "vscr": (NB, H2, D2, L), "uscr": (NB, H2, L, D2), "zscr": (NB, H3, D)}
    aps += [nc.dram_tensor(k, s, f, kind="Internal").ap() for k, s in scratch.items()]
    o = nc.dram_tensor("out", (N, D), f, kind="ExternalOutput").ap()
    program(nc, *aps, o)
    r = run_bass_kernel_spmd(nc, [arrays], core_ids=[0])
    return r.results[0]["out"].reshape(NB, L, D)
```

```python
import numpy as np
import concourse.bass as bass
from concourse import mybir
from contextlib import ExitStack

NB, L, D = 64, 32, 128
N = NB * L
P = 128
T = N // P
J = P // L
CH = 4
NC = N // CH
H1, D1 = 16, 8
G1 = 4
K1 = L + 1
H2, D2 = 4, 32
H3, D3 = 16, 64
C3 = H3 * D3 // P
K3 = L + 2
E, HID = 8, 512
HC = HID // P
CAP = int(1.2 * (N // E + 1))
SLOTS = E * CAP
TH, NH = T // 2, N // 2
AREA_A = 15200
AREA = AREA_A + 19744
XROWS = SLOTS + 2 * N
SP = -(-SLOTS // P)
YROWS = 3 * N + SLOTS
PADW = L + 3
NEG = -1e30
EPS = 1e-9

CONSTS = [("ident", P), ("hm2", H2), ("ones", P), ("before", P), ("hm4", G1), ("hmv", P), ("hm16", H1),
          ("jm4", J), ("c01", K1), ("nonc", K1), ("maskn", 64), ("maska", 64), ("band", K3), ("jm2", 2),
          ("rank", E), ("ebase", E), ("dummy", 2 * T), ("seg", E * 2 * T), ("tok", T), ("empty", SP), ("slotix", 3)]
WEIGHTS = [("wqkv", 3 * D), ("cproj", D), ("ukT", D), ("uvT", D), ("condT", NB),
           ("bq1", 1), ("bk1", 1), ("ukb", 1), ("uvb", 1), ("cpb", 1), ("bv1r", D),
           ("qpT", D), ("kpT", D), ("vpT", D),
           ("bpT", H2), ("gw1T", 2 * D), ("gw2T", 2 * H1), ("opT", D), ("wq3", C3 * P), ("wk3", C3 * P),
           ("wv3", C3 * P), ("wo3", C3 * P), ("rwT", E),
           ("cwq", 4), ("cwk", 4), ("cwv", 4),
           ("firs", 7), ("firl", 31), ("gb1", 2), ("onw", 1), ("bq3", C3), ("bk3", C3), ("bv3", C3), ("bo3", 1),
           ("fb1", E * HC), ("fb2", E), ("lsc", E),
           ("gb2r", H1), ("alphar", 4), ("rbr", E)]


def offsets(fields):
    at, out = 0, {}
    for name, width in fields:
        out[name] = (at, width)
        at += width
    return out, at


def program(nc, xT, w, cst, mask, fc1, fc2, xscr, yscr, nscr, vscr, uscr, zscr, out):
    fp32, i32 = mybir.dt.float32, mybir.dt.int32
    ALU, ACT, AX = mybir.AluOpType, mybir.ActivationFunctionType, mybir.AxisListType
    wo, WW = offsets(WEIGHTS)
    co, CW = offsets(CONSTS)
    ctx = ExitStack()
    with ctx:
        def sb(name, cols, parts=P, dt=fp32):
            return ctx.enter_context(nc.sbuf_tensor(name, [parts, cols], dt))

        def sem(name):
            return ctx.enter_context(nc.semaphore(name))

        W = sb("W", WW)
        Cn = sb("Cn", CW)
        XT = sb("XT", N)
        hT = sb("hT", N)
        Z2 = sb("Z2", T * P, 64)
        kimg = sb("kimg", NB)
        vimg = sb("vimg", NB)
        ak3 = sb("ak3", C3 * NB)
        av3 = sb("av3", C3 * NB)
        SM = sb("SM", 2464)
        AR = sb("AR", AREA)
        PS = ctx.enter_context(nc.psum_tensor("PS", [P, 8, 512], fp32))

        def wt(name, a=0, b=None):
            o, n = wo[name]
            return W[:, o + a:o + (n if b is None else b)]

        def cs(name, a=0, b=None):
            o, n = co[name]
            return Cn[:, o + a:o + (n if b is None else b)]

        def ar(at, n, parts=P):
            return AR[0:parts, at:at + n]

        small_at = [0]

        def small(n):
            a = small_at[0]
            small_at[0] += n
            return SM[:, a:a + n]

        ident = cs("ident")

        def br(at, n):
            return AR[:, AREA_A + at:AREA_A + at + n]

        def bank(i, cols=512, at=0):
            return PS[:, i, at:at + cols]

        Qd = ar(0, 4096).rearrange("p (g n) -> p g n", g=G1)
        K0 = ar(4096, 1056).rearrange("p (g t k) -> p g t k", g=G1, t=TH)
        Kx = ar(5152, 1056).rearrange("p (r g h k) -> p r g h k", r=2, g=G1, h=4)
        S2 = ar(6208, 1056).rearrange("p (r h k) -> p r h k", r=2, h=H1)
        P1 = ar(7264, 1056).rearrange("p (r h k) -> p r h k", r=2, h=H1)
        Pn1 = ar(8320, 512)
        PT1 = ar(8832, 1024).rearrange("p (r g n) -> p r g n", r=2, g=G1)
        Vt1 = ar(9856, 512).rearrange("p (j c) -> p j c", j=J)
        Vx1 = ar(10368, 1024).rearrange("p (r j c) -> p r j c", r=2, j=J)
        Z1 = AR[0:64, 11392:13440].rearrange("p (t c) -> p t c", t=T)
        Mk = ar(13440, 528).rearrange("p (t k) -> p t k", t=T)
        aT1 = ar(13968, 256).rearrange("p (r n) -> p r n", r=2)
        Pie1 = ar(14224, 128).rearrange("p (r j h) -> p r j h", r=2, j=J)
        PiT1 = ar(14352, 256).rearrange("p (r n) -> p r n", r=2)
        Xr = ar(14608, 512).rearrange("p (j o n) -> p j o n", j=J, o=4)
        mx1 = small(2 * H1).rearrange("p (r h) -> p r h", r=2)
        sm1 = small(H1)
        rs1 = small(H1)
        vie = br(0, 1024).rearrange("p (b h) -> p b h", h=H1)
        Z2s = AR[0:64, AREA_A + 1024:AREA_A + 3072].rearrange("p (h c) -> p h c", h=H3)

        pre = [br(1120 * i, 1120).rearrange("p (b l) -> p b l", b=NB // 2) for i in range(3)]
        qkv = [br(3360 + NH * i, NH) for i in range(3)]
        qkv3 = [x.rearrange("p (b l) -> p b l", b=NB // 2) for x in qkv]
        sqr = [br(0, NH), br(NH, NH)]
        g1T = br(0, 2 * NH).rearrange("p (m n) -> p m n", m=2)
        fl = br(2240, NH).rearrange("p (b l) -> p b l", b=NB // 2)
        O = br(3360, NH).rearrange("p (t h c) -> p t h c", t=TH, h=H2)
        OS = br(4384, NH).rearrange("p (t h c) -> p t h c", t=TH, h=H2)
        OT = br(5408, NH)
        VB = br(6432, NH).rearrange("p (h t c) -> p h t c", h=H2, t=TH)
        PN = br(6432, NH).rearrange("p (i k) -> p i k", i=L)
        U = br(7456, NH).rearrange("p (i c) -> p i c", i=L)
        prod = [br(8480 + NH * i, NH).rearrange("p (b l) -> p b l", b=NB // 2) for i in range(2)]
        DV = br(8480, 3 * NH).rearrange("p (t r c) -> p t r c", t=TH, r=3)
        DD = br(2240, NH).rearrange("p (t h c) -> p t h c", t=TH, h=H2)
        fs = br(10528, NH).rearrange("p (b l) -> p b l", b=NB // 2)
        GN = br(11552, 2048).rearrange("p (h t n) -> p h t n", h=H2, t=TH)
        tmpU = br(11552, 31 * L).rearrange("p (i c) -> p i c", i=31)
        UT = br(12576, NH).rearrange("p (h t c) -> p h t c", h=H2, t=TH)
        GA = br(13600, 2048).rearrange("p (h t n) -> p h t n", h=H2, t=TH)
        BR = br(15648, 4096).rearrange("p (t r h c) -> p t r h c", t=TH, r=4, h=H2)
        beta, nk, nq, cf1, cf2 = (small(TH * H2).rearrange("p (h t) -> p h t", h=H2) for _ in range(5))
        gate, mu, sd, bmx = (small(TH * 16).rearrange("p (t r h) -> p t r h", t=TH, r=4) for _ in range(4))
        lmx, oms = (small(TH * 4).rearrange("p (t h) -> p t h", t=TH) for _ in range(2))

        qs = ar(0, 1024).rearrange("p (c n) -> p c n", c=C3)
        kpl = ar(1024, 1024).rearrange("p (c n) -> p c n", c=C3)
        kx3 = ar(2048, 2176).rearrange("p (c j h k) -> p c j h k", c=C3, j=J, h=2)
        kt3 = ar(4224, 1024)
        Sc = ar(5248, 544).rearrange("p (h k) -> p h k", h=H3)
        P3 = ar(5792, 544).rearrange("p (h k) -> p h k", h=H3)
        Pn3 = ar(6336, 512)
        PTc = ar(6848, 512)
        PTd = ar(7360, 1024).rearrange("p (h i q) -> p h i q", h=H3, i=2)
        aT3 = ar(8384, 1024).rearrange("p (c n) -> p c n", c=C3)
        Pie3 = ar(9408, 64).rearrange("p (j h) -> p j h", j=J)
        PiT3 = AR[0:64, 9472:9600]
        YT = ar(9600, 128)
        EZ = ar(12304, SP * (D + 1)).rearrange("p (a c) -> p a c", a=SP)
        Y = ar(10240, T * (D + 1)).rearrange("p (t c) -> p t c", t=T)
        FW = br(0, 8192).rearrange("p (e s n) -> p e s n", e=E, s=2)
        mx3, sm3, rs3 = small(H3), small(H3), small(H3)

        LG = small(T * E).rearrange("p (t e) -> p t e", t=T)
        lm = small(T)
        OH = small(2 * T * E).rearrange("p (s t e) -> p s t e", s=2, t=T)
        tq = small(T * E).rearrange("p (t e) -> p t e", t=T)
        tv = small(2 * T).rearrange("p (s t) -> p s t", s=2)
        tk = small(2 * T).rearrange("p (s t) -> p s t", s=2)
        vl = small(2 * T).rearrange("p (s t) -> p s t", s=2)
        tot = small(2 * T * E)
        run_ = small(2 * T * E)
        pos = small(2 * T * E).rearrange("p (s t e) -> p s t e", s=2, t=T)
        pown, keep, slot, sidx, gidx = (small(2 * T) for _ in range(5))
        sI, gI = (small(2 * T).bitcast(i32) for _ in range(2))
        XG = ar(0, 6 * (D + 1)).rearrange("p (r s c) -> p r s c", r=2, s=3)
        XGT = ar(776, 2 * CAP).rearrange("p (r n) -> p r n", r=2)
        GH = ar(776 + 2 * CAP, 2 * HC * CAP).rearrange("p (r m n) -> p r m n", r=2, m=HC)
        YE = ar(776 + 10 * CAP, 2 * CAP).rearrange("p (r n) -> p r n", r=2)
        YO = ar(776 + 12 * CAP, 768).rearrange("p (r s c) -> p r s c", r=2, s=3)
        X1 = br(8192, N).rearrange("p (t c) -> p t c", t=T)
        YG = br(10240, 2 * N).rearrange("p (s t c) -> p s t c", s=2, t=T)
        RO = br(14336, N).rearrange("p (t c) -> p t c", t=T)
        RPARTS = [(0, P), (P, 2 * P), (2 * P, CAP)]

        s_w, s_wb, s_c, s_am = sem("weights_in"), sem("more_weights_in"), sem("consts_in"), sem("mask_in")
        s_x = [sem(f"x{c}_in") for c in range(CH)]
        s_img, s_imgsb = sem("img_ps"), sem("img_sb")
        s_qp, s_kp, s_qsw, s_ksw = sem("q_ps"), sem("k_ps"), sem("q_swz"), sem("k_swz")
        s_zero, s_k00 = sem("zeroed"), sem("k_img_slot")
        s_vie, s_z1p, s_z1 = sem("vie"), sem("z1_ps"), sem("z1_sb")
        s_ak, s_ak3, s_z2p, s_z2s, s_z2d, s_z2 = sem("ak_ps"), sem("ak_sb"), sem("z2_ps"), sem("z2_sb"), sem("z2_dram"), sem("z2_in")
        s_mk = sem("mask_sum")
        a_kx, a_s, a_s1, a_mx, a_s3, a_p, a_pn, a_xr = (sem(f"a_{n}") for n in ("kx", "s", "s1", "mx", "s3", "p", "pn", "xr"))
        a_pie, a_t, a_pt, a_v, a_vt, a_vx, a_pv, a_at, a_h, a_hs = (
            sem(f"a_{n}") for n in ("pie", "t", "pt", "v", "vt", "vx", "pv", "at", "h", "hs"))
        ch_v, ch_a = sem("dve_chain"), sem("act_chain")
        b_full, b_free = [sem(f"b_full{i}") for i in range(2)], [sem(f"b_free{i}") for i in range(2)]
        (b_pad, b_cv, b_silu, b_qm, b_qa, b_sq, b_coef, b_vb, b_gsc, b_vd, b_u0, b_nd, b_pn, b_solved, b_ud,
         b_fm, b_fa, b_fl, b_st, b_dev, b_dd, b_ddsq, b_dsq, b_std, b_stds, b_ee, b_exp, b_wts, b_mixp, b_mix, b_osq, b_ors, b_on,
         b_utm) = (sem(f"b_{n}") for n in (
             "pad cv silu qm qa sq coef vb gsc vd u0 nd pn solved ud fm fa fl st dev dd ddsq dsq std stds ee exp wts "
             "mixp mix osq ors on utm").split())
        (c_q, c_qs, c_k, c_ks, c_kx, c_t, c_ts, c_s, c_s1, c_mx, c_s3, c_p, c_pn, c_ptc, c_pie, c_ptd, c_pit, c_pits, c_pv, c_at,
         c_y, c_ys, c_yt, c_ytm, c_lg, c_zero) = (sem(f"c_{n}") for n in (
             "q qs k ks kx t ts s s1 mx s3 p pn ptc pie ptd pit pits pv at y ys yt ytm lg zero").split())
        (d_ex, d_exps, d_oh, d_cum, d_slot, d_sc, d_xt, d_xts, d_f1, d_f1s, d_f2, d_ye, d_yt, d_yts, d_x1t, d_x1s, d_out, d_fin,
         d_xz, d_fw, d_zt, d_yz, d_di) = (sem(f"d_{n}") for n in (
             "ex exps oh cum slot sc xt xts f1 f1s f2 ye yt yts x1t x1s out fin xz fw zt yz di").split())
        d_xg, d_yd = [sem(f"d_xg{r}") for r in range(2)], [sem(f"d_yd{r}") for r in range(2)]
        d_ga = [sem(f"d_ga{c}") for c in range(CH)]
        block = ctx.enter_context(nc.Block())

        USES = []
        for half in range(2):
            USES += [(half, n, c) for n in "vkq" for c in range(2)] + [(half, n, 0) for n in ("vt0", "vt1", "beta", "nk", "nq")]
            USES += [(half, "gn", h) for h in range(H2)] + [(half, "ga", h) for h in range(H2)]
            USES += [(half, "g1", n) for n in range(4)] + [(half, "g2", 0)] + [(half, n, c) for n in ("fs", "fl") for c in range(2)]
            USES += [(half, "o", n) for n in range(4)] + [(half, "ot", c) for c in range(2)] + [(half, "op", c) for c in range(2)]

        def use(half, name, n=0):
            i = USES.index((half, name, n))
            return 6 + i % 2, b_full[i % 2], b_free[i % 2], i // 2 + 1

        def await_full(eng, *u):
            b, full, _, n = use(*u)
            eng.wait_ge(full, n)
            return b

        def await_freed(eng, *u):
            _, _, free, n = use(*u)
            eng.wait_ge(free, n)

        def freed(ins, *u):
            ins.then_inc(use(*u)[2], 1)

        @block.sync
        def _(sp):
            sp.dma_start(W[:, 0:wo["qpT"][0]], w[:, 0:wo["qpT"][0]]).then_inc(s_w, 16)
            for c in range(2):
                sp.dma_start(XT[:, c * NC:(c + 1) * NC], xT[:, c * NC:(c + 1) * NC]).then_inc(s_x[c], 16)
            sp.dma_start(Cn[:, :], cst).then_inc(s_c, 16)
            sp.dma_start(W[:, wo["qpT"][0]:WW], w[:, wo["qpT"][0]:WW]).then_inc(s_wb, 16)
            for c in range(2, CH):
                sp.dma_start(XT[:, c * NC:(c + 1) * NC], xT[:, c * NC:(c + 1) * NC]).then_inc(s_x[c], 16)
            sp.wait_ge(s_z2s, 2)
            sp.dma_start(zscr.rearrange("b h c -> b (h c)"), AR[0:64, AREA_A + 1024:AREA_A + 3072]).then_inc(s_z2d, 16)
            sp.wait_ge(s_z2d, 16)
            sp.dma_start(Z2[:, :].rearrange("p (t c) -> p t c", t=T),
                         zscr.rearrange("(t j) h c -> (j h) t c", j=J)).then_inc(s_z2, 16)

            def pairs(half):
                sp.wait_ge(b_vb, half + 1)
                sp.dma_start(vscr[half], br(6432, NH)).then_inc(b_vd, 16)
                sp.wait_ge(b_vd, 16 * (half + 1))
                for j in range(J):
                    sp.dma_start(U[32 * j:32 * j + 32, :, :], vscr[half].rearrange("(j i) (p c) -> j p i c", j=J, c=D2)[j]).then_inc(b_u0, 16)
                sp.wait_ge(b_gsc, H2 * (half + 1))
                for j in range(J):
                    sp.dma_start(nscr[half].rearrange("(j i) (p k) -> j i p k", j=J, k=L)[j],
                                 GN[32 * j:32 * j + 32, :, :, 32 * (j % 2):32 * (j % 2) + 32].rearrange("i h t k -> i (h t) k")).then_inc(b_nd, 16)
                sp.wait_ge(b_nd, 16 * J * (half + 1))
                for j in range(J):
                    sp.dma_start(PN[32 * j:32 * j + 32, :, :], nscr[half].rearrange("(j i) (p k) -> j p i k", j=J, k=L)[j]).then_inc(b_pn, 16)
                sp.wait_ge(b_solved, half + 1)
                for j in range(J):
                    sp.dma_start(uscr[half].rearrange("(j i) (p c) -> j p i c", j=J, c=D2)[j], U[32 * j:32 * j + 32, :, :]).then_inc(b_ud, 16)
                sp.wait_ge(b_ud, 16 * J * (half + 1))
                sp.dma_start(br(12576, NH), uscr[half]).then_inc(b_utm, 16)

            pairs(0)
            pairs(1)
            for c in range(2):
                await_freed(sp, 1, "op", c)
            sp.dma_start(FW[:, :, 0, :], fc1).then_inc(d_fw, 16)
            sp.dma_start(FW[:, :, 1, :], fc2).then_inc(d_fw, 16)
            sp.wait_ge(d_zt, 2)
            full = SLOTS // P * P
            sp.dma_start(xscr[0:full, :].rearrange("(a p) c -> p a c", p=P), EZ[:, 0:full // P, :]).then_inc(d_xz, 16)
            sp.dma_start(xscr[full:SLOTS, :], EZ[0:SLOTS - full, full // P, :]).then_inc(d_xz, 16)
            for a in range(0, 2 * N, 4 * P):
                sp.dma_start(yscr[a:a + 4 * P, :].rearrange("(a p) c -> p a c", p=P), EZ[:, 0:4, 0:D]).then_inc(d_yz, 16)
            sp.wait_ge(d_sc, 16 * 2 * T)
            for e in range(E):
                if e >= 2:
                    sp.wait_ge(d_di, e - 1)
                for s, (a, b) in enumerate(RPARTS):
                    sp.dma_start(XG[0:b - a, e % 2, s, :], xscr[e * CAP + a:e * CAP + b, :]).then_inc(d_xg[e % 2], 16)
            for r in range(2):
                sp.wait_ge(d_yd[r], 16 * 3 * E // 2)
            for c in range(CH):
                for s in range(2):
                    sp.dma_start(YG[:, s, 4 * c:4 * c + 4, :], yscr[s * N + c * NC:s * N + (c + 1) * NC, :].rearrange("(t p) c -> p t c", p=P)).then_inc(d_ga[c], 16)
            for c in range(CH):
                sp.wait_ge(d_fin, 4 * c + 4)
                sp.dma_start(out[c * NC:(c + 1) * NC, :].rearrange("(t p) c -> p t c", p=P), RO[:, 4 * c:4 * c + 4, :]).then_inc(d_out, 16)
            sp.wait_ge(d_out, 16 * CH)

        @block.gpsimd
        def _(pool):
            mv = mask.rearrange("(t j) k -> j t k", j=J)
            pool.memset(Mk[:, :, :], 0.0).then_inc(s_mk, 1)
            pool.memset(Qd, 0.0).then_inc(s_zero, 1)
            pool.wait_ge(s_mk, 1)
            for j in range(J):
                pool.dma_start(Mk[32 * j:32 * j + 32, :, 1:K1], mv[j:j + 1].broadcast_to([32, T, L])).then_inc(s_am, 16)
            pool.wait_ge(s_c, 16)
            pool.wait_ge(s_imgsb, 2)
            pool.tensor_tensor(vie, vimg[:, :].rearrange("p (b o) -> p b o", o=1).broadcast_to([P, NB, H1]),
                               cs("hm16").rearrange("p (o h) -> p o h", o=1).broadcast_to([P, NB, H1]), ALU.mult).then_inc(s_vie, 1)
            pool.wait_ge(s_am, 16 * J)
            pool.tensor_tensor(Mk[:, :, :], Mk[:, :, :], cs("nonc").rearrange("p (o k) -> p o k", o=1).broadcast_to([P, T, K1]), ALU.add).then_inc(s_mk, 1)
            hm4 = cs("hm4").rearrange("p (o h u) -> p o h u", o=1, u=1).broadcast_to([P, G1, 4, K1])

            def expand(t):
                if t % 4 == 0:
                    pool.wait_ge(s_k00, 16 * (t // 4 + 1))
                    pool.wait_ge(s_ksw, 16 * (t // 4 + 1))
                if t >= 2:
                    pool.wait_ge(a_s, t - 1)
                pool.tensor_tensor(Kx[:, t % 2], K0[:, :, t % TH, :].rearrange("p g (o k) -> p g o k", o=1).broadcast_to([P, G1, 4, K1]),
                                   hm4, ALU.mult).then_inc(a_kx, 1)

            def repeat(t):
                pool.wait_ge(s_x[t // 4], 16)
                if t >= 1:
                    pool.wait_ge(a_v, t)
                pool.tensor_copy(Xr, XT[:, t * P:(t + 1) * P].rearrange("p (j o n) -> p j o n", j=J, o=1).broadcast_to([P, J, 4, L])).then_inc(a_xr, 1)

            def shift(t):
                pool.wait_ge(a_mx, t + 1)
                pool.tensor_tensor(S2[:, t % 2], S2[:, t % 2], mx1[:, t % 2].rearrange("p (h o) -> p h o", o=1).broadcast_to([P, H1, K1]),
                                   ALU.subtract).then_inc(a_s3, 1)

            def values(t):
                pool.wait_ge(a_vt, t + 1)
                if t >= 2:
                    pool.wait_ge(a_pv, t - 1)
                pool.tensor_tensor(Vx1[:, t % 2], Vt1, cs("hmv").rearrange("p (o c) -> p o c", o=1).broadcast_to([P, J, P]),
                                   ALU.mult).then_inc(a_vx, 1)

            def tile1(t, pieces=()):
                if t < T:
                    expand(t)
                    repeat(t)
                if 1 <= t <= T:
                    shift(t - 1)
                    values(t - 1)
                for piece in pieces:
                    piece(0)

            def q_sum(half):
                for i in range(1, 4):
                    pool.wait_ge(b_qm, 4 * half + i + 1)
                    if i > 1:
                        pool.wait_ge(b_qa, 3 * half + i - 1)
                    pool.tensor_tensor(qkv3[0], qkv3[0], prod[i % 2], ALU.add).then_inc(b_qa, 1)

            def v_scaled(half):
                pool.wait_ge(b_coef, half + 1)
                for c in range(2):
                    await_freed(pool, half, f"vt{c}")
                if half:
                    pool.wait_ge(b_solved, 1)
                pool.tensor_tensor(VB, BR[:, :, 2].rearrange("p t h c -> p h t c"),
                                   cf1.rearrange("p h (t o) -> p h t o", o=1).broadcast_to([P, H2, TH, D2]), ALU.mult).then_inc(b_vb, 1)

            def couplings(half):
                for h in range(H2):
                    await_freed(pool, half, "gn", h)
                    pool.tensor_tensor(GN[:, h], GN[:, h], cf2[:, h].rearrange("p (t o) -> p t o", o=1).broadcast_to([P, TH, 64]), ALU.mult).then_inc(b_gsc, 1)

            def short_sum(half, a, b):
                for lag in range(a, b):
                    pool.wait_ge(b_fm, 7 * half + lag + 1)
                    if lag > 1:
                        pool.wait_ge(b_fa, 6 * half + lag - 1)
                    pool.tensor_tensor(fs[:, :, lag:L], fs[:, :, lag:L], prod[lag % 2][:, :, 0:L - lag], ALU.add).then_inc(b_fa, 1)

            def deviations(half):
                pool.wait_ge(b_st, half + 1)
                for t in range(TH):
                    pool.tensor_tensor(DV[:, t].rearrange("p r (h c) -> p (r h) c", h=H2), BR[:, t, 0:3].rearrange("p r h c -> p (r h) c"),
                                       mu[:, t, 0:3].rearrange("p r (h o) -> p (r h) o", o=1).broadcast_to([P, 12, D2]), ALU.subtract).then_inc(b_dev, 1)

            def mix(half):
                pool.wait_ge(b_wts, half + 1)
                for g in range(2):
                    v = BR[:, 4 * g:4 * g + 4, 0:1]
                    pool.tensor_tensor(v.rearrange("p t r h c -> p t (r h) c"), v.rearrange("p t r h c -> p t (r h) c"),
                                       gate[:, 4 * g:4 * g + 4, 0:1].rearrange("p t r (h o) -> p t (r h) o", o=1).broadcast_to([P, 4, H2, D2]), ALU.mult).then_inc(b_mixp, 1)

            def zero3():
                pool.wait_ge(a_h, T)
                pool.wait_ge(a_s, T)
                pool.memset(kx3, 0.0).then_inc(c_zero, 1)
                pool.memset(EZ[:, :, 0:D], 0.0).then_inc(d_zt, 1)
                pool.tensor_copy(EZ[:, :, D], cs("empty")).then_inc(d_zt, 1)
                pool.tensor_copy(Y[:, :, D], cs("tok")).then_inc(c_zero, 1)

            def shift3(t):
                pool.wait_ge(c_mx, t + 1)
                pool.tensor_tensor(Sc, Sc, mx3.rearrange("p (h o) -> p h o", o=1).broadcast_to([P, H3, K3]), ALU.subtract).then_inc(c_s3, 1)

            def diag3(t):
                pool.wait_ge(c_ptc, t + 1)
                if t >= 1:
                    pool.wait_ge(c_pv, t)
                pool.tensor_tensor(PTd, PTc.rearrange("p (h o q) -> p h o q", h=H3, o=1).broadcast_to([P, H3, 2, L]),
                                   cs("jm2").rearrange("p (o i u) -> p o i u", o=1, u=1).broadcast_to([P, H3, 2, L]), ALU.mult).then_inc(c_ptd, 1)

            def tile3(t, pieces=()):
                if t >= 1:
                    diag3(t - 1)
                if t < T:
                    shift3(t)
                for piece in pieces:
                    piece(1)

            for t in range(TH + 2):
                tile1(t)
            PIECES = ((), (q_sum,), (lambda h: short_sum(h, 1, 3),), (v_scaled, couplings, lambda h: short_sum(h, 3, 5)),
                      (lambda h: short_sum(h, 5, 7),), (), (), (deviations,))
            for piece in PIECES[0]:
                piece(0)
            for i in range(1, TH):
                tile1(TH + 1 + i, PIECES[i])
            mix(0)
            zero3()
            for t in range(TH):
                tile3(t, PIECES[t])
            mix(1)
            for t in range(TH, T + 1):
                tile3(t)
            pool.wait_ge(d_slot, 1)
            pool.wait_ge(d_xz, 16 * 2)
            pool.wait_ge(c_zero, 2)
            pool.wait_ge(c_ytm, T)
            for s in range(2):
                for t in range(T):
                    pool.indirect_dma_start(out=xscr, out_offset=bass.IndirectOffsetOnAxis(ap=sI[:, s * T + t:s * T + t + 1], axis=0),
                                            in_=Y[:, t, :], in_offset=None).then_inc(d_sc, 16)
            pool.wait_ge(d_yz, 16 * 8)
            for e in range(E):
                pool.wait_ge(d_di, e + 1)
                pool.wait_ge(d_yts, e + 1)
                for s, (a, b) in enumerate(RPARTS):
                    pool.indirect_dma_start(out=yscr, out_offset=bass.IndirectOffsetOnAxis(ap=gI[0:b - a, 3 * e + s:3 * e + s + 1], axis=0),
                                            in_=YO[0:b - a, e % 2, s, :], in_offset=None).then_inc(d_yd[e % 2], 16)

        @block.tensor
        def _(pe):
            mm = pe.matmul

            def q_proj(n):
                pe.wait_ge(s_x[n], 16)
                mm(bank(n if n < 2 else 6), wt("wqkv", 0, D), XT[:, n * NC:(n + 1) * NC], start=True, stop=True).then_inc(s_qp, 1)

            def k_proj(n):
                mm(bank(2 + n if n < 2 else 7), wt("wqkv", D, 2 * D), XT[:, n * NC:(n + 1) * NC], start=True, stop=True).then_inc(s_kp, 1)

            pe.wait_ge(s_w, 16)
            mm(bank(4, NB), wt("ukT"), wt("condT"), start=True, stop=True)
            mm(bank(4, NB, NB), wt("uvT"), wt("condT"), start=True, stop=True).then_inc(s_img, 1)
            for n in range(2):
                q_proj(n)
                k_proj(n)
            pe.wait_ge(s_vie, 1)
            for t in range(T):
                if t % 4 == 0 and t >= 8:
                    pe.wait_ge(s_z1, t // 4 - 1)
                ins = mm(PS[0:64, 6 + (t // 4) % 2, (t % 4) * P:(t % 4 + 1) * P], vie[:, J * t:J * t + J, :], wt("cproj"), start=True, stop=True)
                if t % 4 == 3:
                    ins.then_inc(s_z1p, 1)

            def image_values():
                pe.wait_ge(s_wb, 16)
                pe.wait_ge(s_z1, 4)
                for i, name in enumerate(("wk3", "wv3")):
                    for c in range(C3):
                        ins = mm(bank(6 + i, NB, NB * c), wt(name, c * P, (c + 1) * P), wt("condT"), start=True, stop=True)
                ins.then_inc(s_ak, 1)

            def image_output(r):
                pe.wait_ge(s_ak3, 2)
                if r:
                    pe.wait_ge(s_z2s, 1)
                for i in range(8):
                    h = 8 * r + i
                    o = 64 * (h % 2)
                    ins = mm(PS[0:64, 6 + (h % 2), (i // 2) * P:(i // 2 + 1) * P], av3[o:o + 64, (h // 2) * NB:(h // 2 + 1) * NB],
                             wt("wo3", (h // 2) * P, (h // 2 + 1) * P)[o:o + 64], start=True, stop=True)
                ins.then_inc(s_z2p, 1)

            def scores(t):
                pe.wait_ge(a_kx, t + 1)
                pe.wait_ge(s_qsw, 16 * (t // 4 + 1))
                if t == 0:
                    pe.wait_ge(s_qsw, 32)
                else:
                    pe.wait_ge(a_s1, 2 * t)
                for g in range(G1):
                    ins = mm(PS[:, g // 2, (g % 2) * 132:(g % 2 + 1) * 132], Qd[:, g, (t % TH) * P:(t % TH + 1) * P],
                             Kx[:, t % 2, g].rearrange("p h k -> p (h k)"), start=True, stop=True)
                ins.then_inc(a_s, 1)

            def v_rows(t):
                pe.wait_ge(a_xr, t + 1)
                if t >= 1:
                    pe.wait_ge(a_vt, t)
                if t == 0:
                    pe.wait_ge(s_ksw, 32)
                for j in range(J):
                    ins = mm(PS[:, 3, j * P:(j + 1) * P], Xr[:, j].rearrange("p o n -> p (o n)"),
                             wt("wqkv", 2 * D, 3 * D), start=True, stop=True)
                ins.then_inc(a_v, 1)

            def turn(t):
                pe.wait_ge(a_pn, t + 1)
                pe.wait_ge(a_pie, t + 1)
                if t >= 1:
                    pe.wait_ge(a_pt, 2 * t)
                    pe.wait_ge(a_hs, t)
                for g in range(G1):
                    pe.transpose(PS[:, 2, g * P:(g + 1) * P], Pn1[:, g * P:(g + 1) * P], ident)
                pe.transpose(PS[0:64, 4, 0:P], Pie1[:, t % 2].rearrange("p j h -> p (j h)"), ident).then_inc(a_t, 1)

            def weigh(t):
                pe.wait_ge(a_pt, 2 * t + 2)
                pe.wait_ge(a_vx, t + 1)
                if t >= 1:
                    pe.wait_ge(a_at, t)
                for j in range(J):
                    for g in range(G1):
                        ins = mm(PS[32 * g:32 * g + 32, 5, 32 * j:32 * j + 32], Vx1[:, t % 2, j, 32 * g:32 * g + 32],
                                 PT1[:, t % 2, g, 32 * j:32 * j + 32], start=True, stop=True)
                ins.then_inc(a_pv, 1)

            def project(t):
                pe.wait_ge(a_at, t + 1)
                mm(PS[:, 4, P:2 * P], Z1[:, t, :], PiT1[0:64, t % 2], start=True, stop=False)
                mm(PS[:, 4, P:2 * P], wt("cproj"), aT1[:, t % 2], start=False, stop=True).then_inc(a_h, 1)

            def tile1(t, pieces=()):
                if t < T:
                    if t in (5, 8):
                        n = 2 if t == 5 else 3
                        if n == 2:
                            pe.wait_ge(s_z2s, 2)
                        else:
                            pe.wait_ge(s_qsw, 48)
                            pe.wait_ge(s_ksw, 48)
                        q_proj(n)
                        k_proj(n)
                    scores(t)
                    v_rows(t)
                for piece in pieces:
                    piece(0)
                if t >= 2:
                    weigh(t - 2)
                    project(t - 2)
                if 1 <= t <= T:
                    turn(t - 1)

            def take(half, name, n=0):
                b, _, free, count = use(half, name, n)
                if count > 1:
                    pe.wait_ge(free, count - 1)
                return b

            def filled(ins, half, name, n=0):
                ins.then_inc(use(half, name, n)[1], 1)

            def proj(half):
                if half == 0:
                    pe.wait_ge(s_qsw, 64)
                    pe.wait_ge(s_ksw, 64)
                for i, name in ((2, "v"), (1, "k"), (0, "q")):
                    for c in range(2):
                        n = 2 * half + c
                        pe.wait_ge(a_hs, 4 * n + 4)
                        b = take(half, name, c)
                        filled(mm(bank(b), wt(name + "pT"), hT[:, n * NC:(n + 1) * NC], start=True, stop=True), half, name, c)

            def v_turn(half):
                pe.wait_ge(b_silu, 3 * half + 1)
                for c in range(2):
                    b = take(half, f"vt{c}")
                    for i in range(4):
                        t = 4 * c + i
                        ins = pe.transpose(bank(b, P, i * P), qkv[2][:, t * P:(t + 1) * P], ident)
                    filled(ins, half, f"vt{c}")
                b = take(half, "beta")
                for t in range(TH):
                    n = TH * half + t
                    ins = mm(bank(b, H2, H2 * t), hT[:, n * P:(n + 1) * P], wt("bpT"), start=True, stop=True)
                filled(ins, half, "beta")

            def norms(half):
                for i, name in ((1, "nk"), (0, "nq")):
                    pe.wait_ge(b_sq, 2 * half + 2 - i)
                    b = take(half, name)
                    for t in range(TH):
                        ins = mm(bank(b, H2, H2 * t), sqr[i][:, t * P:(t + 1) * P], cs("hm2"), start=True, stop=True)
                    filled(ins, half, name)

            def gram(half, name, lhs, rhs):
                for h in range(H2):
                    b = take(half, name, h)
                    for t in range(TH):
                        for f in range(2):
                            c0 = t * P + 64 * f
                            ins = mm(PS[64 * f:64 * f + 64, b, 64 * t:64 * t + 64], lhs[32 * h:32 * h + 32, c0:c0 + 64],
                                     rhs[32 * h:32 * h + 32, c0:c0 + 64], start=True, stop=True)
                    filled(ins, half, name, h)

            def couplings(half):
                pe.wait_ge(b_silu, 3 * half + 3)
                gram(half, "gn", qkv[1], qkv[1])

            def readings(half):
                gram(half, "ga", qkv[1], qkv[0])

            def gates(half):
                for n in range(4):
                    m, c = n // 2, n % 2
                    b = take(half, "g1", n)
                    filled(mm(bank(b), wt("gw1T", m * P, (m + 1) * P), hT[:, (2 * half + c) * NC:(2 * half + c + 1) * NC], start=True, stop=True), half, "g1", n)
                for n in (2, 3):
                    await_freed(pe, half, "g1", n)
                b = take(half, "g2")
                for t in range(TH):
                    for m in range(2):
                        ins = mm(bank(b, H1, H1 * t), g1T[:, m, t * P:(t + 1) * P], wt("gw2T", m * H1, (m + 1) * H1), start=(m == 0), stop=(m == 1))
                filled(ins, half, "g2")

            def filters_turn(half):
                for name, x, done, n in (("fs", fs, b_fa, 6 * half + 6), ("fl", fl, b_fl, half + 1)):
                    pe.wait_ge(done, n)
                    for c in range(2):
                        b = take(half, name, c)
                        for i in range(4):
                            t = 4 * c + i
                            ins = pe.transpose(bank(b, P, i * P), x[:, J * t:J * t + J, :].rearrange("p b l -> p (b l)"), ident)
                        filled(ins, half, name, c)

            def read_out(half):
                pe.wait_ge(b_utm, 16 * (half + 1))
                for n in range(4):
                    c, f = n // 2, n % 2
                    b = take(half, "o", n)
                    for i in range(4):
                        for h in range(H2):
                            ins = mm(PS[64 * f:64 * f + 64, b, i * P + 32 * h:i * P + 32 * h + 32], GA[64 * f:64 * f + 64, h, 4 * c + i, :],
                                     UT[64 * f:64 * f + 64, h, 4 * c + i, :], start=True, stop=True)
                    filled(ins, half, "o", n)

            def out_proj(half):
                for c in range(2):
                    pe.wait_ge(b_on, 2 * half + c + 1)
                    b = take(half, "ot", c)
                    for i in range(4):
                        ins = pe.transpose(bank(b, P, i * P), O[:, 4 * c + i].rearrange("p h c -> p (h c)"), ident)
                    filled(ins, half, "ot", c)
                for c in range(2):
                    await_freed(pe, half, "ot", c)
                    b = take(half, "op", c)
                    filled(mm(bank(b), wt("opT"), OT[:, c * NC:(c + 1) * NC], start=True, stop=True), half, "op", c)

            def proj3(t, name, done):
                x = XT[:, t * P:(t + 1) * P]
                for c in range(C3):
                    if name == "wk3" and c % 4 == 0:
                        pe.wait_ge(c_qs, 2 * t + 1 + c // 4)
                    ins = mm(PS[:, c // 4, (c % 4) * P:(c % 4 + 1) * P], wt(name, c * P, (c + 1) * P), x, start=True, stop=True)
                    if c % 4 == 3:
                        ins.then_inc(done, 1)

            def image3(t):
                pe.wait_ge(c_pie, t + 1)
                if t >= 1:
                    pe.wait_ge(c_ys, t)
                pe.transpose(PS[0:64, 4, 0:P], Pie3.rearrange("p j h -> p (j h)"), ident).then_inc(c_pit, 1)

            def weigh3(t):
                pe.wait_ge(c_ptd, t + 1)
                pe.wait_ge(c_ts, 2 * t + 2)
                pe.wait_ge(c_pits, t + 1)
                if t >= 1:
                    pe.wait_ge(c_ytm, t)
                    pe.wait_ge(c_lg, t)
                for f in range(2):
                    for h in range(H3):
                        o = 64 * (h % 2)
                        ins = mm(PS[o:o + 64, 4 + f, (h // 2) * 64:(h // 2 + 1) * 64], kt3[64 * f:64 * f + 64, 64 * h:64 * h + 64],
                                 PTd[64 * f:64 * f + 64, h].rearrange("p i q -> p (i q)"), start=True, stop=True)
                ins.then_inc(c_pv, 1)

            def keys3(t):
                pe.wait_ge(c_ks, 2 * t + 2)
                for c in range(C3):
                    ins = pe.transpose(PS[:, c // 4, (c % 4) * P:(c % 4 + 1) * P], kpl[:, c, :], ident)
                ins.then_inc(c_t, 1)

            def scores3(t):
                pe.wait_ge(c_kx, t + 1)
                if t >= 1:
                    pe.wait_ge(c_s1, 2 * t)
                for j in range(J):
                    for c in range(C3):
                        ins = mm(PS[32 * j:32 * j + 32, 2 + c // 4, (c % 4) * 68:(c % 4 + 1) * 68], qs[:, c, 32 * j:32 * j + 32],
                                 kx3[:, c, j].rearrange("p h k -> p (h k)"), start=True, stop=True)
                ins.then_inc(c_s, 1)

            def output3(t):
                pe.wait_ge(c_at, 2 * t + 2)
                mm(bank(4, P), Z2[:, t * P:(t + 1) * P], PiT3, start=True, stop=False)
                for c in range(C3):
                    ins = mm(bank(4, P), wt("wo3", c * P, (c + 1) * P), aT3[:, c, :], start=False, stop=(c == C3 - 1))
                ins.then_inc(c_y, 1)

            def turn3(t):
                pe.wait_ge(c_ys, t + 1)
                pe.transpose(bank(5, P), YT, ident)
                mm(bank(5, E, P), YT, wt("rwT"), start=True, stop=True).then_inc(c_yt, 1)

            def tile3(t, pieces=()):
                if t < T:
                    if t % (T // CH) == 0:
                        await_freed(pe, t // TH, "op", t // 4 % 2)
                    if t >= 1:
                        pe.wait_ge(c_ts, 2 * t)
                    proj3(t, "wq3", c_q)
                    proj3(t, "wk3", c_k)
                if t >= 1:
                    image3(t - 1)
                    weigh3(t - 1)
                if t < T:
                    keys3(t)
                    scores3(t)
                for piece in pieces:
                    piece(1)
                if t >= 1:
                    output3(t - 1)
                    turn3(t - 1)

            image_values()
            for t in range(TH):
                tile1(t)
                if t in (1, 3):
                    image_output(t // 2)
            PIECES = ((proj,), (v_turn,), (norms,), (couplings,), (readings,), (gates, filters_turn), (), (read_out,))
            for t in range(TH, TH + 2):
                tile1(t)
            for piece in PIECES[0]:
                piece(0)
            for i in range(1, TH):
                tile1(TH + 1 + i, PIECES[i])
            tile1(T + 1)
            out_proj(0)
            pe.wait_ge(s_z2, 16)
            for t in range(TH):
                tile3(t, PIECES[t])
            out_proj(1)
            for t in range(TH, T + 1):
                tile3(t)

            pe.wait_ge(d_oh, 1)
            ohf = OH[:, :, :, :].rearrange("p s t e -> p (s t e)")
            mm(bank(1, 2 * T * E), cs("before"), ohf, start=True, stop=True)
            mm(bank(2, 2 * T * E), cs("ones"), ohf, start=True, stop=True).then_inc(d_cum, 1)
            for c in range(CH):
                if c >= 1:
                    pe.wait_ge(d_x1s, c)
                for i in range(4):
                    t = 4 * c + i
                    ins = pe.transpose(bank(7, P, i * P), XT[:, t * P:(t + 1) * P], ident)
                ins.then_inc(d_x1t, 1)
            pe.wait_ge(d_slot, 1)
            pe.wait_ge(d_fw, 32)
            def rows_in(e):
                pe.wait_ge(d_xg[e % 2], 16 * 3 * (e // 2 + 1))
                if e:
                    pe.wait_ge(d_xts, e)
                for s, (a, b) in enumerate(RPARTS):
                    ins = pe.transpose(bank(0, b - a, a), XG[0:b - a, e % 2, s, 0:D], cs("ident")[0:b - a, 0:b - a])
                ins.then_inc(d_xt, 1)

            def hidden(e):
                pe.wait_ge(d_xts, e + 1)
                for m in range(HC):
                    if e:
                        pe.wait_ge(d_f1s, HC * (e - 1) + m + 1)
                    mm(bank(1 + m, CAP), FW[:, e, 0, m * P:(m + 1) * P], XGT[:, e % 2], start=True, stop=True).then_inc(d_f1, 1)

            def result(e):
                if e:
                    pe.wait_ge(d_ye, e)
                for m in range(HC):
                    pe.wait_ge(d_f1s, HC * e + m + 1)
                    ins = mm(bank(5, CAP), FW[:, e, 1, m * P:(m + 1) * P], GH[:, e % 2, m], start=(m == 0), stop=(m == HC - 1))
                ins.then_inc(d_f2, 1)

            def rows_out(e):
                pe.wait_ge(d_ye, e + 1)
                if e:
                    pe.wait_ge(d_yts, e)
                for s, (a, b) in enumerate(RPARTS):
                    ins = pe.transpose(PS[0:b - a, 6, s * P:(s + 1) * P], YE[:, e % 2, a:b], ident)
                ins.then_inc(d_yt, 1)

            rows_in(0)
            for e in range(E):
                hidden(e)
                if e < E - 1:
                    rows_in(e + 1)
                if e:
                    rows_out(e - 1)
                result(e)
            rows_out(E - 1)

        @block.scalar
        def _(act):
            A = act.activation
            act.wait_ge(s_w, 16)
            act.wait_ge(s_img, 1)
            A(kimg[:, :], bank(4, NB), ACT.Identity, bias=wt("ukb")).then_inc(s_imgsb, 1)
            A(vimg[:, :], bank(4, NB, NB), ACT.Identity, bias=wt("uvb")).then_inc(s_imgsb, 1)

            def k_swizzle(n):
                act.wait_ge(s_kp, n + 1)
                kps = bank(2 + n if n < 2 else 7).rearrange("p (t j n) -> p t j n", j=J, n=L)
                if n >= 2:
                    act.wait_ge(a_kx, 4 * (n - 1))
                s = 4 * (n % 2)
                for g in range(G1):
                    for j in range(J):
                        A(K0[32 * j:32 * j + 32, g, s:s + 4, 1:K1], kps[32 * g:32 * g + 32, :, j, :], ACT.Identity,
                          bias=wt("bk1")[32 * g:32 * g + 32]).then_inc(s_ksw, 1)

            def softexp(t):
                act.wait_ge(a_s3, t + 1)
                if t >= 2:
                    act.wait_ge(a_pie, t - 1)
                A(P1[:, t % 2].rearrange("p h k -> p (h k)"), S2[:, t % 2].rearrange("p h k -> p (h k)"), ACT.Exp).then_inc(a_p, 1)

            def turned(t):
                act.wait_ge(a_t, t + 1)
                if t >= 2:
                    act.wait_ge(a_pv, t - 1)
                A(PT1[:, t % 2].rearrange("p g n -> p (g n)"), bank(2), ACT.Copy).then_inc(a_pt, 1)
                if t >= 2:
                    act.wait_ge(a_h, t - 1)
                A(PiT1[0:64, t % 2], PS[0:64, 4, 0:P], ACT.Copy).then_inc(a_pt, 1)

            def weighed(t):
                act.wait_ge(a_pv, t + 1)
                A(aT1[:, t % 2], bank(5, P), ACT.Copy).then_inc(a_at, 1)

            def projected(t):
                act.wait_ge(a_h, t + 1)
                A(hT[:, t * P:(t + 1) * P], bank(4, P, P), ACT.Identity, bias=wt("cpb")).then_inc(a_hs, 1)

            def tile1(t, pieces=()):
                if 1 <= t <= T:
                    softexp(t - 1)
                for piece in pieces:
                    piece(0)
                if t >= 2:
                    weighed(t - 2)
                    projected(t - 2)
                if 1 <= t <= T:
                    turned(t - 1)
                if t in (5, 8):
                    k_swizzle(2 if t == 5 else 3)

            def out_of_bank(dst, src, *u, func=ACT.Copy, **kw):
                freed(A(dst, src, func, **kw), *u)

            def inputs(half):
                act.wait_ge(b_pad, half + 1)
                for i, name in ((2, "v"), (1, "k"), (0, "q")):
                    for c in range(2):
                        b = await_full(act, half, name, c)
                        out_of_bank(pre[i][:, 16 * c:16 * c + 16, 3:PADW], bank(b).rearrange("p (b l) -> p b l", l=L), half, name, c)

            def v_rows_out(half):
                act.wait_ge(b_cv, 2 * half + 1)
                A(qkv[2], qkv[2], ACT.Silu).then_inc(b_silu, 1)
                act.wait_ge(b_cv, 2 * half + 2)
                A(qkv[1], qkv[1], ACT.Silu).then_inc(b_silu, 1)
                for c in range(2):
                    await_freed(act, half, "q", c)
                for i in range(4):
                    if i >= 3:
                        act.wait_ge(b_qa, 3 * half + i - 2)
                    A(prod[i % 2] if i else qkv3[0], pre[0][:, :, i:i + L], ACT.Copy, scale=wt("cwq", i, i + 1)).then_inc(b_qm, 1)
                for c in range(2):
                    b = await_full(act, half, f"vt{c}")
                    freed(A(BR[:, 4 * c:4 * c + 4, 2].rearrange("p t h c -> p t (h c)"), bank(b).rearrange("p (t n) -> p t n", n=P), ACT.Copy), half, f"vt{c}")
                act.wait_ge(b_qa, 3 * half + 3)
                A(qkv[0], qkv[0], ACT.Silu).then_inc(b_silu, 1)
                b = await_full(act, half, "beta")
                freed(A(beta, bank(b, TH * H2).rearrange("p (t h) -> p h t", h=H2), ACT.Sigmoid), half, "beta")

            def squares(half):
                act.wait_ge(b_silu, 3 * half + 3)
                A(sqr[1], qkv[1], ACT.Square).then_inc(b_sq, 1)
                A(sqr[0], qkv[0], ACT.Square).then_inc(b_sq, 1)
                for name, x in (("nk", nk), ("nq", nq)):
                    b = await_full(act, half, name)
                    freed(A(x, bank(b, TH * H2).rearrange("p (t h) -> p h t", h=H2), ACT.Sqrt), half, name)

            def short_taps(half, a, b):
                for lag in range(a, b):
                    if lag >= 3:
                        act.wait_ge(b_fa, 6 * half + lag - 2)
                    if lag:
                        A(prod[lag % 2][:, :, 0:L - lag], qkv3[2][:, :, 0:L - lag], ACT.Copy, scale=wt("firs", 6 - lag, 7 - lag)).then_inc(b_fm, 1)
                    else:
                        A(fs, qkv3[2], ACT.Copy, scale=wt("firs", 6, 7)).then_inc(b_fm, 1)

            def gelus(half):
                for n in range(4):
                    m, c = n // 2, n % 2
                    b = await_full(act, half, "g1", n)
                    freed(A(g1T[:, m, c * NC:(c + 1) * NC], bank(b), ACT.Gelu, bias=wt("gb1", m, m + 1)), half, "g1", n)
                b = await_full(act, half, "g2")
                freed(A(gate.rearrange("p t r h -> p (t r h)"), bank(b, TH * H1), ACT.Copy), half, "g2")

            def rows_out(half):
                for r, name in ((0, "fs"), (1, "fl")):
                    for c in range(2):
                        b = await_full(act, half, name, c)
                        freed(A(BR[:, 4 * c:4 * c + 4, r].rearrange("p t h c -> p t (h c)"), bank(b).rearrange("p (t n) -> p t n", n=P), ACT.Copy), half, name, c)

            def variances(half):
                for t in range(TH):
                    act.wait_ge(b_dev, TH * half + t + 1)
                    A(DV[:, t], DV[:, t], ACT.Square).then_inc(b_dsq, 1)

            def delta_variance(half):
                for g in range(2):
                    act.wait_ge(b_dd, 2 * half + g + 1)
                    A(DD[:, 4 * g:4 * g + 4], DD[:, 4 * g:4 * g + 4], ACT.Square).then_inc(b_ddsq, 1)
                act.wait_ge(b_std, half + 1)
                A(sd, sd, ACT.Sqrt, scale=1.0 / (D2 - 1)).then_inc(b_stds, 1)

            def gate_exp(half):
                act.wait_ge(b_ee, half + 1)
                A(gate, gate, ACT.Exp).then_inc(b_exp, 1)

            def finish(half):
                act.wait_ge(b_mix, half + 1)
                A(OS, O, ACT.Square).then_inc(b_osq, 1)
                act.wait_ge(b_ors, 2 * half + 1)
                A(oms, oms, ACT.Sqrt).then_inc(b_ors, 1)
                for c in range(2):
                    b = await_full(act, half, "ot", c)
                    freed(A(OT[:, c * NC:(c + 1) * NC], bank(b), ACT.Copy, scale=wt("onw")), half, "ot", c)

            def project3s(t, dst, bias, ready, done):
                for c in range(C3):
                    if c % 4 == 0:
                        act.wait_ge(ready, 2 * t + 1 + c // 4)
                    ins = A(dst[:, c, :], PS[:, c // 4, (c % 4) * P:(c % 4 + 1) * P], ACT.Identity, bias=wt(bias, c, c + 1))
                    if c % 4 == 3:
                        ins.then_inc(done, 1)

            def softexp3(t):
                act.wait_ge(c_s3, t + 1)
                if t >= 1:
                    act.wait_ge(c_pie, t)
                A(P3.rearrange("p h k -> p (h k)"), Sc.rearrange("p h k -> p (h k)"), ACT.Exp).then_inc(c_p, 1)

            def image3s(t):
                act.wait_ge(c_pit, t + 1)
                A(PiT3, PS[0:64, 4, 0:P], ACT.Copy).then_inc(c_pits, 1)

            def keys3s(t):
                act.wait_ge(c_t, t + 1)
                for i in range(2):
                    A(kt3[:, 512 * i:512 * i + 512], bank(i), ACT.Copy).then_inc(c_ts, 1)

            def weighed3(t):
                act.wait_ge(c_pv, t + 1)
                for f in range(2):
                    A(aT3[:, :, 64 * f:64 * f + 64], bank(4 + f).rearrange("p (c n) -> p c n", c=C3), ACT.Copy).then_inc(c_at, 1)

            def out3(t):
                act.wait_ge(c_y, t + 1)
                A(YT, bank(4, P), ACT.Identity, bias=wt("bo3")).then_inc(c_ys, 1)
                act.wait_ge(c_yt, t + 1)
                A(Y[:, t, 0:D], bank(5, P), ACT.Copy).then_inc(c_ytm, 1)

            def tile3(t, pieces=()):
                if t < T:
                    if t == 0:
                        act.wait_ge(c_zero, 1)
                    project3s(t, qs, "bq3", c_q, c_qs)
                if t >= 1:
                    image3s(t - 1)
                if t < T:
                    if t >= 1:
                        act.wait_ge(c_kx, t)
                    project3s(t, kpl, "bk3", c_k, c_ks)
                if t >= 1:
                    weighed3(t - 1)
                if t < T:
                    keys3s(t)
                for piece in pieces:
                    piece(1)
                if t >= 1:
                    out3(t - 1)
                if t < T:
                    softexp3(t)

            for n in range(2):
                k_swizzle(n)
            for i in range(4):
                act.wait_ge(s_z1p, i + 1)
                A(Z1[:, 4 * i:4 * i + 4, :].rearrange("p t c -> p (t c)"), PS[0:64, 6 + i % 2, :], ACT.Copy).then_inc(s_z1, 1)
            act.wait_ge(s_wb, 16)
            act.wait_ge(s_ak, 1)
            for c in range(C3):
                A(ak3[:, c * NB:(c + 1) * NB], bank(6, NB, NB * c), ACT.Identity, bias=wt("bk3", c, c + 1))
            for c in range(C3):
                ins = A(av3[:, c * NB:(c + 1) * NB], bank(7, NB, NB * c), ACT.Identity, bias=wt("bv3", c, c + 1))
            ins.then_inc(s_ak3, 2)
            for t in range(TH):
                tile1(t)
                if t in (1, 3):
                    r = t // 2
                    act.wait_ge(s_z2p, r + 1)
                    for o in range(2):
                        ins = A(Z2s[:, 8 * r + o:8 * r + 8:2, :], PS[0:64, 6 + o, :].rearrange("p (h c) -> p h c", c=P), ACT.Copy)
                    ins.then_inc(s_z2s, 1)
            PIECES = ((inputs,), (v_rows_out,), (squares, lambda h: short_taps(h, 0, 3)), (lambda h: short_taps(h, 3, 5),),
                      (lambda h: short_taps(h, 5, 7),), (gelus, rows_out), (), (variances,))
            for t in range(TH, TH + 2):
                tile1(t)
            for piece in PIECES[0]:
                piece(0)
            for i in range(1, TH):
                tile1(TH + 1 + i, PIECES[i])
            tile1(T + 1)
            for rest in (delta_variance, gate_exp, finish):
                rest(0)
            for t in range(TH):
                tile3(t, PIECES[t])
            for rest in (delta_variance, gate_exp, finish):
                rest(1)
            for t in range(TH, T + 1):
                tile3(t)

            act.wait_ge(d_ex, 1)
            A(LG, LG, ACT.Exp).then_inc(d_exps, 1)
            for e in range(E):
                for m in range(HC):
                    act.wait_ge(d_f1, HC * e + m + 1)
                    A(GH[:, e % 2, m], bank(1 + m, CAP), ACT.Gelu, bias=wt("fb1", e * HC + m, e * HC + m + 1)).then_inc(d_f1s, 1)

        @block.vector
        def _(dve):
            chain = [0]

            def link(ins):
                chain[0] += 1
                ins.then_inc(ch_v, 1)
                dve.wait_ge(ch_v, chain[0])

            def q_swizzle(n):
                dve.wait_ge(s_qp, n + 1)
                qps = bank(n if n < 2 else 6).rearrange("p (t j n) -> p t j n", j=J, n=L)
                s = n % 2
                if n >= 2:
                    dve.wait_ge(a_s, 4 * (n - 1))
                for g in range(G1):
                    for j in range(J):
                        dve.tensor_scalar(Qd[32 * j:32 * j + 32, g].rearrange("p (s t j n) -> p s t j n", s=2, j=J, n=L)[:, s, :, j, :],
                                          qps[32 * g:32 * g + 32, :, j, :], wt("bq1")[32 * g:32 * g + 32], None, ALU.add).then_inc(s_qsw, 1)
                dve.wait_ge(s_imgsb, 2)
                if n >= 2:
                    dve.wait_ge(a_kx, 4 * (n - 1))
                for g in range(G1):
                    for j in range(J):
                        dve.tensor_copy(K0[32 * j:32 * j + 32, g, 4 * s:4 * s + 4, 0],
                                        kimg[32 * g:32 * g + 32, :].rearrange("p (n t j) -> p n j t", n=CH, j=J)[:, n, j, :]).then_inc(s_k00, 1)

            def mask1(t):
                dve.wait_ge(a_s, t + 1)
                for i in range(2):
                    dve.scalar_tensor_tensor(out=S2[:, t % 2, 8 * i:8 * i + 8, :], in0=PS[:, i, 0:264].rearrange("p (h k) -> p h k", h=8),
                                             scalar=float(1.0 / np.sqrt(np.float32(D1))),
                                             in1=cs("c01").rearrange("p (o k) -> p o k", o=1).broadcast_to([P, 8, K1]),
                                             op0=ALU.mult, op1=ALU.mult).then_inc(a_s1, 1)
                dve.wait_ge(a_s1, 2 * t + 2)
                link(dve.tensor_tensor(S2[:, t % 2], S2[:, t % 2], Mk[:, t:t + 1, :].broadcast_to([P, H1, K1]), ALU.add))
                dve.tensor_reduce(mx1[:, t % 2], S2[:, t % 2], AX.X, ALU.max).then_inc(a_mx, 1)

            def values1(t):
                dve.wait_ge(a_v, t + 1)
                if t >= 1:
                    dve.wait_ge(a_vx, t)
                dve.tensor_tensor(Vt1, PS[:, 3, :].rearrange("p (j c) -> p j c", j=J),
                                  wt("bv1r").rearrange("p (o c) -> p o c", o=1).broadcast_to([P, J, P]), ALU.add).then_inc(a_vt, 1)

            def norm1(t):
                dve.wait_ge(a_p, t + 1)
                link(dve.tensor_reduce(sm1, P1[:, t % 2], AX.X, ALU.add))
                link(dve.reciprocal(rs1, sm1))
                if t >= 1:
                    dve.wait_ge(a_t, t)
                dve.tensor_tensor(Pn1.rearrange("p (h k) -> p h k", h=H1), P1[:, t % 2, :, 1:K1],
                                  rs1.rearrange("p (h o) -> p h o", o=1).broadcast_to([P, H1, L]), ALU.mult).then_inc(a_pn, 1)
                link(dve.tensor_tensor(sm1, P1[:, t % 2, :, 0], rs1, ALU.mult))
                dve.tensor_tensor(Pie1[:, t % 2], sm1.rearrange("p (o h) -> p o h", o=1).broadcast_to([P, J, H1]),
                                  cs("jm4").rearrange("p (j o) -> p j o", o=1).broadcast_to([P, J, H1]), ALU.mult).then_inc(a_pie, 1)

            def tile1(t, pieces=(), fill=None):
                if t < T:
                    mask1(t)
                if fill:
                    fill(0)
                if t < T:
                    values1(t)
                if t in (5, 8):
                    q_swizzle(2 if t == 5 else 3)
                for piece in pieces:
                    piece(0)
                if 1 <= t <= T:
                    norm1(t - 1)

            def convolve(half, i, name):
                for c in range(2):
                    await_freed(dve, half, name, c)
                y = qkv3[i]
                link(dve.tensor_scalar(y, pre[i][:, :, 0:L], wt("cw" + name, 0, 1), None, ALU.mult))
                for k in range(1, 4):
                    ins = dve.scalar_tensor_tensor(out=y, in0=pre[i][:, :, k:k + L], scalar=wt("cw" + name, k, k + 1), in1=y, op0=ALU.mult, op1=ALU.add)
                    if k < 3:
                        link(ins)
                ins.then_inc(b_cv, 1)

            def zero_pads(half):
                dve.memset(br(0, 3360).rearrange("p (b l) -> p b l", l=PADW)[:, :, 0:3], 0.0).then_inc(b_pad, 1)

            def coefficients(half):
                for name in ("beta", "nk", "nq"):
                    await_freed(dve, half, name)
                dve.reciprocal(nq, nq)
                link(dve.reciprocal(nk, nk))
                link(dve.tensor_tensor(cf1, beta, nk, ALU.mult))
                dve.tensor_tensor(cf2, cf1, nk, ALU.mult).then_inc(b_coef, 1)

            def couple(half, name, lag=None):
                G, m = (GN, "maskn") if name == "gn" else (GA, "maska")
                for h in range(H2):
                    b = await_full(dve, half, name, h)
                    freed(dve.tensor_tensor(G[:, h], bank(b).rearrange("p (t n) -> p t n", n=64),
                                            cs(m).rearrange("p (o n) -> p o n", o=1).broadcast_to([P, TH, 64]), ALU.mult), half, name, h)
                    if lag:
                        long_filter(half, lag + 2 * h, lag + 2 * h + 2)

            def long_filter(half, a, b):
                v = qkv3[2]
                if a == 0:
                    dve.wait_ge(b_silu, 3 * half + 1)
                    link(dve.tensor_scalar(fl, v, wt("firl", 30, 31), None, ALU.mult))
                for lag in range(max(a, 1), b):
                    ins = dve.scalar_tensor_tensor(out=fl[:, :, lag:L], in0=v[:, :, 0:L - lag], scalar=wt("firl", 30 - lag, 31 - lag),
                                                   in1=fl[:, :, lag:L], op0=ALU.mult, op1=ALU.add)
                    if lag < 30:
                        link(ins)
                    else:
                        ins.then_inc(b_fl, 1)

            def gate_in(half):
                await_freed(dve, half, "g2")
                g = gate.rearrange("p t r h -> p t (r h)")
                dve.tensor_tensor(g, g, wt("gb2r").rearrange("p (o n) -> p o n", o=1).broadcast_to([P, TH, H1]), ALU.add)

            def solve(half, a, b):
                if a == 0:
                    dve.wait_ge(b_u0, 16 * J * (half + 1))
                    dve.wait_ge(b_pn, 16 * J * (half + 1))
                for j in range(a, b):
                    m = L - 1 - j
                    link(dve.tensor_tensor(tmpU[:, 0:m, :], PN[:, j + 1:L, j:j + 1].broadcast_to([P, m, D2]),
                                           U[:, j:j + 1, :].broadcast_to([P, m, D2]), ALU.mult))
                    ins = dve.tensor_tensor(U[:, j + 1:L, :], U[:, j + 1:L, :], tmpU[:, 0:m, :], ALU.add)
                    if j < L - 2:
                        link(ins)
                    else:
                        ins.then_inc(b_solved, 1)

            def stats(half):
                for name in ("fs", "fl"):
                    for c in range(2):
                        await_freed(dve, half, name, c)
                for g in range(2):
                    t = slice(4 * g, 4 * g + 4)
                    x = BR[:, t, 0:3].rearrange("p t r h c -> p t (r h) c")
                    dve.tensor_reduce(bmx[:, t, 0:3].rearrange("p t r h -> p t (r h)"), x, AX.X, ALU.max)
                    link(dve.tensor_reduce(mu[:, t, 0:3].rearrange("p t r h -> p t (r h)"), x, AX.X, ALU.add))
                dve.tensor_scalar(mu[:, :, 0:3], mu[:, :, 0:3], 1.0 / D2, None, ALU.mult).then_inc(b_st, 1)

            def spreads(half):
                dve.wait_ge(b_dsq, TH * (half + 1))
                for g in range(2):
                    t = slice(4 * g, 4 * g + 4)
                    dve.tensor_reduce(sd[:, t, 0:3].rearrange("p t r h -> p t (r h)"), DV[:, t].rearrange("p t r (h c) -> p t (r h) c", h=H2), AX.X, ALU.add)

            def delta_stats(half):
                for n in range(4):
                    c, f = n // 2, n % 2
                    b = await_full(dve, half, "o", n)
                    o = slice(64 * f, 64 * f + 64)
                    freed(dve.tensor_tensor(BR[o, 4 * c:4 * c + 4, 3], PS[o, b, :].rearrange("p (t h c) -> p t h c", t=4, h=H2),
                                            nq[o, :, 4 * c:4 * c + 4].rearrange("p h (t u) -> p t h u", u=1).broadcast_to([64, 4, H2, D2]), ALU.mult), half, "o", n)
                for n in range(2, 4):
                    await_freed(dve, half, "o", n)
                for g in range(2):
                    t = slice(4 * g, 4 * g + 4)
                    link(dve.tensor_reduce(mu[:, t, 3], BR[:, t, 3], AX.X, ALU.add))
                    link(dve.tensor_scalar(mu[:, t, 3], mu[:, t, 3], 1.0 / D2, None, ALU.mult))
                    dve.tensor_tensor(DD[:, t], BR[:, t, 3], mu[:, t, 3].rearrange("p t (h o) -> p t h o", o=1).broadcast_to([P, 4, H2, D2]),
                                      ALU.subtract).then_inc(b_dd, 1)
                link(dve.tensor_reduce(bmx[:, :, 3], BR[:, :, 3], AX.X, ALU.max))

            def mixture(half):
                for g in range(2):
                    dve.wait_ge(b_ddsq, 2 * half + g + 1)
                    ins = dve.tensor_reduce(sd[:, 4 * g:4 * g + 4, 3], DD[:, 4 * g:4 * g + 4], AX.X, ALU.add)
                ins.then_inc(b_std, 1)
                link(dve.tensor_tensor(bmx, mu, bmx, ALU.add))
                dve.wait_ge(b_stds, half + 1)
                link(dve.tensor_tensor(bmx, bmx, sd, ALU.add))
                link(dve.tensor_scalar(bmx, bmx, 1.0 / 3.0, None, ALU.mult))
                al = wt("alphar").rearrange("p (o u h) -> p o u h", o=1, u=1).broadcast_to([P, TH, 4, H2])
                link(dve.tensor_tensor(bmx, bmx, al, ALU.mult))
                link(dve.tensor_tensor(gate, gate, bmx, ALU.add))
                link(dve.tensor_reduce(lmx, gate.rearrange("p t r h -> p t h r"), AX.X, ALU.max))
                bc = lambda x: x.rearrange("p t (o h) -> p t o h", o=1).broadcast_to([P, TH, 4, H2])
                dve.tensor_tensor(gate, gate, bc(lmx), ALU.subtract).then_inc(b_ee, 1)

            def mixed(half):
                bc = lambda x: x.rearrange("p t (o h) -> p t o h", o=1).broadcast_to([P, TH, 4, H2])
                dve.wait_ge(b_exp, half + 1)
                link(dve.tensor_reduce(lmx, gate.rearrange("p t r h -> p t h r"), AX.X, ALU.add))
                link(dve.reciprocal(lmx, lmx))
                dve.tensor_tensor(gate, gate, bc(lmx), ALU.mult).then_inc(b_wts, 1)
                dve.wait_ge(b_wts, half + 1)
                for r in (1, 2, 3):
                    for g in range(2):
                        t = slice(4 * g, 4 * g + 4)
                        ins = dve.tensor_tensor(BR[:, t, r], BR[:, t, r], gate[:, t, r].rearrange("p t (h o) -> p t h o", o=1).broadcast_to([P, 4, H2, D2]), ALU.mult)
                link(ins)
                link(dve.tensor_tensor(O, BR[:, :, 1], BR[:, :, 2], ALU.add))
                link(dve.tensor_tensor(O, O, BR[:, :, 3], ALU.add))
                dve.wait_ge(b_mixp, 2 * half + 2)
                dve.tensor_tensor(O, O, BR[:, :, 0], ALU.add).then_inc(b_mix, 1)

            def normalise(half):
                dve.wait_ge(b_osq, half + 1)
                link(dve.tensor_reduce(oms, OS, AX.X, ALU.add))
                dve.tensor_scalar(oms, oms, 1.0 / D2, 1e-5, ALU.mult, ALU.add).then_inc(b_ors, 1)
                dve.wait_ge(b_ors, 2 * half + 2)
                link(dve.reciprocal(oms, oms))
                for c in range(2):
                    dve.tensor_tensor(O[:, 4 * c:4 * c + 4], O[:, 4 * c:4 * c + 4],
                                      oms[:, 4 * c:4 * c + 4].rearrange("p t (h o) -> p t h o", o=1).broadcast_to([P, 4, H2, D2]), ALU.mult).then_inc(b_on, 1)

            def residual(half):
                for c in range(2):
                    b = await_full(dve, half, "op", c)
                    n = 2 * half + c
                    freed(dve.tensor_tensor(XT[:, n * NC:(n + 1) * NC], XT[:, n * NC:(n + 1) * NC], bank(b), ALU.add), half, "op", c)

            def keys3(t):
                dve.wait_ge(c_ks, 2 * t + 2)
                if t == 0:
                    dve.wait_ge(c_zero, 1)
                else:
                    dve.wait_ge(c_s, t)
                for f in range(2):
                    o = slice(64 * f, 64 * f + 64)
                    dve.tensor_copy(kx3[o, :, :, f, 0], ak3[o, :].rearrange("p (c b) -> p c b", c=C3)[:, :, J * t:J * t + J])
                    ins = dve.tensor_copy(kx3[o, :, :, f, 1:L + 1], kpl[o].rearrange("p c (j n) -> p c j n", j=J))
                ins.then_inc(c_kx, 1)

            def mask3(t):
                dve.wait_ge(c_s, t + 1)
                if t >= 1:
                    dve.wait_ge(c_p, t)
                for i in range(2):
                    dve.scalar_tensor_tensor(out=Sc[:, 8 * i:8 * i + 8, :], in0=PS[:, 2 + i, 0:272].rearrange("p (h k) -> p h k", h=8), scalar=1.0 / 8.0,
                                             in1=cs("band").rearrange("p (o k) -> p o k", o=1).broadcast_to([P, 8, K3]), op0=ALU.mult, op1=ALU.add).then_inc(c_s1, 1)
                dve.wait_ge(c_s1, 2 * t + 2)
                dve.tensor_reduce(mx3, Sc, AX.X, ALU.max).then_inc(c_mx, 1)

            def norm3(t):
                dve.wait_ge(c_p, t + 1)
                link(dve.tensor_reduce(sm3, P3, AX.X, ALU.add))
                link(dve.reciprocal(rs3, sm3))
                dve.tensor_tensor(Pn3.rearrange("p (h k) -> p h k", h=H3), P3[:, :, 1:L + 1],
                                  rs3.rearrange("p (h o) -> p h o", o=1).broadcast_to([P, H3, L]), ALU.mult).then_inc(c_pn, 1)
                link(dve.tensor_tensor(sm3, P3[:, :, 0], rs3, ALU.mult))
                if t >= 1:
                    dve.wait_ge(c_pit, t)
                dve.tensor_tensor(Pie3, sm3.rearrange("p (o h) -> p o h", o=1).broadcast_to([P, J, H3]),
                                  cs("jm4").rearrange("p (j o) -> p j o", o=1).broadcast_to([P, J, H3]), ALU.mult).then_inc(c_pie, 1)
                dve.wait_ge(c_pn, t + 1)
                if t >= 1:
                    dve.wait_ge(c_ptd, t)
                dve.transpose(PTc, Pn3).then_inc(c_ptc, 1)

            def logits3(t):
                dve.wait_ge(c_ytm, t + 1)
                dve.tensor_tensor(LG[:, t], bank(5, E, P), wt("rbr"), ALU.add).then_inc(c_lg, 1)

            def tile3(t, pieces=(), fill=None):
                if t < T:
                    keys3(t)
                if fill:
                    fill(1)
                if t < T:
                    mask3(t)
                for piece in pieces:
                    piece(1)
                if t >= 1:
                    logits3(t - 1)
                if t < T:
                    norm3(t)

            dve.wait_ge(s_w, 16)
            dve.wait_ge(s_zero, 1)
            for n in range(2):
                q_swizzle(n)
            dve.wait_ge(s_c, 16)
            dve.wait_ge(s_mk, 2)
            for t in range(TH):
                tile1(t)
            dve.wait_ge(s_wb, 16)
            dve.wait_ge(s_z2d, 16)
            dve.wait_ge(s_z1, 4)
            zero_pads(0)
            for t in range(TH, TH + 2):
                tile1(t)
            PIECES = {3: (coefficients, lambda h: couple(h, "gn", 20),), 4: (lambda h: couple(h, "ga"),), 7: (stats, gate_in, delta_stats, spreads)}
            BETWEEN = (lambda h: convolve(h, 2, "v"), lambda h: long_filter(h, 0, 5), lambda h: long_filter(h, 10, 15),
                       lambda h: long_filter(h, 28, 31), lambda h: solve(h, 0, 3), lambda h: solve(h, 6, 10), lambda h: solve(h, 15, 21), lambda h: None)
            INSIDE = (None, lambda h: convolve(h, 1, "k"), lambda h: long_filter(h, 5, 10), lambda h: long_filter(h, 15, 20), None,
                      lambda h: solve(h, 3, 6), lambda h: solve(h, 10, 15), lambda h: solve(h, 21, L - 1))
            BETWEEN[0](0)
            for i in range(1, TH):
                tile1(TH + 1 + i, PIECES.get(i, ()), INSIDE[i])
                BETWEEN[i](0)
            for rest in (mixture, mixed, normalise, residual):
                rest(0)
            zero_pads(1)
            for t in range(TH):
                tile3(t, PIECES.get(t, ()), INSIDE[t])
                BETWEEN[t](1)
            for rest in (mixture, mixed, normalise, residual):
                rest(1)
            for t in range(TH, T + 1):
                tile3(t)

            dve.wait_ge(c_lg, T)
            eb = lambda x: x.rearrange("p (t o) -> p t o", o=1).broadcast_to([P, T, E])
            rk = cs("rank").rearrange("p (o e) -> p o e", o=1).broadcast_to([P, T, E])
            link(dve.tensor_reduce(lm, LG, AX.X, ALU.max))
            dve.tensor_tensor(LG, LG, eb(lm), ALU.subtract).then_inc(d_ex, 1)
            dve.wait_ge(d_exps, 1)
            link(dve.tensor_reduce(lm, LG, AX.X, ALU.add))
            link(dve.reciprocal(lm, lm))
            link(dve.tensor_tensor(LG, LG, eb(lm), ALU.mult))
            for s in range(2):
                link(dve.tensor_reduce(tv[:, s], LG, AX.X, ALU.max))
                link(dve.tensor_tensor(tq, LG, eb(tv[:, s]), ALU.is_equal))
                link(dve.tensor_tensor(tq, tq, rk, ALU.mult))
                link(dve.tensor_reduce(tk[:, s], tq, AX.X, ALU.max))
                link(dve.tensor_tensor(OH[:, s], rk, eb(tk[:, s]), ALU.is_equal))
                if s == 0:
                    link(dve.scalar_tensor_tensor(out=LG, in0=OH[:, 0], scalar=-4.0, in1=LG, op0=ALU.mult, op1=ALU.add))
            link(dve.tensor_tensor(lm, tv[:, 0], tv[:, 1], ALU.add))
            link(dve.tensor_scalar(lm, lm, EPS, None, ALU.add))
            link(dve.reciprocal(lm, lm))
            link(dve.tensor_tensor(tv, tv, lm.rearrange("p (o t) -> p o t", o=1).broadcast_to([P, 2, T]), ALU.mult))
            link(dve.tensor_scalar(vl, tv, EPS, None, ALU.is_gt))
            dve.tensor_tensor(OH, OH, vl.rearrange("p s (t o) -> p s t o", o=1).broadcast_to([P, 2, T, E]), ALU.mult).then_inc(d_oh, 1)
            dve.wait_ge(d_cum, 1)
            totv = tot.rearrange("p (e s t) -> p e s t", e=E, s=2)
            ohe = OH[:, :, :, :].rearrange("p s t e -> p e s t")
            link(dve.tensor_copy(totv, bank(2, 2 * T * E).rearrange("p (s t e) -> p e s t", s=2, t=T)))
            link(dve.tensor_tensor_scan(out=run_, data0=cs("seg"), data1=tot, initial=0.0, op0=ALU.mult, op1=ALU.add))
            link(dve.tensor_tensor(run_, run_, tot, ALU.subtract))
            link(dve.tensor_tensor(pos, run_.rearrange("p (e s t) -> p s t e", e=E, s=2), bank(1, 2 * T * E).rearrange("p (s t e) -> p s t e", s=2, t=T), ALU.add))
            st = lambda x: x.rearrange("p (s t) -> p s t", s=2)
            link(dve.tensor_tensor(pos, pos, OH, ALU.mult))
            link(dve.tensor_reduce(st(pown), pos, AX.X, ALU.add))
            eb4 = cs("ebase").rearrange("p (o u e) -> p o u e", o=1, u=1).broadcast_to([P, 2, T, E])
            link(dve.tensor_tensor(pos, OH, eb4, ALU.mult))
            link(dve.tensor_reduce(st(slot), pos, AX.X, ALU.add))
            link(dve.tensor_scalar(keep, pown, float(CAP), None, ALU.is_lt))
            link(dve.tensor_tensor(st(keep), st(keep), vl, ALU.mult))
            link(dve.tensor_tensor(slot, slot, pown, ALU.add))
            link(dve.tensor_tensor(tv, tv, st(keep), ALU.mult))
            link(dve.tensor_tensor(slot, slot, keep, ALU.mult))
            link(dve.tensor_scalar(pown, keep, -1.0, 1.0, ALU.mult, ALU.add))
            link(dve.tensor_tensor(sidx, pown, cs("dummy"), ALU.mult))
            link(dve.tensor_tensor(sidx, sidx, slot, ALU.add))
            dve.tensor_copy(sI, sidx).then_inc(d_slot, 1)
            for c in range(CH):
                dve.wait_ge(d_x1t, c + 1)
                dve.tensor_copy(X1[:, 4 * c:4 * c + 4, :].rearrange("p t c -> p (t c)"), bank(7)).then_inc(d_x1s, 1)

            def rows_in(e):
                dve.wait_ge(d_xt, e + 1)
                if e >= 2:
                    dve.wait_ge(d_ye, e - 1)
                dve.tensor_copy(XGT[:, e % 2], bank(0, CAP)).then_inc(d_xts, 1)
                g = gidx[:, 3 * e:3 * e + 3]
                link(dve.tensor_scalar(g, cs("slotix"), run_[:, e * 2 * T + T:e * 2 * T + T + 1], float(N), ALU.is_ge, ALU.mult))
                for s, (a, b) in enumerate(RPARTS):
                    ins = dve.tensor_tensor(g[0:b - a, s:s + 1], g[0:b - a, s:s + 1], XG[0:b - a, e % 2, s, D:D + 1], ALU.add)
                link(ins)
                dve.tensor_copy(gI[:, 3 * e:3 * e + 3], g).then_inc(d_di, 1)

            def result(e):
                dve.wait_ge(d_f2, e + 1)
                link(dve.tensor_scalar(YE[:, e % 2], bank(5, CAP), wt("fb2", e, e + 1), wt("lsc", e, e + 1), ALU.add, ALU.mult))
                dve.tensor_tensor(YE[:, e % 2], YE[:, e % 2], XGT[:, e % 2], ALU.add).then_inc(d_ye, 1)

            def rows_out(e):
                dve.wait_ge(d_yt, e + 1)
                if e >= 2:
                    dve.wait_ge(d_yd[e % 2], 16 * 3 * (e // 2))
                for s, (a, b) in enumerate(RPARTS):
                    ins = dve.tensor_copy(YO[0:b - a, e % 2, s, :], PS[0:b - a, 6, s * P:(s + 1) * P])
                ins.then_inc(d_yts, 1)

            rows_in(0)
            for e in range(E):
                if e < E - 1:
                    rows_in(e + 1)
                if e:
                    rows_out(e - 1)
                result(e)
            rows_out(E - 1)
            for t in range(T):
                dve.wait_ge(d_ga[t // 4], 16 * 2)
                link(dve.tensor_scalar(RO[:, t, :], YG[:, 0, t, :], tv[:, 0, t:t + 1], None, ALU.mult))
                link(dve.scalar_tensor_tensor(out=RO[:, t, :], in0=YG[:, 1, t, :], scalar=tv[:, 1, t:t + 1], in1=RO[:, t, :], op0=ALU.mult, op1=ALU.add))
                dve.tensor_tensor(RO[:, t, :], RO[:, t, :], X1[:, t, :], ALU.add).then_inc(d_fin, 1)

def constants():
    p = np.arange(P)
    j, q = p // L, p % L
    f = np.float32
    c = {}
    c["ident"] = np.eye(P)
    c["hm2"] = p[:, None] // D2 == np.arange(H2)[None]
    c["ones"] = np.ones((P, P))
    c["before"] = (p[:, None] < p[None])
    c["hm4"] = (p[:, None] % 32) // D1 == np.arange(4)[None]
    c["hmv"] = (p[:, None] // L == (p[None] % 32) // D1)
    c["hm16"] = p[:, None] // D1 == np.arange(H1)[None]
    c["jm4"] = j[:, None] == np.arange(J)[None]
    c["c01"] = np.arange(K1)[None] <= q[:, None] + 1
    c["nonc"] = -10000.0 * (1 - c["c01"])
    k64 = np.arange(64)
    same = (j[:, None] % 2) == (k64[None] // L)
    c["maskn"] = -1.0 * (same & (k64[None] % L < q[:, None]))
    c["maska"] = 1.0 * (same & (q[:, None] <= k64[None] % L))
    band = np.full((P, K3), NEG)
    band[:, 0] = 0
    band[:, 1:L + 1][np.abs(np.arange(L)[None] - q[:, None]) <= 1] = 0
    band[(q == 0) | (q == L - 1), L + 1] = 0
    c["band"] = band
    c["jm2"] = (j[:, None] % 2) == np.arange(2)[None]
    c["rank"] = np.broadcast_to(E - np.arange(E), (P, E))
    c["ebase"] = np.broadcast_to(CAP * np.arange(E), (P, E))
    c["dummy"] = SLOTS + P * np.arange(2 * T)[None] + p[:, None]
    c["seg"] = np.broadcast_to(np.arange(E * 2 * T) % (2 * T) != 0, (P, E * 2 * T))
    c["tok"] = P * np.arange(T)[None] + p[:, None]
    c["empty"] = 2 * N + P * np.arange(SP)[None] + p[:, None]
    c["slotix"] = P * np.arange(3)[None] + p[:, None]
    return np.concatenate([c[n].astype(f) for n, _ in CONSTS], axis=1)


def kernel(**inputs):
    import concourse.bacc as bacc
    from concourse.bass_utils import run_bass_kernel_spmd

    i = {k: np.asarray(v) for k, v in inputs.items()}
    col = lambda a: a.reshape(-1, P).T
    row = lambda a: np.broadcast_to(a.reshape(1, -1), (P, a.size))
    order = lambda a: a.reshape(4, H2, -1)[[0, 1, 3, 2]].reshape(a.shape)
    A, G, S, F = "L0_cond_", "L0_attn_", "L0_cond2_", "L0_ffn_"
    w = {
        "wqkv": i[A + "c_attn_w"], "cproj": i[A + "c_proj_w"], "ukT": i[A + "uk_w"].T, "uvT": i[A + "uv_w"].T,
        "condT": i["cond_1024"].T, "qpT": i[G + "q_proj_w"].T, "kpT": i[G + "k_proj_w"].T, "vpT": i[G + "v_proj_w"].T,
        "bpT": i[G + "b_proj_w"].T, "gw1T": i[G + "gmix_w1"].T,
        "gw2T": order(i[G + "gmix_w2"]).T.reshape(2, P, H1).transpose(1, 0, 2).reshape(P, -1), "opT": i[G + "o_proj_w"].T,
        "wq3": i[S + "WQ_w"], "wk3": i[S + "WK_w"], "wv3": i[S + "WV_w"],
        "wo3": i[S + "WO_w"].reshape(C3, P, D).transpose(1, 0, 2).reshape(P, -1), "rwT": i[F + "router_w"].T,
        "bq1": col(i[A + "c_attn_b"][0:D]), "bk1": col(i[A + "c_attn_b"][D:2 * D]), "ukb": col(i[A + "uk_b"]), "uvb": col(i[A + "uv_b"]),
        "cpb": col(i[A + "c_proj_b"]), "cwq": i[G + "q_conv_w"], "cwk": i[G + "k_conv_w"], "cwv": i[G + "v_conv_w"],
        "firs": i[G + "fir_short_w"].reshape(P, -1), "firl": i[G + "fir_long_w"].reshape(P, -1), "gb1": col(i[G + "gmix_b1"]),
        "onw": np.tile(i[G + "o_norm_w"], H2).reshape(P, 1), "bq3": col(i[S + "WQ_b"]), "bk3": col(i[S + "WK_b"]), "bv3": col(i[S + "WV_b"]),
        "bo3": col(i[S + "WO_b"]), "fb1": col(i[F + "fc1_b"]), "fb2": i[F + "fc2_b"].T, "lsc": i[F + "layer_scale"].T,
        "bv1r": row(i[A + "c_attn_b"][2 * D:]), "gb2r": row(order(i[G + "gmix_b2"])), "alphar": row(i[G + "alpha"]), "rbr": row(i[F + "router_b"]),
    }
    for n, width in WEIGHTS:
        assert w[n].shape == (P, width), (n, w[n].shape)
    arrays = {
        "xT": np.ascontiguousarray(i["x"].reshape(N, D).T),
        "w": np.ascontiguousarray(np.concatenate([w[n] for n, _ in WEIGHTS], axis=1)),
        "cst": constants(),
        "mask": np.ascontiguousarray(i["mask_Bx1x1xS_ff0"].reshape(NB, L)),
        "fc1": np.ascontiguousarray(i[F + "fc1_w"].transpose(2, 0, 1)),
        "fc2": np.ascontiguousarray(i[F + "fc2_w"].transpose(2, 0, 1).reshape(HC, P, E, D).transpose(1, 2, 0, 3).reshape(P, E, HID)),
    }
    nc = bacc.Bacc("TRN2", target_bir_lowering=False, num_devices=1)
    f = mybir.dt.float32
    aps = [nc.dram_tensor(k, a.shape, f, kind="ExternalInput").ap() for k, a in arrays.items()]
    scratch = {"xscr": (XROWS, D + 1), "yscr": (YROWS, D), "nscr": (2, P, 1024), "vscr": (2, P, 1024), "uscr": (2, P, 1024), "zscr": (NB, H3, D)}
    aps += [nc.dram_tensor(k, s, f, kind="Internal").ap() for k, s in scratch.items()]
    o = nc.dram_tensor("out", (N, D), f, kind="ExternalOutput").ap()
    program(nc, *aps, o)
    r = run_bass_kernel_spmd(nc, [arrays], core_ids=[0])
    return r.results[0]["out"].reshape(NB, L, D)
```

```python
import numpy as np
import concourse.bass as bass
from concourse import mybir
from contextlib import ExitStack

NB, L, D = 64, 32, 128
N = NB * L
P = 128
T = N // P
J = P // L
CH = 4
NC = N // CH
H1, D1 = 16, 8
G1 = 4
K1 = L + 1
H2, D2 = 4, 32
DS = 24
H3, D3 = 16, 64
C3 = H3 * D3 // P
K3 = L + 2
E, HID = 8, 512
HC = HID // P
CAP = int(1.2 * (N // E + 1))
SLOTS = E * CAP
TH, NH = T // 2, N // 2
AREA_A = 15200
AREA = AREA_A + 19744
XROWS = SLOTS + 2 * N
SCOLS = -(-SLOTS // P)
YROWS = 3 * N + SLOTS
PADW = L + 3
NEG = -1e30
EPS = 1e-9

CONSTS = [("ident", P), ("hm2", H2), ("ones", P), ("before", P), ("hm4", G1), ("hmv", P), ("hm16", H1),
          ("jm4", J), ("c01", K1), ("nonc", K1), ("maskn", 64), ("maska", 64), ("band", K3), ("jm2", 2),
          ("rank", E), ("ebase", E), ("dummy", 2 * T), ("seg8", E * 8), ("seg4", E * 4), ("seg16", E * T), ("tok", T), ("empty", SCOLS), ("slotix", 3)]
WEIGHTS = [("wqkv", 3 * D), ("cproj", D), ("ukT", D), ("uvT", D), ("condT", NB),
           ("bq1", 1), ("bk1", 1), ("ukb", 1), ("uvb", 1), ("cpb", 1), ("bv1r", D),
           ("qpT", D), ("kpT", D), ("vpT", D),
           ("bpT", H2), ("gw1T", 2 * D), ("gw2T", 2 * H1), ("opT", D), ("wq3", C3 * P), ("wk3", C3 * P),
           ("wv3", C3 * P), ("wo3", C3 * P), ("rwT", E),
           ("cwq", 4), ("cwk", 4), ("cwv", 4),
           ("firs", 7), ("firl", 31), ("gb1", 2), ("onw", 1), ("bq3", C3), ("bk3", C3), ("bv3", C3), ("bo3", 1),
           ("fb1", E * HC), ("fb2", E), ("lsc", E),
           ("gb2r", H1), ("alphar", 4), ("rbr", E)]


def offsets(fields):
    at, out = 0, {}
    for name, width in fields:
        out[name] = (at, width)
        at += width
    return out, at


def program(nc, xT, w, cst, mask, fc1, fc2, xscr, yscr, nscr, vscr, uscr, zscr, out):
    fp32, i32 = mybir.dt.float32, mybir.dt.int32
    ALU, ACT, AX = mybir.AluOpType, mybir.ActivationFunctionType, mybir.AxisListType
    wo, WW = offsets(WEIGHTS)
    co, CW = offsets(CONSTS)
    ctx = ExitStack()
    with ctx:
        def sb(name, cols, parts=P, dt=fp32):
            return ctx.enter_context(nc.sbuf_tensor(name, [parts, cols], dt))

        def sem(name):
            return ctx.enter_context(nc.semaphore(name))

        W = sb("W", WW)
        Cn = sb("Cn", CW)
        XT = sb("XT", N)
        hT = sb("hT", N)
        Z2 = sb("Z2", T * P, 64)
        kimg = sb("kimg", NB)
        vimg = sb("vimg", NB)
        ak3 = sb("ak3", C3 * NB)
        av3 = sb("av3", C3 * NB)
        SM = sb("SM", 2464)
        AR = sb("AR", AREA)
        PS = ctx.enter_context(nc.psum_tensor("PS", [P, 8, 512], fp32))

        def wt(name, a=0, b=None):
            o, n = wo[name]
            return W[:, o + a:o + (n if b is None else b)]

        def cs(name, a=0, b=None):
            o, n = co[name]
            return Cn[:, o + a:o + (n if b is None else b)]

        def ar(at, n, parts=P):
            return AR[0:parts, at:at + n]

        small_at = [0]

        def small(n):
            a = small_at[0]
            small_at[0] += n
            return SM[:, a:a + n]

        ident = cs("ident")

        def br(at, n):
            return AR[:, AREA_A + at:AREA_A + at + n]

        def bank(i, cols=512, at=0):
            return PS[:, i, at:at + cols]

        Qd = ar(0, 4096).rearrange("p (g n) -> p g n", g=G1)
        K0 = ar(4096, 1056).rearrange("p (g t k) -> p g t k", g=G1, t=TH)
        Kx = ar(5152, 1056).rearrange("p (r g h k) -> p r g h k", r=2, g=G1, h=4)
        S2 = ar(6208, 1056).rearrange("p (r h k) -> p r h k", r=2, h=H1)
        P1 = ar(7264, 1056).rearrange("p (r h k) -> p r h k", r=2, h=H1)
        Pn1 = ar(8320, 512)
        PT1 = ar(8832, 1024).rearrange("p (r g n) -> p r g n", r=2, g=G1)
        Vt1 = ar(9856, 512).rearrange("p (j c) -> p j c", j=J)
        Vx1 = ar(10368, 1024).rearrange("p (r j c) -> p r j c", r=2, j=J)
        Z1 = AR[0:64, 11392:13440].rearrange("p (t c) -> p t c", t=T)
        Mk = ar(13440, 528).rearrange("p (t k) -> p t k", t=T)
        aT1 = ar(13968, 256).rearrange("p (r n) -> p r n", r=2)
        Pie1 = ar(14224, 128).rearrange("p (r j h) -> p r j h", r=2, j=J)
        PiT1 = ar(14352, 256).rearrange("p (r n) -> p r n", r=2)
        Xr = ar(14608, 512).rearrange("p (j o n) -> p j o n", j=J, o=4)
        mx1 = small(2 * H1).rearrange("p (r h) -> p r h", r=2)
        sm1 = small(H1)
        rs1 = small(H1)
        vie = br(0, 1024).rearrange("p (b h) -> p b h", h=H1)
        Z2s = AR[0:64, AREA_A + 1024:AREA_A + 3072].rearrange("p (h c) -> p h c", h=H3)

        pre = [br(1120 * i, 1120).rearrange("p (b l) -> p b l", b=NB // 2) for i in range(3)]
        qkv = [br(3360 + NH * i, NH) for i in range(3)]
        qkv3 = [x.rearrange("p (b l) -> p b l", b=NB // 2) for x in qkv]
        sqr = [br(0, NH), br(1120, NH)]
        g1T = br(0, 2 * NH).rearrange("p (m n) -> p m n", m=2)
        fl = br(2240, NH).rearrange("p (b l) -> p b l", b=NB // 2)
        O = br(3360, NH).rearrange("p (t h c) -> p t h c", t=TH, h=H2)
        OS = br(4384, NH).rearrange("p (t h c) -> p t h c", t=TH, h=H2)
        OT = br(5408, NH)
        VB = br(6432, NH).rearrange("p (h t c) -> p h t c", h=H2, t=TH)
        PN = br(6432, NH).rearrange("p (i k) -> p i k", i=L)
        U = br(7456, NH).rearrange("p (i c) -> p i c", i=L)
        prod = [br(8480 + NH * i, NH).rearrange("p (b l) -> p b l", b=NB // 2) for i in range(2)]
        DV = br(8480, 3 * NH).rearrange("p (t r c) -> p t r c", t=TH, r=3)
        DD = br(2240, NH).rearrange("p (t h c) -> p t h c", t=TH, h=H2)
        fs = br(10528, NH).rearrange("p (b l) -> p b l", b=NB // 2)
        GN = br(11552, 2048).rearrange("p (h t n) -> p h t n", h=H2, t=TH)
        tmpU = br(11552, 31 * L).rearrange("p (i c) -> p i c", i=31)
        tmpP = br(8480, 31 * (D2 - DS)).rearrange("p (i c) -> p i c", i=31)
        UT = br(12576, NH).rearrange("p (h t c) -> p h t c", h=H2, t=TH)
        GA = br(13600, 2048).rearrange("p (h t n) -> p h t n", h=H2, t=TH)
        BR = br(15648, 4096).rearrange("p (t r h c) -> p t r h c", t=TH, r=4, h=H2)
        beta, nk, nq, cf1, cf2 = (small(TH * H2).rearrange("p (h t) -> p h t", h=H2) for _ in range(5))
        gate, mu, sd, bmx = (small(TH * 16).rearrange("p (t r h) -> p t r h", t=TH, r=4) for _ in range(4))
        lmx, oms = (small(TH * 4).rearrange("p (t h) -> p t h", t=TH) for _ in range(2))

        qs = ar(0, 1024).rearrange("p (c n) -> p c n", c=C3)
        kpl = ar(1024, 1024).rearrange("p (c n) -> p c n", c=C3)
        kx3 = ar(2048, 2176).rearrange("p (c j h k) -> p c j h k", c=C3, j=J, h=2)
        kt3 = ar(4224, 1024)
        Sc = ar(5248, 544).rearrange("p (h k) -> p h k", h=H3)
        P3 = ar(5792, 544).rearrange("p (h k) -> p h k", h=H3)
        Pn3 = ar(6336, 512)
        PTc = ar(6848, 512)
        PTd = ar(7360, 1024).rearrange("p (h i q) -> p h i q", h=H3, i=2)
        aT3 = ar(8384, 1024).rearrange("p (c n) -> p c n", c=C3)
        Pie3 = ar(9408, 64).rearrange("p (j h) -> p j h", j=J)
        PiT3 = AR[0:64, 9472:9600]
        YT = ar(9600, 128)
        EZ = ar(12304, SCOLS * (D + 1)).rearrange("p (a c) -> p a c", a=SCOLS)
        Y = ar(10240, T * (D + 1)).rearrange("p (t c) -> p t c", t=T)
        FW = br(0, 8192).rearrange("p (e s n) -> p e s n", e=E, s=2)
        mx3, sm3, rs3 = small(H3), small(H3), small(H3)

        LG = small(T * E).rearrange("p (t e) -> p t e", t=T)
        lm = small(T)
        OH = small(2 * T * E).rearrange("p (s t e) -> p s t e", s=2, t=T)
        tq = small(T * E).rearrange("p (t e) -> p t e", t=T)
        tv = small(2 * T).rearrange("p (s t) -> p s t", s=2)
        tk = small(2 * T).rearrange("p (s t) -> p s t", s=2)
        vl = small(2 * T).rearrange("p (s t) -> p s t", s=2)
        tot, run_, pos_ = (small(T * E) for _ in range(3))
        carry, add = small(E), small(E)
        pown, keep, slot, sidx, gidx = (small(2 * T) for _ in range(5))
        sI, gI = (small(2 * T).bitcast(i32) for _ in range(2))
        XG = ar(0, 6 * (D + 1)).rearrange("p (r s c) -> p r s c", r=2, s=3)
        XGT = ar(776, 2 * CAP).rearrange("p (r n) -> p r n", r=2)
        GH = ar(776 + 2 * CAP, 2 * HC * CAP).rearrange("p (r m n) -> p r m n", r=2, m=HC)
        YE = ar(776 + 10 * CAP, 2 * CAP).rearrange("p (r n) -> p r n", r=2)
        YO = ar(776 + 12 * CAP, 768).rearrange("p (r s c) -> p r s c", r=2, s=3)
        X1 = br(8192, N).rearrange("p (t c) -> p t c", t=T)
        YG = br(10240, 2 * N).rearrange("p (s t c) -> p s t c", s=2, t=T)
        RO = br(14336, N).rearrange("p (t c) -> p t c", t=T)
        ROUTES = [(0, 8), (8, 12), (12, 16)]
        RPARTS = [(0, P), (P, 2 * P), (2 * P, CAP)]

        s_w, s_wb, s_c, s_am = sem("weights_in"), sem("more_weights_in"), sem("consts_in"), sem("mask_in")
        s_x = [sem(f"x{c}_in") for c in range(CH)]
        s_img, s_imgsb = sem("img_ps"), sem("img_sb")
        s_qp, s_kp, s_qsw, s_ksw = sem("q_ps"), sem("k_ps"), sem("q_swz"), sem("k_swz")
        s_zero, s_k00 = sem("zeroed"), sem("k_img_slot")
        s_vie, s_z1p, s_z1 = sem("vie"), sem("z1_ps"), sem("z1_sb")
        s_ak, s_ak3, s_z2p, s_z2s, s_z2d, s_z2 = sem("ak_ps"), sem("ak_sb"), sem("z2_ps"), sem("z2_sb"), sem("z2_dram"), sem("z2_in")
        s_mk = sem("mask_sum")
        a_kx, a_s, a_s1, a_mx, a_s3, a_p, a_pn, a_xr = (sem(f"a_{n}") for n in ("kx", "s", "s1", "mx", "s3", "p", "pn", "xr"))
        a_pie, a_t, a_pt, a_v, a_vt, a_vx, a_pv, a_at, a_h, a_hs = (
            sem(f"a_{n}") for n in ("pie", "t", "pt", "v", "vt", "vx", "pv", "at", "h", "hs"))
        ch_v, ch_p = sem("dve_chain"), sem("pool_chain")
        b_full, b_free = [sem(f"b_full{i}") for i in range(2)], [sem(f"b_free{i}") for i in range(2)]
        (b_pad, b_cv, b_silu, b_qm, b_qa, b_sq, b_coef, b_vb, b_gsc, b_vd, b_u0, b_nd, b_pn, b_solved, b_ud,
         b_fm, b_fa, b_fl, b_st, b_dev, b_dd, b_ddsq, b_dsq, b_std, b_stds, b_ee, b_exp, b_wts, b_mixp, b_mix, b_osq, b_ors, b_on,
         b_utm) = (sem(f"b_{n}") for n in (
             "pad cv silu qm qa sq coef vb gsc vd u0 nd pn solved ud fm fa fl st dev dd ddsq dsq std stds ee exp wts "
             "mixp mix osq ors on utm").split())
        (c_q, c_qs, c_k, c_ks, c_kx, c_t, c_ts, c_s, c_s1, c_mx, c_s3, c_p, c_pn, c_ptc, c_pie, c_ptd, c_pit, c_pits, c_pv, c_at,
         c_y, c_ys, c_yt, c_ytm, c_lg, c_zero) = (sem(f"c_{n}") for n in (
             "q qs k ks kx t ts s s1 mx s3 p pn ptc pie ptd pit pits pv at y ys yt ytm lg zero").split())
        (d_ex, d_exps, d_oh, d_cum, d_slot, d_sc, d_xt, d_xts, d_f1, d_f1s, d_f2, d_ye, d_yt, d_yts, d_x1t, d_x1s, d_out, d_fin,
         d_xz, d_fw, d_zt, d_yz, d_di) = (sem(f"d_{n}") for n in (
             "ex exps oh cum slot sc xt xts f1 f1s f2 ye yt yts x1t x1s out fin xz fw zt yz di").split())
        d_xg, d_yd = [sem(f"d_xg{r}") for r in range(2)], [sem(f"d_yd{r}") for r in range(2)]
        d_ga = [sem(f"d_ga{c}") for c in range(CH)]
        block = ctx.enter_context(nc.Block())

        USES = []
        for half in range(2):
            USES += [(half, n, c) for n in "vkq" for c in range(2)] + [(half, n, 0) for n in ("vt0", "vt1", "beta", "nk", "nq")]
            USES += [(half, "gn", h) for h in range(H2)] + [(half, "ga", h) for h in range(H2)]
            USES += [(half, "g1", n) for n in range(4)] + [(half, "g2", 0)] + [(half, n, c) for n in ("fs", "fl") for c in range(2)]
            USES += [(half, "o", n) for n in range(4)] + [(half, "ot", c) for c in range(2)] + [(half, "op", c) for c in range(2)]

        def use(half, name, n=0):
            i = USES.index((half, name, n))
            return 6 + i % 2, b_full[i % 2], b_free[i % 2], i // 2 + 1

        def await_full(eng, *u):
            b, full, _, n = use(*u)
            eng.wait_ge(full, n)
            return b

        QB, KB = (0, 5, 6, 6), (1, 2, 7, 7)

        def await_freed(eng, *u):
            _, _, free, n = use(*u)
            eng.wait_ge(free, n)

        def freed(ins, *u):
            ins.then_inc(use(*u)[2], 1)

        @block.sync
        def _(sp):
            sp.dma_start(W[:, 0:wo["qpT"][0]], w[:, 0:wo["qpT"][0]]).then_inc(s_w, 16)
            for c in range(2):
                sp.dma_start(XT[:, c * NC:(c + 1) * NC], xT[:, c * NC:(c + 1) * NC]).then_inc(s_x[c], 16)
            sp.dma_start(Cn[:, :], cst).then_inc(s_c, 16)
            mv = mask.rearrange("(t j) k -> j t k", j=J)
            sp.wait_ge(s_mk, 1)
            for j in range(J):
                sp.dma_start(Mk[32 * j:32 * j + 32, :, 1:K1], mv[j:j + 1].broadcast_to([32, T, L])).then_inc(s_am, 16)
            sp.dma_start(W[:, wo["qpT"][0]:WW], w[:, wo["qpT"][0]:WW]).then_inc(s_wb, 16)
            for c in range(2, CH):
                sp.dma_start(XT[:, c * NC:(c + 1) * NC], xT[:, c * NC:(c + 1) * NC]).then_inc(s_x[c], 16)
            sp.wait_ge(s_z2s, 2)
            sp.dma_start(zscr.rearrange("b h c -> b (h c)"), AR[0:64, AREA_A + 1024:AREA_A + 3072]).then_inc(s_z2d, 16)
            sp.wait_ge(s_z2d, 16)
            sp.dma_start(Z2[:, :].rearrange("p (t c) -> p t c", t=T),
                         zscr.rearrange("(t j) h c -> (j h) t c", j=J)).then_inc(s_z2, 16)

            def pairs(half):
                sp.wait_ge(b_vb, half + 1)
                sp.dma_start(vscr[half], br(6432, NH)).then_inc(b_vd, 16)
                sp.wait_ge(b_vd, 16 * (half + 1))
                for j in range(J):
                    sp.dma_start(U[32 * j:32 * j + 32, :, :], vscr[half].rearrange("(j i) (p c) -> j p i c", j=J, c=D2)[j]).then_inc(b_u0, 16)
                sp.wait_ge(b_gsc, H2 * (half + 1))
                for j in range(J):
                    sp.dma_start(nscr[half].rearrange("(j i) (p k) -> j i p k", j=J, k=L)[j],
                                 GN[32 * j:32 * j + 32, :, :, 32 * (j % 2):32 * (j % 2) + 32].rearrange("i h t k -> i (h t) k")).then_inc(b_nd, 16)
                sp.wait_ge(b_nd, 16 * J * (half + 1))
                for j in range(J):
                    sp.dma_start(PN[32 * j:32 * j + 32, :, :], nscr[half].rearrange("(j i) (p k) -> j p i k", j=J, k=L)[j]).then_inc(b_pn, 16)
                sp.wait_ge(b_solved, 2 * half + 2)
                for j in range(J):
                    sp.dma_start(uscr[half].rearrange("(j i) (p c) -> j p i c", j=J, c=D2)[j], U[32 * j:32 * j + 32, :, :]).then_inc(b_ud, 16)
                sp.wait_ge(b_ud, 16 * J * (half + 1))
                sp.dma_start(br(12576, NH), uscr[half]).then_inc(b_utm, 16)

            pairs(0)
            sp.wait_ge(d_zt, 2)
            full = SLOTS // P * P
            sp.dma_start(xscr[0:full, :].rearrange("(a p) c -> p a c", p=P), EZ[:, 0:full // P, :]).then_inc(d_xz, 16)
            sp.dma_start(xscr[full:SLOTS, :], EZ[0:SLOTS - full, full // P, :]).then_inc(d_xz, 16)
            for a in range(0, 2 * N, 4 * P):
                sp.dma_start(yscr[a:a + 4 * P, :].rearrange("(a p) c -> p a c", p=P), EZ[:, 0:4, 0:D]).then_inc(d_yz, 16)
            pairs(1)
            for c in range(2):
                await_freed(sp, 1, "op", c)
            sp.dma_start(FW[:, :, 0, :], fc1).then_inc(d_fw, 16)
            sp.dma_start(FW[:, :, 1, :], fc2).then_inc(d_fw, 16)
            sp.wait_ge(d_sc, 16 * 2 * T)
            for e in range(E):
                if e >= 2:
                    sp.wait_ge(d_di, e - 1)
                for s, (a, b) in enumerate(RPARTS):
                    sp.dma_start(XG[0:b - a, e % 2, s, :], xscr[e * CAP + a:e * CAP + b, :]).then_inc(d_xg[e % 2], 16)
            for r in range(2):
                sp.wait_ge(d_yd[r], 16 * 3 * E // 2)
            for c in range(CH):
                for s in range(2):
                    sp.dma_start(YG[:, s, 4 * c:4 * c + 4, :], yscr[s * N + c * NC:s * N + (c + 1) * NC, :].rearrange("(t p) c -> p t c", p=P)).then_inc(d_ga[c], 16)
            for c in range(CH):
                sp.wait_ge(d_fin, c + 1)
                sp.dma_start(out[c * NC:(c + 1) * NC, :].rearrange("(t p) c -> p t c", p=P), RO[:, 4 * c:4 * c + 4, :]).then_inc(d_out, 16)
            sp.wait_ge(d_out, 16 * CH)

        @block.gpsimd
        def _(pool):
            chain = [0]
            pool.memset(Mk[:, :, :], 0.0).then_inc(s_mk, 1)
            pool.memset(Qd, 0.0).then_inc(s_zero, 1)
            pool.wait_ge(s_c, 16)
            pool.wait_ge(s_imgsb, 2)
            pool.tensor_tensor(vie, vimg[:, :].rearrange("p (b o) -> p b o", o=1).broadcast_to([P, NB, H1]),
                               cs("hm16").rearrange("p (o h) -> p o h", o=1).broadcast_to([P, NB, H1]), ALU.mult).then_inc(s_vie, 1)
            hm4 = cs("hm4").rearrange("p (o h u) -> p o h u", o=1, u=1).broadcast_to([P, G1, 4, K1])

            def expand(t):
                if t % 4 == 0:
                    pool.wait_ge(s_k00, 16 * (t // 4 + 1))
                    pool.wait_ge(s_ksw, 16 * (t // 4 + 1))
                if t >= 2:
                    pool.wait_ge(a_s, t - 1)
                pool.tensor_tensor(Kx[:, t % 2], K0[:, :, t % TH, :].rearrange("p g (o k) -> p g o k", o=1).broadcast_to([P, G1, 4, K1]),
                                   hm4, ALU.mult).then_inc(a_kx, 1)

            def repeat(t):
                pool.wait_ge(s_x[t // 4], 16)
                if t >= 1:
                    pool.wait_ge(a_v, t)
                pool.tensor_copy(Xr, XT[:, t * P:(t + 1) * P].rearrange("p (j o n) -> p j o n", j=J, o=1).broadcast_to([P, J, 4, L])).then_inc(a_xr, 1)

            def shift(t):
                pool.wait_ge(a_mx, t + 1)
                pool.tensor_tensor(S2[:, t % 2], S2[:, t % 2], mx1[:, t % 2].rearrange("p (h o) -> p h o", o=1).broadcast_to([P, H1, K1]),
                                   ALU.subtract).then_inc(a_s3, 1)

            def values(t):
                pool.wait_ge(a_vt, t + 1)
                if t >= 2:
                    pool.wait_ge(a_pv, t - 1)
                pool.tensor_tensor(Vx1[:, t % 2], Vt1, cs("hmv").rearrange("p (o c) -> p o c", o=1).broadcast_to([P, J, P]),
                                   ALU.mult).then_inc(a_vx, 1)

            def tile1(t, pieces=()):
                if 1 <= t <= T:
                    shift(t - 1)
                    values(t - 1)
                if t < T - 1:
                    expand(t + 1)
                    repeat(t + 1)
                for piece in pieces:
                    piece(0)

            def q_sum(half, a, b):
                for i in range(a, b):
                    pool.wait_ge(b_qm, 4 * half + i + 1)
                    if i > 1:
                        pool.wait_ge(b_qa, 3 * half + i - 1)
                    pool.tensor_tensor(qkv3[0], qkv3[0], prod[i % 2], ALU.add).then_inc(b_qa, 1)

            def v_scaled(half):
                pool.wait_ge(b_coef, half + 1)
                for c in range(2):
                    await_freed(pool, half, f"vt{c}")
                if half:
                    pool.wait_ge(b_solved, 2)
                pool.tensor_tensor(VB, BR[:, :, 2].rearrange("p t h c -> p h t c"),
                                   cf1.rearrange("p h (t o) -> p h t o", o=1).broadcast_to([P, H2, TH, D2]), ALU.mult).then_inc(b_vb, 1)

            def couplings(half):
                for h in range(H2):
                    await_freed(pool, half, "gn", h)
                    pool.tensor_tensor(GN[:, h], GN[:, h], cf2[:, h].rearrange("p (t o) -> p t o", o=1).broadcast_to([P, TH, 64]), ALU.mult).then_inc(b_gsc, 1)

            def short_sum(half, a, b):
                for lag in range(a, b):
                    pool.wait_ge(b_fm, 7 * half + lag + 1)
                    if lag > 1:
                        pool.wait_ge(b_fa, 6 * half + lag - 1)
                    pool.tensor_tensor(fs[:, :, lag:L], fs[:, :, lag:L], prod[lag % 2][:, :, 0:L - lag], ALU.add).then_inc(b_fa, 1)

            def solve(half, a, b):
                if a == 0:
                    pool.wait_ge(b_fa, 6 * (half + 1))
                    pool.wait_ge(b_u0, 16 * J * (half + 1))
                    pool.wait_ge(b_pn, 16 * J * (half + 1))
                for j in range(a, b):
                    m = L - 1 - j
                    chain[0] += 1
                    pool.tensor_tensor(tmpP[:, 0:m, :], PN[:, j + 1:L, j:j + 1].broadcast_to([P, m, D2 - DS]),
                                       U[:, j:j + 1, DS:D2].broadcast_to([P, m, D2 - DS]), ALU.mult).then_inc(ch_p, 1)
                    pool.wait_ge(ch_p, chain[0])
                    ins = pool.tensor_tensor(U[:, j + 1:L, DS:D2], U[:, j + 1:L, DS:D2], tmpP[:, 0:m, :], ALU.add)
                    if j < L - 2:
                        chain[0] += 1
                        ins.then_inc(ch_p, 1)
                        pool.wait_ge(ch_p, chain[0])
                    else:
                        ins.then_inc(b_solved, 1)

            def deviations(half):
                pool.wait_ge(b_st, half + 1)
                pool.wait_ge(b_solved, 2 * half + 2)
                for t in range(TH):
                    pool.tensor_tensor(DV[:, t].rearrange("p r (h c) -> p (r h) c", h=H2), BR[:, t, 0:3].rearrange("p r h c -> p (r h) c"),
                                       mu[:, t, 0:3].rearrange("p r (h o) -> p (r h) o", o=1).broadcast_to([P, 12, D2]), ALU.subtract).then_inc(b_dev, 1)

            def mix(half):
                pool.wait_ge(b_wts, half + 1)
                for g in range(2):
                    v = BR[:, 4 * g:4 * g + 4, 0:1]
                    pool.tensor_tensor(v.rearrange("p t r h c -> p t (r h) c"), v.rearrange("p t r h c -> p t (r h) c"),
                                       gate[:, 4 * g:4 * g + 4, 0:1].rearrange("p t r (h o) -> p t (r h) o", o=1).broadcast_to([P, 4, H2, D2]), ALU.mult).then_inc(b_mixp, 1)

            def zero3():
                pool.wait_ge(a_h, T)
                pool.wait_ge(a_s, T)
                pool.memset(kx3, 0.0).then_inc(c_zero, 1)
                pool.memset(EZ[:, :, 0:D], 0.0).then_inc(d_zt, 1)
                pool.tensor_copy(EZ[:, :, D], cs("empty")).then_inc(d_zt, 1)
                pool.tensor_copy(Y[:, :, D], cs("tok")).then_inc(c_zero, 1)

            def shift3(t):
                pool.wait_ge(c_mx, t + 1)
                pool.tensor_tensor(Sc, Sc, mx3.rearrange("p (h o) -> p h o", o=1).broadcast_to([P, H3, K3]), ALU.subtract).then_inc(c_s3, 1)

            def diag3(t):
                pool.wait_ge(c_ptc, t + 1)
                if t >= 1:
                    pool.wait_ge(c_pv, t)
                pool.tensor_tensor(PTd, PTc.rearrange("p (h o q) -> p h o q", h=H3, o=1).broadcast_to([P, H3, 2, L]),
                                   cs("jm2").rearrange("p (o i u) -> p o i u", o=1, u=1).broadcast_to([P, H3, 2, L]), ALU.mult).then_inc(c_ptd, 1)

            def tile3(t, pieces=()):
                if t >= 1:
                    diag3(t - 1)
                if t < T:
                    shift3(t)
                for piece in pieces:
                    piece(1)

            def scatter(s, a, b):
                for t in range(a, b):
                    pool.indirect_dma_start(out=xscr, out_offset=bass.IndirectOffsetOnAxis(ap=sI[:, s * T + t:s * T + t + 1], axis=0),
                                            in_=Y[:, t, :], in_offset=None).then_inc(d_sc, 16)

            repeat(0)
            pool.wait_ge(s_am, 16 * J)
            pool.tensor_tensor(Mk[:, :, :], Mk[:, :, :], cs("nonc").rearrange("p (o k) -> p o k", o=1).broadcast_to([P, T, K1]), ALU.add).then_inc(s_mk, 1)
            expand(0)
            for t in range(TH + 2):
                tile1(t)
            PIECES = ((), (lambda h: q_sum(h, 1, 3),), (lambda h: q_sum(h, 3, 4), lambda h: short_sum(h, 1, 3)), (v_scaled, couplings, lambda h: short_sum(h, 3, 5)),
                      (lambda h: short_sum(h, 5, 7), lambda h: solve(h, 0, 4)), (lambda h: solve(h, 4, 12),), (lambda h: solve(h, 12, L - 1),), (deviations,))
            for piece in PIECES[0]:
                piece(0)
            for i in range(1, TH - 1):
                tile1(TH + 1 + i, PIECES[i])
            tile1(T)
            for piece in PIECES[-1]:
                piece(0)
            mix(0)
            zero3()
            for piece in PIECES[0]:
                piece(1)
            for t in range(TH - 1):
                tile3(t, PIECES[t + 1])
            tile3(TH - 1)
            mix(1)
            for t in range(TH, T + 1):
                tile3(t)
                for k, (a, b) in enumerate(ROUTES[:2]):
                    at = a + 2 * (t - b - 4) if k == 0 else a + 2 * (t - T)
                    if a <= at < b:
                        if k == 0 and at == a:
                            pool.wait_ge(d_xz, 16 * 2)
                            pool.wait_ge(c_zero, 2)
                        pool.wait_ge(d_slot, k + 1)
                        pool.wait_ge(c_ytm, b)
                        scatter(0, at, at + 2)
            scatter(0, ROUTES[1][0] + 2, ROUTES[1][1])
            pool.wait_ge(c_ytm, T)
            pool.wait_ge(d_slot, 3)
            scatter(0, *ROUTES[2])
            pool.wait_ge(d_slot, 4)
            scatter(1, 0, T)
            pool.wait_ge(d_yz, 16 * 8)
            for e in range(E):
                pool.wait_ge(d_di, e + 1)
                pool.wait_ge(d_yts, e + 1)
                for s, (a, b) in enumerate(RPARTS):
                    pool.indirect_dma_start(out=yscr, out_offset=bass.IndirectOffsetOnAxis(ap=gI[0:b - a, 3 * e + s:3 * e + s + 1], axis=0),
                                            in_=YO[0:b - a, e % 2, s, :], in_offset=None).then_inc(d_yd[e % 2], 16)

        @block.tensor
        def _(pe):
            mm = pe.matmul

            def q_proj(n):
                pe.wait_ge(s_x[n], 16)
                mm(bank(QB[n]), wt("wqkv", 0, D), XT[:, n * NC:(n + 1) * NC], start=True, stop=True).then_inc(s_qp, 1)

            def k_proj(n):
                mm(bank(KB[n]), wt("wqkv", D, 2 * D), XT[:, n * NC:(n + 1) * NC], start=True, stop=True).then_inc(s_kp, 1)

            pe.wait_ge(s_w, 16)
            mm(bank(4, NB), wt("ukT"), wt("condT"), start=True, stop=True)
            mm(bank(4, NB, NB), wt("uvT"), wt("condT"), start=True, stop=True).then_inc(s_img, 1)
            for n in range(2):
                q_proj(n)
                k_proj(n)
            def image_projected():
                pe.wait_ge(s_vie, 1)
                for t in range(T):
                    if t % 4 == 0 and t >= 8:
                        pe.wait_ge(s_z1, t // 4 - 1)
                    ins = mm(PS[0:64, 6 + (t // 4) % 2, (t % 4) * P:(t % 4 + 1) * P], vie[:, J * t:J * t + J, :], wt("cproj"), start=True, stop=True)
                    if t % 4 == 3:
                        ins.then_inc(s_z1p, 1)

            def image_values():
                pe.wait_ge(s_wb, 16)
                pe.wait_ge(s_z1, 4)
                for i, name in enumerate(("wk3", "wv3")):
                    for c in range(C3):
                        ins = mm(bank(6 + i, NB, NB * c), wt(name, c * P, (c + 1) * P), wt("condT"), start=True, stop=True)
                ins.then_inc(s_ak, 1)

            def image_output(r):
                pe.wait_ge(s_ak3, 2)
                if r:
                    pe.wait_ge(s_z2s, 1)
                for i in range(8):
                    h = 8 * r + i
                    o = 64 * (h % 2)
                    ins = mm(PS[0:64, 6 + (h % 2), (i // 2) * P:(i // 2 + 1) * P], av3[o:o + 64, (h // 2) * NB:(h // 2 + 1) * NB],
                             wt("wo3", (h // 2) * P, (h // 2 + 1) * P)[o:o + 64], start=True, stop=True)
                ins.then_inc(s_z2p, 1)

            def scores(t):
                pe.wait_ge(a_kx, t + 1)
                pe.wait_ge(s_qsw, 16 * (t // 4 + 1))
                if t:
                    pe.wait_ge(a_s1, 2 * t)
                for g in range(G1):
                    ins = mm(PS[:, g // 2, (g % 2) * 132:(g % 2 + 1) * 132], Qd[:, g, (t % TH) * P:(t % TH + 1) * P],
                             Kx[:, t % 2, g].rearrange("p h k -> p (h k)"), start=True, stop=True)
                ins.then_inc(a_s, 1)

            def v_rows(t):
                pe.wait_ge(a_xr, t + 1)
                if t >= 1:
                    pe.wait_ge(a_vt, t)
                for j in range(J):
                    ins = mm(PS[:, 3, j * P:(j + 1) * P], Xr[:, j].rearrange("p o n -> p (o n)"),
                             wt("wqkv", 2 * D, 3 * D), start=True, stop=True)
                ins.then_inc(a_v, 1)

            def turn(t):
                pe.wait_ge(a_pn, t + 1)
                pe.wait_ge(a_pie, t + 1)
                if t == 0:
                    pe.wait_ge(s_ksw, 32)
                else:
                    pe.wait_ge(a_pt, 2 * t)
                    pe.wait_ge(a_hs, t)
                for g in range(G1):
                    pe.transpose(PS[:, 2, g * P:(g + 1) * P], Pn1[:, g * P:(g + 1) * P], ident)
                pe.transpose(PS[0:64, 4, 0:P], Pie1[:, t % 2].rearrange("p j h -> p (j h)"), ident).then_inc(a_t, 1)

            def weigh(t):
                pe.wait_ge(a_pt, 2 * t + 2)
                pe.wait_ge(a_vx, t + 1)
                if t == 0:
                    pe.wait_ge(s_qsw, 32)
                else:
                    pe.wait_ge(a_at, t)
                for j in range(J):
                    for g in range(G1):
                        ins = mm(PS[32 * g:32 * g + 32, 5, 32 * j:32 * j + 32], Vx1[:, t % 2, j, 32 * g:32 * g + 32],
                                 PT1[:, t % 2, g, 32 * j:32 * j + 32], start=True, stop=True)
                ins.then_inc(a_pv, 1)

            def project(t):
                pe.wait_ge(a_at, t + 1)
                mm(PS[:, 4, P:2 * P], Z1[:, t, :], PiT1[0:64, t % 2], start=True, stop=False)
                mm(PS[:, 4, P:2 * P], wt("cproj"), aT1[:, t % 2], start=False, stop=True).then_inc(a_h, 1)

            def tile1(t, pieces=()):
                if t < T:
                    if t in (5, 8):
                        n = 2 if t == 5 else 3
                        if n == 2:
                            pe.wait_ge(s_z2s, 2)
                        else:
                            pe.wait_ge(s_qsw, 48)
                            pe.wait_ge(s_ksw, 48)
                        q_proj(n)
                        k_proj(n)
                    scores(t)
                    v_rows(t)
                for piece in pieces:
                    piece(0)
                if t >= 2:
                    weigh(t - 2)
                    project(t - 2)
                if 1 <= t <= T:
                    turn(t - 1)

            def take(half, name, n=0):
                b, _, free, count = use(half, name, n)
                if count > 1:
                    pe.wait_ge(free, count - 1)
                return b

            def filled(ins, half, name, n=0):
                ins.then_inc(use(half, name, n)[1], 1)

            def proj(half):
                if half == 0:
                    pe.wait_ge(s_qsw, 64)
                    pe.wait_ge(s_ksw, 64)
                for i, name in ((2, "v"), (1, "k"), (0, "q")):
                    for c in range(2):
                        n = 2 * half + c
                        pe.wait_ge(a_hs, 4 * n + 4)
                        b = take(half, name, c)
                        filled(mm(bank(b), wt(name + "pT"), hT[:, n * NC:(n + 1) * NC], start=True, stop=True), half, name, c)

            def v_turn(half):
                pe.wait_ge(b_silu, 3 * half + 1)
                for c in range(2):
                    b = take(half, f"vt{c}")
                    for i in range(4):
                        t = 4 * c + i
                        ins = pe.transpose(bank(b, P, i * P), qkv[2][:, t * P:(t + 1) * P], ident)
                    filled(ins, half, f"vt{c}")
                b = take(half, "beta")
                for t in range(TH):
                    n = TH * half + t
                    ins = mm(bank(b, H2, H2 * t), hT[:, n * P:(n + 1) * P], wt("bpT"), start=True, stop=True)
                filled(ins, half, "beta")

            def norms(half, i):
                name = "nk" if i else "nq"
                pe.wait_ge(b_sq, 2 * half + 2 - i)
                b = take(half, name)
                for t in range(TH):
                    ins = mm(bank(b, H2, H2 * t), sqr[i][:, t * P:(t + 1) * P], cs("hm2"), start=True, stop=True)
                filled(ins, half, name)

            def gram(half, name, lhs, rhs):
                for h in range(H2):
                    b = take(half, name, h)
                    for t in range(TH):
                        for f in range(2):
                            c0 = t * P + 64 * f
                            ins = mm(PS[64 * f:64 * f + 64, b, 64 * t:64 * t + 64], lhs[32 * h:32 * h + 32, c0:c0 + 64],
                                     rhs[32 * h:32 * h + 32, c0:c0 + 64], start=True, stop=True)
                    filled(ins, half, name, h)

            def couplings(half):
                gram(half, "gn", qkv[1], qkv[1])

            def readings(half):
                gram(half, "ga", qkv[1], qkv[0])

            def gates(half):
                for n in range(4):
                    m, c = n // 2, n % 2
                    b = take(half, "g1", n)
                    filled(mm(bank(b), wt("gw1T", m * P, (m + 1) * P), hT[:, (2 * half + c) * NC:(2 * half + c + 1) * NC], start=True, stop=True), half, "g1", n)
                for n in (2, 3):
                    await_freed(pe, half, "g1", n)
                b = take(half, "g2")
                for t in range(TH):
                    for m in range(2):
                        ins = mm(bank(b, H1, H1 * t), g1T[:, m, t * P:(t + 1) * P], wt("gw2T", m * H1, (m + 1) * H1), start=(m == 0), stop=(m == 1))
                filled(ins, half, "g2")

            def filters_turn(half):
                for name, x, done, n in (("fs", fs, b_fa, 6 * half + 6), ("fl", fl, b_fl, half + 1)):
                    pe.wait_ge(done, n)
                    for c in range(2):
                        b = take(half, name, c)
                        for i in range(4):
                            t = 4 * c + i
                            ins = pe.transpose(bank(b, P, i * P), x[:, J * t:J * t + J, :].rearrange("p b l -> p (b l)"), ident)
                        filled(ins, half, name, c)

            def read_out(half):
                pe.wait_ge(b_utm, 16 * (half + 1))
                for n in range(4):
                    c, f = n // 2, n % 2
                    b = take(half, "o", n)
                    for i in range(4):
                        for h in range(H2):
                            ins = mm(PS[64 * f:64 * f + 64, b, i * P + 32 * h:i * P + 32 * h + 32], GA[64 * f:64 * f + 64, h, 4 * c + i, :],
                                     UT[64 * f:64 * f + 64, h, 4 * c + i, :], start=True, stop=True)
                    filled(ins, half, "o", n)

            def out_proj(half):
                for c in range(2):
                    pe.wait_ge(b_on, 2 * half + c + 1)
                    b = take(half, "ot", c)
                    for i in range(4):
                        ins = pe.transpose(bank(b, P, i * P), O[:, 4 * c + i].rearrange("p h c -> p (h c)"), ident)
                    filled(ins, half, "ot", c)
                for c in range(2):
                    await_freed(pe, half, "ot", c)
                    b = take(half, "op", c)
                    filled(mm(bank(b), wt("opT"), OT[:, c * NC:(c + 1) * NC], start=True, stop=True), half, "op", c)

            def proj3(t, name, done):
                x = XT[:, t * P:(t + 1) * P]
                for c in range(C3):
                    if name == "wk3" and c % 4 == 0:
                        pe.wait_ge(c_qs, 2 * t + 1 + c // 4)
                    ins = mm(PS[:, c // 4, (c % 4) * P:(c % 4 + 1) * P], wt(name, c * P, (c + 1) * P), x, start=True, stop=True)
                    if c % 4 == 3:
                        ins.then_inc(done, 1)

            def image3(t):
                pe.wait_ge(c_pie, t + 1)
                if t >= 1:
                    pe.wait_ge(c_ys, t)
                pe.transpose(PS[0:64, 4, 0:P], Pie3.rearrange("p j h -> p (j h)"), ident).then_inc(c_pit, 1)

            def weigh3(t):
                pe.wait_ge(c_ptd, t + 1)
                pe.wait_ge(c_ts, 2 * t + 2)
                pe.wait_ge(c_pits, t + 1)
                if t >= 1:
                    pe.wait_ge(c_ytm, t)
                    pe.wait_ge(c_lg, t)
                for f in range(2):
                    for h in range(H3):
                        o = 64 * (h % 2)
                        ins = mm(PS[o:o + 64, 4 + f, (h // 2) * 64:(h // 2 + 1) * 64], kt3[64 * f:64 * f + 64, 64 * h:64 * h + 64],
                                 PTd[64 * f:64 * f + 64, h].rearrange("p i q -> p (i q)"), start=True, stop=True)
                ins.then_inc(c_pv, 1)

            def keys3(t):
                pe.wait_ge(c_ks, 2 * t + 2)
                for c in range(C3):
                    ins = pe.transpose(PS[:, c // 4, (c % 4) * P:(c % 4 + 1) * P], kpl[:, c, :], ident)
                ins.then_inc(c_t, 1)

            def scores3(t):
                pe.wait_ge(c_kx, t + 1)
                if t >= 1:
                    pe.wait_ge(c_s1, 2 * t)
                for j in range(J):
                    for c in range(C3):
                        ins = mm(PS[32 * j:32 * j + 32, 2 + c // 4, (c % 4) * 68:(c % 4 + 1) * 68], qs[:, c, 32 * j:32 * j + 32],
                                 kx3[:, c, j].rearrange("p h k -> p (h k)"), start=True, stop=True)
                ins.then_inc(c_s, 1)

            def output3(t):
                pe.wait_ge(c_at, 2 * t + 2)
                mm(bank(4, P), Z2[:, t * P:(t + 1) * P], PiT3, start=True, stop=False)
                for c in range(C3):
                    ins = mm(bank(4, P), wt("wo3", c * P, (c + 1) * P), aT3[:, c, :], start=False, stop=(c == C3 - 1))
                ins.then_inc(c_y, 1)

            def turn3(t):
                pe.wait_ge(c_ys, t + 1)
                pe.transpose(bank(5, P), YT, ident)
                mm(bank(5, E, P), YT, wt("rwT"), start=True, stop=True).then_inc(c_yt, 1)

            def tile3(t, pieces=()):
                if t < T:
                    if t % (T // CH) == 0:
                        await_freed(pe, t // TH, "op", t // 4 % 2)
                    if t >= 1:
                        pe.wait_ge(c_ts, 2 * t)
                    proj3(t, "wq3", c_q)
                    proj3(t, "wk3", c_k)
                if t >= 1:
                    image3(t - 1)
                    weigh3(t - 1)
                if t < T:
                    keys3(t)
                    scores3(t)
                if t >= 1:
                    output3(t - 1)
                for piece in pieces:
                    piece(1)
                if t >= 1:
                    turn3(t - 1)

            for t in range(TH):
                tile1(t)
                if t == 0:
                    image_projected()
                    image_values()
                if t in (1, 3):
                    image_output(t // 2)
            PIECES = ((proj,), (v_turn,), (lambda h: norms(h, 1),), (lambda h: norms(h, 0), couplings), (readings,), (gates, filters_turn), (), (read_out,))
            for t in range(TH, TH + 2):
                tile1(t)
            for piece in PIECES[0]:
                piece(0)
            for i in range(1, TH - 1):
                tile1(TH + 1 + i, PIECES[i])
            for t in range(T, T + 2):
                tile1(t)
            read_out(0)
            out_proj(0)
            pe.wait_ge(s_z2, 16)
            for piece in PIECES[0]:
                piece(1)
            for t in range(TH - 1):
                tile3(t, PIECES[t + 1] if t < TH - 2 else ())
            read_out(1)
            tile3(TH - 1)
            out_proj(1)
            def count(k, s, a, b):
                pe.wait_ge(d_oh, k + 1)
                ohf = OH[:, s, a:b].rearrange("p t e -> p (t e)")
                bk, c0 = (1 if s else 6), a * E
                mm(bank(bk, (b - a) * E, c0), cs("before"), ohf, start=True, stop=True)
                mm(bank(bk, (b - a) * E, c0 + T * E), cs("ones"), ohf, start=True, stop=True).then_inc(d_cum, 1)

            for t in range(TH, T + 1):
                tile3(t)
                for k, (a, b) in enumerate(ROUTES[:2]):
                    if t == b + 2:
                        count(k, 0, a, b)

            count(2, 0, *ROUTES[2])
            count(2, 1, 0, T)
            for c in range(CH):
                if c >= 1:
                    pe.wait_ge(d_x1s, c)
                for i in range(4):
                    t = 4 * c + i
                    ins = pe.transpose(bank(7, P, i * P), XT[:, t * P:(t + 1) * P], ident)
                ins.then_inc(d_x1t, 1)
            pe.wait_ge(d_slot, 4)
            pe.wait_ge(d_fw, 32)
            def rows_in(e):
                pe.wait_ge(d_xg[e % 2], 16 * 3 * (e // 2 + 1))
                if e:
                    pe.wait_ge(d_xts, e)
                for s, (a, b) in enumerate(RPARTS):
                    ins = pe.transpose(bank(0, b - a, a), XG[0:b - a, e % 2, s, 0:D], cs("ident")[0:b - a, 0:b - a])
                ins.then_inc(d_xt, 1)

            def hidden(e):
                pe.wait_ge(d_xts, e + 1)
                for m in range(HC):
                    if e:
                        pe.wait_ge(d_f1s, HC * (e - 1) + m + 1)
                    mm(bank(1 + m, CAP), FW[:, e, 0, m * P:(m + 1) * P], XGT[:, e % 2], start=True, stop=True).then_inc(d_f1, 1)

            def result(e):
                if e:
                    pe.wait_ge(d_ye, e)
                for m in range(HC):
                    pe.wait_ge(d_f1s, HC * e + m + 1)
                    ins = mm(bank(5, CAP), FW[:, e, 1, m * P:(m + 1) * P], GH[:, e % 2, m], start=(m == 0), stop=(m == HC - 1))
                ins.then_inc(d_f2, 1)

            def rows_out(e):
                pe.wait_ge(d_ye, e + 1)
                if e:
                    pe.wait_ge(d_yts, e)
                for s, (a, b) in enumerate(RPARTS):
                    ins = pe.transpose(PS[0:b - a, 6, s * P:(s + 1) * P], YE[:, e % 2, a:b], ident)
                ins.then_inc(d_yt, 1)

            rows_in(0)
            for e in range(E):
                hidden(e)
                if e < E - 1:
                    rows_in(e + 1)
                if e:
                    rows_out(e - 1)
                result(e)
            rows_out(E - 1)

        @block.scalar
        def _(act):
            A = act.activation
            act.wait_ge(s_w, 16)
            act.wait_ge(s_img, 1)
            A(kimg[:, :], bank(4, NB), ACT.Identity, bias=wt("ukb")).then_inc(s_imgsb, 1)
            A(vimg[:, :], bank(4, NB, NB), ACT.Identity, bias=wt("uvb")).then_inc(s_imgsb, 1)

            def k_swizzle(n):
                act.wait_ge(s_kp, n + 1)
                kps = bank(KB[n]).rearrange("p (t j n) -> p t j n", j=J, n=L)
                if n >= 2:
                    act.wait_ge(a_kx, 4 * (n - 1))
                s = 4 * (n % 2)
                for g in range(G1):
                    for j in range(J):
                        A(K0[32 * j:32 * j + 32, g, s:s + 4, 1:K1], kps[32 * g:32 * g + 32, :, j, :], ACT.Identity,
                          bias=wt("bk1")[32 * g:32 * g + 32]).then_inc(s_ksw, 1)

            def softexp(t):
                act.wait_ge(a_s3, t + 1)
                if t >= 2:
                    act.wait_ge(a_pie, t - 1)
                A(P1[:, t % 2].rearrange("p h k -> p (h k)"), S2[:, t % 2].rearrange("p h k -> p (h k)"), ACT.Exp).then_inc(a_p, 1)

            def turned(t):
                act.wait_ge(a_t, t + 1)
                if t >= 2:
                    act.wait_ge(a_pv, t - 1)
                A(PT1[:, t % 2].rearrange("p g n -> p (g n)"), bank(2), ACT.Copy).then_inc(a_pt, 1)
                if t >= 2:
                    act.wait_ge(a_h, t - 1)
                A(PiT1[0:64, t % 2], PS[0:64, 4, 0:P], ACT.Copy).then_inc(a_pt, 1)

            def weighed(t):
                act.wait_ge(a_pv, t + 1)
                A(aT1[:, t % 2], bank(5, P), ACT.Copy).then_inc(a_at, 1)

            def projected(t):
                act.wait_ge(a_h, t + 1)
                A(hT[:, t * P:(t + 1) * P], bank(4, P, P), ACT.Identity, bias=wt("cpb")).then_inc(a_hs, 1)

            def tile1(t, pieces=()):
                if 1 <= t <= T:
                    softexp(t - 1)
                for piece in pieces:
                    piece(0)
                if t >= 2:
                    weighed(t - 2)
                    projected(t - 2)
                if 1 <= t <= T:
                    turned(t - 1)
                if t in (5, 8):
                    k_swizzle(2 if t == 5 else 3)

            def out_of_bank(dst, src, *u, func=ACT.Copy, **kw):
                freed(A(dst, src, func, **kw), *u)

            def inputs(half):
                act.wait_ge(b_pad, half + 1)
                for i, name in ((2, "v"), (1, "k"), (0, "q")):
                    for c in range(2):
                        b = await_full(act, half, name, c)
                        out_of_bank(pre[i][:, 16 * c:16 * c + 16, 3:PADW], bank(b).rearrange("p (b l) -> p b l", l=L), half, name, c)

            def q_taps(half, a, b):
                for i in range(a, b):
                    if i >= 3:
                        act.wait_ge(b_qa, 3 * half + i - 2)
                    A(prod[i % 2] if i else qkv3[0], pre[0][:, :, i:i + L], ACT.Copy, scale=wt("cwq", i, i + 1)).then_inc(b_qm, 1)

            def v_rows_out(half):
                act.wait_ge(b_cv, 2 * half + 1)
                A(qkv[2], qkv[2], ACT.Silu).then_inc(b_silu, 1)
                for c in range(2):
                    b = await_full(act, half, f"vt{c}")
                    freed(A(BR[:, 4 * c:4 * c + 4, 2].rearrange("p t h c -> p t (h c)"), bank(b).rearrange("p (t n) -> p t n", n=P), ACT.Copy), half, f"vt{c}")
                act.wait_ge(b_cv, 2 * half + 2)
                A(qkv[1], qkv[1], ACT.Silu).then_inc(b_silu, 1)
                for c in range(2):
                    await_freed(act, half, "q", c)
                q_taps(half, 0, 3)
                act.wait_ge(b_silu, 3 * half + 2)
                A(sqr[1], qkv[1], ACT.Square).then_inc(b_sq, 1)

            def q_rest(half):
                q_taps(half, 3, 4)
                b = await_full(act, half, "beta")
                freed(A(beta, bank(b, TH * H2).rearrange("p (t h) -> p h t", h=H2), ACT.Sigmoid), half, "beta")
                norm_out(half, "nk", nk)
                act.wait_ge(b_qa, 3 * half + 3)
                act.wait_ge(b_qm, 4 * half + 4)
                A(qkv[0], qkv[0], ACT.Silu).then_inc(b_silu, 1)
                act.wait_ge(b_silu, 3 * half + 3)
                A(sqr[0], qkv[0], ACT.Square).then_inc(b_sq, 1)

            def norm_out(half, name, x):
                b = await_full(act, half, name)
                freed(A(x, bank(b, TH * H2).rearrange("p (t h) -> p h t", h=H2), ACT.Sqrt), half, name)

            def short_taps(half, a, b):
                for lag in range(a, b):
                    if lag >= 3:
                        act.wait_ge(b_fa, 6 * half + lag - 2)
                    if lag:
                        A(prod[lag % 2][:, :, 0:L - lag], qkv3[2][:, :, 0:L - lag], ACT.Copy, scale=wt("firs", 6 - lag, 7 - lag)).then_inc(b_fm, 1)
                    else:
                        A(fs, qkv3[2], ACT.Copy, scale=wt("firs", 6, 7)).then_inc(b_fm, 1)

            def gelus(half):
                for n in range(4):
                    m, c = n // 2, n % 2
                    b = await_full(act, half, "g1", n)
                    freed(A(g1T[:, m, c * NC:(c + 1) * NC], bank(b), ACT.Gelu, bias=wt("gb1", m, m + 1)), half, "g1", n)
                b = await_full(act, half, "g2")
                freed(A(gate.rearrange("p t r h -> p (t r h)"), bank(b, TH * H1), ACT.Copy), half, "g2")

            def rows_out(half):
                for r, name in ((0, "fs"), (1, "fl")):
                    for c in range(2):
                        b = await_full(act, half, name, c)
                        freed(A(BR[:, 4 * c:4 * c + 4, r].rearrange("p t h c -> p t (h c)"), bank(b).rearrange("p (t n) -> p t n", n=P), ACT.Copy), half, name, c)

            def variances(half):
                for t in range(TH):
                    act.wait_ge(b_dev, TH * half + t + 1)
                    A(DV[:, t], DV[:, t], ACT.Square).then_inc(b_dsq, 1)

            def delta_variance(half):
                for g in range(2):
                    act.wait_ge(b_dd, 2 * half + g + 1)
                    A(DD[:, 4 * g:4 * g + 4], DD[:, 4 * g:4 * g + 4], ACT.Square).then_inc(b_ddsq, 1)
                act.wait_ge(b_std, half + 1)
                A(sd, sd, ACT.Sqrt, scale=1.0 / (D2 - 1)).then_inc(b_stds, 1)

            def gate_exp(half):
                act.wait_ge(b_ee, half + 1)
                A(gate, gate, ACT.Exp).then_inc(b_exp, 1)

            def finish(half):
                for g in range(2):
                    act.wait_ge(b_mix, 2 * half + g + 1)
                    A(OS[:, 4 * g:4 * g + 4], O[:, 4 * g:4 * g + 4], ACT.Square).then_inc(b_osq, 1)
                act.wait_ge(b_ors, 2 * half + 1)
                A(oms, oms, ACT.Sqrt).then_inc(b_ors, 1)
                for c in range(2):
                    b = await_full(act, half, "ot", c)
                    freed(A(OT[:, c * NC:(c + 1) * NC], bank(b), ACT.Copy, scale=wt("onw")), half, "ot", c)

            def project3s(t, dst, bias, ready, done):
                for c in range(C3):
                    if c % 4 == 0:
                        act.wait_ge(ready, 2 * t + 1 + c // 4)
                    ins = A(dst[:, c, :], PS[:, c // 4, (c % 4) * P:(c % 4 + 1) * P], ACT.Identity, bias=wt(bias, c, c + 1))
                    if c % 4 == 3:
                        ins.then_inc(done, 1)

            def softexp3(t):
                act.wait_ge(c_s3, t + 1)
                if t >= 1:
                    act.wait_ge(c_pie, t)
                A(P3.rearrange("p h k -> p (h k)"), Sc.rearrange("p h k -> p (h k)"), ACT.Exp).then_inc(c_p, 1)

            def image3s(t):
                act.wait_ge(c_pit, t + 1)
                A(PiT3, PS[0:64, 4, 0:P], ACT.Copy).then_inc(c_pits, 1)

            def keys3s(t):
                act.wait_ge(c_t, t + 1)
                for i in range(2):
                    A(kt3[:, 512 * i:512 * i + 512], bank(i), ACT.Copy).then_inc(c_ts, 1)

            def weighed3(t):
                act.wait_ge(c_pv, t + 1)
                for f in range(2):
                    A(aT3[:, :, 64 * f:64 * f + 64], bank(4 + f).rearrange("p (c n) -> p c n", c=C3), ACT.Copy).then_inc(c_at, 1)

            def out3(t):
                act.wait_ge(c_y, t + 1)
                A(YT, bank(4, P), ACT.Identity, bias=wt("bo3")).then_inc(c_ys, 1)

            def rows3(t):
                act.wait_ge(c_yt, t + 1)
                A(Y[:, t, 0:D], bank(5, P), ACT.Copy).then_inc(c_ytm, 1)

            def tile3(t, pieces=()):
                if t < T:
                    if t == 0:
                        act.wait_ge(c_zero, 1)
                    project3s(t, qs, "bq3", c_q, c_qs)
                if t >= 1:
                    image3s(t - 1)
                if t < T:
                    if t >= 1:
                        act.wait_ge(c_kx, t)
                    project3s(t, kpl, "bk3", c_k, c_ks)
                if t >= 1:
                    weighed3(t - 1)
                if t < T:
                    keys3s(t)
                if t < TH:
                    softexp3(t)
                if t >= 1:
                    out3(t - 1)
                for piece in pieces:
                    piece(1)
                if t >= 1:
                    rows3(t - 1)
                if TH <= t < T:
                    softexp3(t)

            for n in range(2):
                k_swizzle(n)
            for i in range(4):
                act.wait_ge(s_z1p, i + 1)
                A(Z1[:, 4 * i:4 * i + 4, :].rearrange("p t c -> p (t c)"), PS[0:64, 6 + i % 2, :], ACT.Copy).then_inc(s_z1, 1)
            act.wait_ge(s_wb, 16)
            act.wait_ge(s_ak, 1)
            for c in range(C3):
                A(ak3[:, c * NB:(c + 1) * NB], bank(6, NB, NB * c), ACT.Identity, bias=wt("bk3", c, c + 1))
            for c in range(C3):
                ins = A(av3[:, c * NB:(c + 1) * NB], bank(7, NB, NB * c), ACT.Identity, bias=wt("bv3", c, c + 1))
            ins.then_inc(s_ak3, 2)
            for t in range(TH):
                tile1(t)
                if t in (1, 3):
                    r = t // 2
                    act.wait_ge(s_z2p, r + 1)
                    for o in range(2):
                        ins = A(Z2s[:, 8 * r + o:8 * r + 8:2, :], PS[0:64, 6 + o, :].rearrange("p (h c) -> p h c", c=P), ACT.Copy)
                    ins.then_inc(s_z2s, 1)
            PIECES = ((inputs,), (v_rows_out,), (q_rest, lambda h: short_taps(h, 0, 3)), (lambda h: norm_out(h, "nq", nq), lambda h: short_taps(h, 3, 5)),
                      (lambda h: short_taps(h, 5, 7),), (gelus, rows_out), (), (variances,))
            for t in range(TH, TH + 2):
                tile1(t)
            for piece in PIECES[0]:
                piece(0)
            for i in range(1, TH - 1):
                tile1(TH + 1 + i, PIECES[i])
            for t in range(T, T + 2):
                tile1(t)
            for rest in (variances, delta_variance, gate_exp, finish):
                rest(0)
            for piece in PIECES[0]:
                piece(1)
            for t in range(TH - 1):
                tile3(t, PIECES[t + 1] if t < TH - 2 else ())
            for rest in (variances, delta_variance, gate_exp):
                rest(1)
            tile3(TH - 1)
            finish(1)
            for t in range(TH, T + 1):
                tile3(t)
                for k, (a, b) in enumerate(ROUTES):
                    if t == min(b + 1, T):
                        act.wait_ge(d_ex, k + 1)
                        A(LG[:, a:b], LG[:, a:b], ACT.Exp).then_inc(d_exps, 1)

            for e in range(E):
                for m in range(HC):
                    act.wait_ge(d_f1, HC * e + m + 1)
                    A(GH[:, e % 2, m], bank(1 + m, CAP), ACT.Gelu, bias=wt("fb1", e * HC + m, e * HC + m + 1)).then_inc(d_f1s, 1)

        @block.vector
        def _(dve):
            chain = [0]

            def link(ins):
                chain[0] += 1
                ins.then_inc(ch_v, 1)
                dve.wait_ge(ch_v, chain[0])

            def q_swizzle(n):
                dve.wait_ge(s_qp, n + 1)
                qps = bank(QB[n]).rearrange("p (t j n) -> p t j n", j=J, n=L)
                s = n % 2
                if n >= 2:
                    dve.wait_ge(a_s, 4 * (n - 1))
                for g in range(G1):
                    for j in range(J):
                        dve.tensor_scalar(Qd[32 * j:32 * j + 32, g].rearrange("p (s t j n) -> p s t j n", s=2, j=J, n=L)[:, s, :, j, :],
                                          qps[32 * g:32 * g + 32, :, j, :], wt("bq1")[32 * g:32 * g + 32], None, ALU.add).then_inc(s_qsw, 1)
                dve.wait_ge(s_imgsb, 2)
                if n >= 2:
                    dve.wait_ge(a_kx, 4 * (n - 1))
                for g in range(G1):
                    for j in range(J):
                        dve.tensor_copy(K0[32 * j:32 * j + 32, g, 4 * s:4 * s + 4, 0],
                                        kimg[32 * g:32 * g + 32, :].rearrange("p (n t j) -> p n j t", n=CH, j=J)[:, n, j, :]).then_inc(s_k00, 1)

            def mask1(t):
                dve.wait_ge(a_s, t + 1)
                for i in range(2):
                    dve.scalar_tensor_tensor(out=S2[:, t % 2, 8 * i:8 * i + 8, :], in0=PS[:, i, 0:264].rearrange("p (h k) -> p h k", h=8),
                                             scalar=float(1.0 / np.sqrt(np.float32(D1))),
                                             in1=cs("c01").rearrange("p (o k) -> p o k", o=1).broadcast_to([P, 8, K1]),
                                             op0=ALU.mult, op1=ALU.mult).then_inc(a_s1, 1)
                dve.wait_ge(a_s1, 2 * t + 2)
                link(dve.tensor_tensor(S2[:, t % 2], S2[:, t % 2], Mk[:, t:t + 1, :].broadcast_to([P, H1, K1]), ALU.add))
                dve.tensor_reduce(mx1[:, t % 2], S2[:, t % 2], AX.X, ALU.max).then_inc(a_mx, 1)

            def values1(t):
                dve.wait_ge(a_v, t + 1)
                if t >= 1:
                    dve.wait_ge(a_vx, t)
                dve.tensor_tensor(Vt1, PS[:, 3, :].rearrange("p (j c) -> p j c", j=J),
                                  wt("bv1r").rearrange("p (o c) -> p o c", o=1).broadcast_to([P, J, P]), ALU.add).then_inc(a_vt, 1)

            def norm1(t):
                dve.wait_ge(a_p, t + 1)
                link(dve.tensor_reduce(sm1, P1[:, t % 2], AX.X, ALU.add))
                link(dve.reciprocal(rs1, sm1))
                if t >= 1:
                    dve.wait_ge(a_t, t)
                dve.tensor_tensor(Pn1.rearrange("p (h k) -> p h k", h=H1), P1[:, t % 2, :, 1:K1],
                                  rs1.rearrange("p (h o) -> p h o", o=1).broadcast_to([P, H1, L]), ALU.mult).then_inc(a_pn, 1)
                link(dve.tensor_tensor(sm1, P1[:, t % 2, :, 0], rs1, ALU.mult))
                dve.tensor_tensor(Pie1[:, t % 2], sm1.rearrange("p (o h) -> p o h", o=1).broadcast_to([P, J, H1]),
                                  cs("jm4").rearrange("p (j o) -> p j o", o=1).broadcast_to([P, J, H1]), ALU.mult).then_inc(a_pie, 1)

            def tile1(t, pieces=(), fill=None):
                if 1 <= t <= T:
                    norm1(t - 1)
                if t < T:
                    mask1(t)
                if fill:
                    fill(0)
                if t < T:
                    values1(t)
                if t in (5, 8):
                    q_swizzle(2 if t == 5 else 3)
                for piece in pieces:
                    piece(0)

            def convolve(half, i, name):
                for c in range(2):
                    await_freed(dve, half, name, c)
                y = qkv3[i]
                link(dve.tensor_scalar(y, pre[i][:, :, 0:L], wt("cw" + name, 0, 1), None, ALU.mult))
                for k in range(1, 4):
                    ins = dve.scalar_tensor_tensor(out=y, in0=pre[i][:, :, k:k + L], scalar=wt("cw" + name, k, k + 1), in1=y, op0=ALU.mult, op1=ALU.add)
                    if k < 3:
                        link(ins)
                ins.then_inc(b_cv, 1)

            def zero_pads(half):
                dve.memset(br(0, 3360).rearrange("p (b l) -> p b l", l=PADW)[:, :, 0:3], 0.0).then_inc(b_pad, 1)

            def coefficients(half):
                for name in ("beta", "nk"):
                    await_freed(dve, half, name)
                link(dve.reciprocal(nk, nk))
                link(dve.tensor_tensor(cf1, beta, nk, ALU.mult))
                dve.tensor_tensor(cf2, cf1, nk, ALU.mult).then_inc(b_coef, 1)

            def couple(half, name, lag=None):
                G, m = (GN, "maskn") if name == "gn" else (GA, "maska")
                for h in range(H2):
                    b = await_full(dve, half, name, h)
                    freed(dve.tensor_tensor(G[:, h], bank(b).rearrange("p (t n) -> p t n", n=64),
                                            cs(m).rearrange("p (o n) -> p o n", o=1).broadcast_to([P, TH, 64]), ALU.mult), half, name, h)
                    if lag:
                        long_filter(half, lag + 2 * h, lag + 2 * h + 2)

            def long_filter(half, a, b):
                v = qkv3[2]
                if a == 0:
                    dve.wait_ge(b_silu, 3 * half + 1)
                    link(dve.tensor_scalar(fl, v, wt("firl", 30, 31), None, ALU.mult))
                for lag in range(max(a, 1), b):
                    ins = dve.scalar_tensor_tensor(out=fl[:, :, lag:L], in0=v[:, :, 0:L - lag], scalar=wt("firl", 30 - lag, 31 - lag),
                                                   in1=fl[:, :, lag:L], op0=ALU.mult, op1=ALU.add)
                    if lag < 30:
                        link(ins)
                    else:
                        ins.then_inc(b_fl, 1)

            def gate_in(half):
                await_freed(dve, half, "g2")
                g = gate.rearrange("p t r h -> p t (r h)")
                dve.tensor_tensor(g, g, wt("gb2r").rearrange("p (o n) -> p o n", o=1).broadcast_to([P, TH, H1]), ALU.add)

            def solve(half, a, b):
                if a == 0:
                    dve.wait_ge(b_u0, 16 * J * (half + 1))
                    dve.wait_ge(b_pn, 16 * J * (half + 1))
                for j in range(a, b):
                    m = L - 1 - j
                    link(dve.tensor_tensor(tmpU[:, 0:m, 0:DS], PN[:, j + 1:L, j:j + 1].broadcast_to([P, m, DS]),
                                           U[:, j:j + 1, 0:DS].broadcast_to([P, m, DS]), ALU.mult))
                    ins = dve.tensor_tensor(U[:, j + 1:L, 0:DS], U[:, j + 1:L, 0:DS], tmpU[:, 0:m, 0:DS], ALU.add)
                    if j < L - 2:
                        link(ins)
                    else:
                        ins.then_inc(b_solved, 1)

            def stats(half):
                for name in ("fs", "fl"):
                    for c in range(2):
                        await_freed(dve, half, name, c)
                for g in range(2):
                    t = slice(4 * g, 4 * g + 4)
                    x = BR[:, t, 0:3].rearrange("p t r h c -> p t (r h) c")
                    dve.tensor_reduce(bmx[:, t, 0:3].rearrange("p t r h -> p t (r h)"), x, AX.X, ALU.max)
                    link(dve.tensor_reduce(mu[:, t, 0:3].rearrange("p t r h -> p t (r h)"), x, AX.X, ALU.add))
                dve.tensor_scalar(mu[:, :, 0:3], mu[:, :, 0:3], 1.0 / D2, None, ALU.mult).then_inc(b_st, 1)

            def spreads(half):
                dve.wait_ge(b_dsq, TH * (half + 1))
                for g in range(2):
                    t = slice(4 * g, 4 * g + 4)
                    dve.tensor_reduce(sd[:, t, 0:3].rearrange("p t r h -> p t (r h)"), DV[:, t].rearrange("p t r (h c) -> p t (r h) c", h=H2), AX.X, ALU.add)

            def delta_stats(half):
                await_freed(dve, half, "nq")
                link(dve.reciprocal(nq, nq))
                for n in range(4):
                    c, f = n // 2, n % 2
                    b = await_full(dve, half, "o", n)
                    o = slice(64 * f, 64 * f + 64)
                    freed(dve.tensor_tensor(BR[o, 4 * c:4 * c + 4, 3], PS[o, b, :].rearrange("p (t h c) -> p t h c", t=4, h=H2),
                                            nq[o, :, 4 * c:4 * c + 4].rearrange("p h (t u) -> p t h u", u=1).broadcast_to([64, 4, H2, D2]), ALU.mult), half, "o", n)
                for n in range(2, 4):
                    await_freed(dve, half, "o", n)
                for g in range(2):
                    t = slice(4 * g, 4 * g + 4)
                    link(dve.tensor_reduce(mu[:, t, 3], BR[:, t, 3], AX.X, ALU.add))
                    link(dve.tensor_scalar(mu[:, t, 3], mu[:, t, 3], 1.0 / D2, None, ALU.mult))
                    dve.tensor_tensor(DD[:, t], BR[:, t, 3], mu[:, t, 3].rearrange("p t (h o) -> p t h o", o=1).broadcast_to([P, 4, H2, D2]),
                                      ALU.subtract).then_inc(b_dd, 1)
                link(dve.tensor_reduce(bmx[:, :, 3], BR[:, :, 3], AX.X, ALU.max))

            def mixture(half):
                for g in range(2):
                    dve.wait_ge(b_ddsq, 2 * half + g + 1)
                    ins = dve.tensor_reduce(sd[:, 4 * g:4 * g + 4, 3], DD[:, 4 * g:4 * g + 4], AX.X, ALU.add)
                ins.then_inc(b_std, 1)
                link(dve.tensor_tensor(bmx, mu, bmx, ALU.add))
                dve.wait_ge(b_stds, half + 1)
                link(dve.tensor_tensor(bmx, bmx, sd, ALU.add))
                link(dve.tensor_scalar(bmx, bmx, 1.0 / 3.0, None, ALU.mult))
                al = wt("alphar").rearrange("p (o u h) -> p o u h", o=1, u=1).broadcast_to([P, TH, 4, H2])
                link(dve.tensor_tensor(bmx, bmx, al, ALU.mult))
                link(dve.tensor_tensor(gate, gate, bmx, ALU.add))
                link(dve.tensor_reduce(lmx, gate.rearrange("p t r h -> p t h r"), AX.X, ALU.max))
                bc = lambda x: x.rearrange("p t (o h) -> p t o h", o=1).broadcast_to([P, TH, 4, H2])
                dve.tensor_tensor(gate, gate, bc(lmx), ALU.subtract).then_inc(b_ee, 1)

            def mixed(half):
                bc = lambda x: x.rearrange("p t (o h) -> p t o h", o=1).broadcast_to([P, TH, 4, H2])
                dve.wait_ge(b_exp, half + 1)
                link(dve.tensor_reduce(lmx, gate.rearrange("p t r h -> p t h r"), AX.X, ALU.add))
                link(dve.reciprocal(lmx, lmx))
                dve.tensor_tensor(gate, gate, bc(lmx), ALU.mult).then_inc(b_wts, 1)
                dve.wait_ge(b_wts, half + 1)
                for g in range(2):
                    t = slice(4 * g, 4 * g + 4)
                    for r in (1, 2, 3):
                        ins = dve.tensor_tensor(BR[:, t, r], BR[:, t, r], gate[:, t, r].rearrange("p t (h o) -> p t h o", o=1).broadcast_to([P, 4, H2, D2]), ALU.mult)
                    link(ins)
                    link(dve.tensor_tensor(O[:, t], BR[:, t, 1], BR[:, t, 2], ALU.add))
                    link(dve.tensor_tensor(O[:, t], O[:, t], BR[:, t, 3], ALU.add))
                    dve.wait_ge(b_mixp, 2 * half + g + 1)
                    dve.tensor_tensor(O[:, t], O[:, t], BR[:, t, 0], ALU.add).then_inc(b_mix, 1)

            def normalise(half):
                for g in range(2):
                    dve.wait_ge(b_osq, 2 * half + g + 1)
                    ins = dve.tensor_reduce(oms[:, 4 * g:4 * g + 4], OS[:, 4 * g:4 * g + 4], AX.X, ALU.add)
                link(ins)
                dve.tensor_scalar(oms, oms, 1.0 / D2, 1e-5, ALU.mult, ALU.add).then_inc(b_ors, 1)
                dve.wait_ge(b_ors, 2 * half + 2)
                link(dve.reciprocal(oms, oms))
                for c in range(2):
                    dve.tensor_tensor(O[:, 4 * c:4 * c + 4], O[:, 4 * c:4 * c + 4],
                                      oms[:, 4 * c:4 * c + 4].rearrange("p t (h o) -> p t h o", o=1).broadcast_to([P, 4, H2, D2]), ALU.mult).then_inc(b_on, 1)

            def residual(half):
                for c in range(2):
                    b = await_full(dve, half, "op", c)
                    n = 2 * half + c
                    freed(dve.tensor_tensor(XT[:, n * NC:(n + 1) * NC], XT[:, n * NC:(n + 1) * NC], bank(b), ALU.add), half, "op", c)

            def keys3(t):
                dve.wait_ge(c_ks, 2 * t + 2)
                if t == 0:
                    dve.wait_ge(c_zero, 1)
                else:
                    dve.wait_ge(c_s, t)
                for f in range(2):
                    o = slice(64 * f, 64 * f + 64)
                    dve.tensor_copy(kx3[o, :, :, f, 0], ak3[o, :].rearrange("p (c b) -> p c b", c=C3)[:, :, J * t:J * t + J])
                    ins = dve.tensor_copy(kx3[o, :, :, f, 1:L + 1], kpl[o].rearrange("p c (j n) -> p c j n", j=J))
                ins.then_inc(c_kx, 1)

            def mask3(t):
                dve.wait_ge(c_s, t + 1)
                if t >= 1:
                    dve.wait_ge(c_p, t)
                for i in range(2):
                    dve.scalar_tensor_tensor(out=Sc[:, 8 * i:8 * i + 8, :], in0=PS[:, 2 + i, 0:272].rearrange("p (h k) -> p h k", h=8), scalar=1.0 / 8.0,
                                             in1=cs("band").rearrange("p (o k) -> p o k", o=1).broadcast_to([P, 8, K3]), op0=ALU.mult, op1=ALU.add).then_inc(c_s1, 1)
                dve.wait_ge(c_s1, 2 * t + 2)
                dve.tensor_reduce(mx3, Sc, AX.X, ALU.max).then_inc(c_mx, 1)

            def norm3(t):
                dve.wait_ge(c_p, t + 1)
                link(dve.tensor_reduce(sm3, P3, AX.X, ALU.add))
                link(dve.reciprocal(rs3, sm3))
                dve.tensor_tensor(Pn3.rearrange("p (h k) -> p h k", h=H3), P3[:, :, 1:L + 1],
                                  rs3.rearrange("p (h o) -> p h o", o=1).broadcast_to([P, H3, L]), ALU.mult).then_inc(c_pn, 1)
                link(dve.tensor_tensor(sm3, P3[:, :, 0], rs3, ALU.mult))
                if t >= 1:
                    dve.wait_ge(c_pit, t)
                dve.tensor_tensor(Pie3, sm3.rearrange("p (o h) -> p o h", o=1).broadcast_to([P, J, H3]),
                                  cs("jm4").rearrange("p (j o) -> p j o", o=1).broadcast_to([P, J, H3]), ALU.mult).then_inc(c_pie, 1)
                dve.wait_ge(c_pn, t + 1)
                if t >= 1:
                    dve.wait_ge(c_ptd, t)
                dve.transpose(PTc, Pn3).then_inc(c_ptc, 1)

            def logits3(t):
                dve.wait_ge(c_ytm, t + 1)
                dve.tensor_tensor(LG[:, t], bank(5, E, P), wt("rbr"), ALU.add).then_inc(c_lg, 1)

            def tile3(t, pieces=(), fill=None, last=None):
                if t < T:
                    keys3(t)
                if fill:
                    fill(1)
                if t < T:
                    mask3(t)
                for piece in pieces:
                    piece(1)
                if t < TH:
                    norm3(t)
                if last:
                    last(1)
                if t >= 1:
                    logits3(t - 1)
                if TH <= t < T:
                    norm3(t)

            dve.wait_ge(s_w, 16)
            dve.wait_ge(s_zero, 1)
            q_swizzle(0)
            dve.wait_ge(s_c, 16)
            dve.wait_ge(s_mk, 2)
            for t in range(TH):
                tile1(t)
                if t == 0:
                    q_swizzle(1)
            dve.wait_ge(s_wb, 16)
            dve.wait_ge(s_z2d, 16)
            dve.wait_ge(s_z1, 4)
            zero_pads(0)
            for t in range(TH, TH + 2):
                tile1(t)
            PIECES = {3: (coefficients, lambda h: couple(h, "gn", 20),), 4: (lambda h: couple(h, "ga"),), 7: (stats, gate_in, delta_stats, spreads)}
            BETWEEN = (lambda h: convolve(h, 2, "v"), lambda h: long_filter(h, 0, 5), lambda h: long_filter(h, 10, 15),
                       lambda h: long_filter(h, 28, 31), lambda h: solve(h, 0, 4), lambda h: solve(h, 8, 13), lambda h: solve(h, 19, 25), lambda h: None)
            INSIDE = (None, lambda h: convolve(h, 1, "k"), lambda h: long_filter(h, 5, 10), lambda h: long_filter(h, 15, 20), None,
                      lambda h: solve(h, 4, 8), lambda h: solve(h, 13, 19), lambda h: solve(h, 25, L - 1))
            BETWEEN[0](0)
            for i in range(1, TH - 1):
                tile1(TH + 1 + i, PIECES.get(i, ()), INSIDE[i])
                BETWEEN[i](0)
            tile1(T)
            INSIDE[-1](0)
            for piece in PIECES[TH - 1]:
                piece(0)
            for rest in (mixture, mixed, normalise, residual):
                rest(0)
            zero_pads(1)
            BETWEEN[0](1)
            for t in range(TH - 1):
                tile3(t, PIECES.get(t + 1, ()) if t < TH - 2 else (), INSIDE[t + 1], BETWEEN[t + 1])
            for piece in PIECES[TH - 1]:
                piece(1)
            mixture(1)
            tile3(TH - 1)
            for rest in (mixed, normalise, residual):
                rest(1)
            def probabilities(a, b):
                link(dve.tensor_reduce(lm[:, a:b], LG[:, a:b], AX.X, ALU.max))
                dve.tensor_tensor(LG[:, a:b], LG[:, a:b], by_expert(lm, a, b), ALU.subtract).then_inc(d_ex, 1)

            def by_expert(x, a, b):
                return x[:, a:b].rearrange("p (t o) -> p t o", o=1).broadcast_to([P, b - a, E])

            def picks(k, a, b):
                rk = cs("rank").rearrange("p (o e) -> p o e", o=1).broadcast_to([P, b - a, E])
                l, q, m = LG[:, a:b], tq[:, a:b], lm[:, a:b]
                dve.wait_ge(d_exps, k + 1)
                link(dve.tensor_reduce(m, l, AX.X, ALU.add))
                link(dve.reciprocal(m, m))
                link(dve.tensor_tensor(l, l, by_expert(lm, a, b), ALU.mult))
                for s in range(2):
                    link(dve.tensor_reduce(tv[:, s, a:b], l, AX.X, ALU.max))
                    link(dve.tensor_tensor(q, l, by_expert(tv[:, s], a, b), ALU.is_equal))
                    link(dve.tensor_tensor(q, q, rk, ALU.mult))
                    link(dve.tensor_reduce(tk[:, s, a:b], q, AX.X, ALU.max))
                    link(dve.tensor_tensor(OH[:, s, a:b], rk, by_expert(tk[:, s], a, b), ALU.is_equal))
                    if s == 0:
                        link(dve.scalar_tensor_tensor(out=l, in0=OH[:, 0, a:b], scalar=-4.0, in1=l, op0=ALU.mult, op1=ALU.add))
                link(dve.tensor_tensor(m, tv[:, 0, a:b], tv[:, 1, a:b], ALU.add))
                link(dve.tensor_scalar(m, m, EPS, None, ALU.add))
                link(dve.reciprocal(m, m))
                link(dve.tensor_tensor(tv[:, :, a:b], tv[:, :, a:b], m.rearrange("p (o t) -> p o t", o=1).broadcast_to([P, 2, b - a]), ALU.mult))
                link(dve.tensor_scalar(vl[:, :, a:b], tv[:, :, a:b], EPS, None, ALU.is_gt))
                for s in range(2):
                    ins = dve.tensor_tensor(OH[:, s, a:b], OH[:, s, a:b], by_expert(vl[:, s], a, b), ALU.mult)
                ins.then_inc(d_oh, 1)

            def place(k, s, a, b):
                n = b - a
                bk, c0 = (1 if s else 6), a * E
                dve.wait_ge(d_cum, k + 1)
                tt, rn, ps = (x[:, 0:E * n] for x in (tot, run_, pos_))
                pt = ps.rearrange("p (t e) -> p t e", e=E)
                link(dve.tensor_copy(tt.rearrange("p (e t) -> p e t", e=E), bank(bk, n * E, c0 + T * E).rearrange("p (t e) -> p e t", e=E)))
                link(dve.tensor_tensor_scan(out=rn, data0=cs(f"seg{n}"), data1=tt, initial=0.0, op0=ALU.mult, op1=ALU.add))
                link(dve.tensor_tensor(rn, rn, tt, ALU.subtract))
                link(dve.tensor_tensor(pt, rn.rearrange("p (e t) -> p t e", e=E), bank(bk, n * E, c0).rearrange("p (t e) -> p t e", e=E), ALU.add))
                link(dve.tensor_tensor(pt, pt, carry.rearrange("p (o e) -> p o e", o=1).broadcast_to([P, n, E]), ALU.add))
                if s == 0:
                    link(dve.tensor_reduce(add, tt.rearrange("p (e t) -> p e t", e=E), AX.X, ALU.add))
                    dve.tensor_tensor(carry, carry, add, ALU.add)
                u = slice(s * T + a, s * T + b)
                link(dve.tensor_tensor(pt, pt, OH[:, s, a:b], ALU.mult))
                link(dve.tensor_reduce(pown[:, u], pt, AX.X, ALU.add))
                link(dve.tensor_tensor(pt, OH[:, s, a:b], cs("ebase").rearrange("p (o e) -> p o e", o=1).broadcast_to([P, n, E]), ALU.mult))
                link(dve.tensor_reduce(slot[:, u], pt, AX.X, ALU.add))
                link(dve.tensor_scalar(keep[:, u], pown[:, u], float(CAP), None, ALU.is_lt))
                link(dve.tensor_tensor(keep[:, u], keep[:, u], vl[:, s, a:b], ALU.mult))
                link(dve.tensor_tensor(slot[:, u], slot[:, u], pown[:, u], ALU.add))
                link(dve.tensor_tensor(slot[:, u], slot[:, u], keep[:, u], ALU.mult))
                link(dve.tensor_scalar(pown[:, u], keep[:, u], -1.0, 1.0, ALU.mult, ALU.add))
                link(dve.tensor_tensor(sidx[:, u], pown[:, u], cs("dummy", s * T + a, s * T + b), ALU.mult))
                link(dve.tensor_tensor(sidx[:, u], sidx[:, u], slot[:, u], ALU.add))
                dve.tensor_copy(sI[:, u], sidx[:, u]).then_inc(d_slot, 1)
                link(dve.tensor_tensor(tv[:, s, a:b], tv[:, s, a:b], keep[:, u], ALU.mult))

            link(dve.memset(carry, 0.0))
            for t in range(TH, T + 1):
                tile3(t)
                for k, (a, b) in enumerate(ROUTES[:2]):
                    if t == b:
                        dve.wait_ge(c_lg, b)
                        probabilities(a, b)
                    if t == b + 1:
                        picks(k, a, b)
                    if t == b + 3:
                        place(k, 0, a, b)
            a, b = ROUTES[2]
            dve.wait_ge(c_lg, T)
            probabilities(a, b)
            picks(2, a, b)
            place(2, 0, a, b)
            place(3, 1, 0, T)

            for c in range(CH):
                dve.wait_ge(d_x1t, c + 1)
                dve.tensor_copy(X1[:, 4 * c:4 * c + 4, :].rearrange("p t c -> p (t c)"), bank(7)).then_inc(d_x1s, 1)

            def rows_in(e):
                dve.wait_ge(d_xt, e + 1)
                if e >= 2:
                    dve.wait_ge(d_ye, e - 1)
                dve.tensor_copy(XGT[:, e % 2], bank(0, CAP)).then_inc(d_xts, 1)
                g = gidx[:, 3 * e:3 * e + 3]
                link(dve.tensor_scalar(g, cs("slotix"), carry[:, e:e + 1], float(N), ALU.is_ge, ALU.mult))
                for s, (a, b) in enumerate(RPARTS):
                    ins = dve.tensor_tensor(g[0:b - a, s:s + 1], g[0:b - a, s:s + 1], XG[0:b - a, e % 2, s, D:D + 1], ALU.add)
                link(ins)
                dve.tensor_copy(gI[:, 3 * e:3 * e + 3], g).then_inc(d_di, 1)

            def result(e):
                dve.wait_ge(d_f2, e + 1)
                link(dve.tensor_scalar(YE[:, e % 2], bank(5, CAP), wt("fb2", e, e + 1), wt("lsc", e, e + 1), ALU.add, ALU.mult))
                dve.tensor_tensor(YE[:, e % 2], YE[:, e % 2], XGT[:, e % 2], ALU.add).then_inc(d_ye, 1)

            def rows_out(e):
                dve.wait_ge(d_yt, e + 1)
                if e >= 2:
                    dve.wait_ge(d_yd[e % 2], 16 * 3 * (e // 2))
                for s, (a, b) in enumerate(RPARTS):
                    ins = dve.tensor_copy(YO[0:b - a, e % 2, s, :], PS[0:b - a, 6, s * P:(s + 1) * P])
                ins.then_inc(d_yts, 1)

            rows_in(0)
            for e in range(E):
                if e < E - 1:
                    rows_in(e + 1)
                if e:
                    rows_out(e - 1)
                result(e)
            rows_out(E - 1)
            for c in range(CH):
                dve.wait_ge(d_ga[c], 16 * 2)
                for t in range(4 * c, 4 * c + 4):
                    ins = dve.scalar_tensor_tensor(out=RO[:, t, :], in0=YG[:, 0, t, :], scalar=tv[:, 0, t:t + 1], in1=X1[:, t, :], op0=ALU.mult, op1=ALU.add)
                link(ins)
                for t in range(4 * c, 4 * c + 4):
                    ins = dve.scalar_tensor_tensor(out=RO[:, t, :], in0=YG[:, 1, t, :], scalar=tv[:, 1, t:t + 1], in1=RO[:, t, :], op0=ALU.mult, op1=ALU.add)
                ins.then_inc(d_fin, 1)


def constants():
    p = np.arange(P)
    j, q = p // L, p % L
    f = np.float32
    c = {}
    c["ident"] = np.eye(P)
    c["hm2"] = p[:, None] // D2 == np.arange(H2)[None]
    c["ones"] = np.ones((P, P))
    c["before"] = (p[:, None] < p[None])
    c["hm4"] = (p[:, None] % 32) // D1 == np.arange(4)[None]
    c["hmv"] = (p[:, None] // L == (p[None] % 32) // D1)
    c["hm16"] = p[:, None] // D1 == np.arange(H1)[None]
    c["jm4"] = j[:, None] == np.arange(J)[None]
    c["c01"] = np.arange(K1)[None] <= q[:, None] + 1
    c["nonc"] = -10000.0 * (1 - c["c01"])
    k64 = np.arange(64)
    same = (j[:, None] % 2) == (k64[None] // L)
    c["maskn"] = -1.0 * (same & (k64[None] % L < q[:, None]))
    c["maska"] = 1.0 * (same & (q[:, None] <= k64[None] % L))
    band = np.full((P, K3), NEG)
    band[:, 0] = 0
    band[:, 1:L + 1][np.abs(np.arange(L)[None] - q[:, None]) <= 1] = 0
    band[(q == 0) | (q == L - 1), L + 1] = 0
    c["band"] = band
    c["jm2"] = (j[:, None] % 2) == np.arange(2)[None]
    c["rank"] = np.broadcast_to(E - np.arange(E), (P, E))
    c["ebase"] = np.broadcast_to(CAP * np.arange(E), (P, E))
    c["dummy"] = SLOTS + P * np.arange(2 * T)[None] + p[:, None]
    for n in (8, 4, 16):
        c[f"seg{n}"] = np.broadcast_to(np.arange(E * n) % n != 0, (P, E * n))
    c["tok"] = P * np.arange(T)[None] + p[:, None]
    c["empty"] = 2 * N + P * np.arange(SCOLS)[None] + p[:, None]
    c["slotix"] = P * np.arange(3)[None] + p[:, None]
    return np.concatenate([c[n].astype(f) for n, _ in CONSTS], axis=1)


def kernel(**inputs):
    import concourse.bacc as bacc
    from concourse.bass_utils import run_bass_kernel_spmd

    i = {k: np.asarray(v) for k, v in inputs.items()}
    col = lambda a: a.reshape(-1, P).T
    row = lambda a: np.broadcast_to(a.reshape(1, -1), (P, a.size))
    order = lambda a: a.reshape(4, H2, -1)[[0, 1, 3, 2]].reshape(a.shape)
    A, G, S, F = "L0_cond_", "L0_attn_", "L0_cond2_", "L0_ffn_"
    w = {
        "wqkv": i[A + "c_attn_w"], "cproj": i[A + "c_proj_w"], "ukT": i[A + "uk_w"].T, "uvT": i[A + "uv_w"].T,
        "condT": i["cond_1024"].T, "qpT": i[G + "q_proj_w"].T, "kpT": i[G + "k_proj_w"].T, "vpT": i[G + "v_proj_w"].T,
        "bpT": i[G + "b_proj_w"].T, "gw1T": i[G + "gmix_w1"].T,
        "gw2T": order(i[G + "gmix_w2"]).T.reshape(2, P, H1).transpose(1, 0, 2).reshape(P, -1), "opT": i[G + "o_proj_w"].T,
        "wq3": i[S + "WQ_w"], "wk3": i[S + "WK_w"], "wv3": i[S + "WV_w"],
        "wo3": i[S + "WO_w"].reshape(C3, P, D).transpose(1, 0, 2).reshape(P, -1), "rwT": i[F + "router_w"].T,
        "bq1": col(i[A + "c_attn_b"][0:D]), "bk1": col(i[A + "c_attn_b"][D:2 * D]), "ukb": col(i[A + "uk_b"]), "uvb": col(i[A + "uv_b"]),
        "cpb": col(i[A + "c_proj_b"]), "cwq": i[G + "q_conv_w"], "cwk": i[G + "k_conv_w"], "cwv": i[G + "v_conv_w"],
        "firs": i[G + "fir_short_w"].reshape(P, -1), "firl": i[G + "fir_long_w"].reshape(P, -1), "gb1": col(i[G + "gmix_b1"]),
        "onw": np.tile(i[G + "o_norm_w"], H2).reshape(P, 1), "bq3": col(i[S + "WQ_b"]), "bk3": col(i[S + "WK_b"]), "bv3": col(i[S + "WV_b"]),
        "bo3": col(i[S + "WO_b"]), "fb1": col(i[F + "fc1_b"]), "fb2": i[F + "fc2_b"].T, "lsc": i[F + "layer_scale"].T,
        "bv1r": row(i[A + "c_attn_b"][2 * D:]), "gb2r": row(order(i[G + "gmix_b2"])), "alphar": row(i[G + "alpha"]), "rbr": row(i[F + "router_b"]),
    }
    for n, width in WEIGHTS:
        assert w[n].shape == (P, width), (n, w[n].shape)
    arrays = {
        "xT": np.ascontiguousarray(i["x"].reshape(N, D).T),
        "w": np.ascontiguousarray(np.concatenate([w[n] for n, _ in WEIGHTS], axis=1)),
        "cst": constants(),
        "mask": np.ascontiguousarray(i["mask_Bx1x1xS_ff0"].reshape(NB, L)),
        "fc1": np.ascontiguousarray(i[F + "fc1_w"].transpose(2, 0, 1)),
        "fc2": np.ascontiguousarray(i[F + "fc2_w"].transpose(2, 0, 1).reshape(HC, P, E, D).transpose(1, 2, 0, 3).reshape(P, E, HID)),
    }
    nc = bacc.Bacc("TRN2", target_bir_lowering=False, num_devices=1)
    f = mybir.dt.float32
    aps = [nc.dram_tensor(k, a.shape, f, kind="ExternalInput").ap() for k, a in arrays.items()]
    scratch = {"xscr": (XROWS, D + 1), "yscr": (YROWS, D), "nscr": (2, P, 1024), "vscr": (2, P, 1024), "uscr": (2, P, 1024), "zscr": (NB, H3, D)}
    aps += [nc.dram_tensor(k, s, f, kind="Internal").ap() for k, s in scratch.items()]
    o = nc.dram_tensor("out", (N, D), f, kind="ExternalOutput").ap()
    program(nc, *aps, o)
    r = run_bass_kernel_spmd(nc, [arrays], core_ids=[0])
    return r.results[0]["out"].reshape(NB, L, D)
```
